# Optimizing a Trainium2 kernel written in Bass

```python
import numpy as np
import jax
import jax.numpy as jnp

def _softmax(x, axis=-1):
    return jax.nn.softmax(x, axis=axis)

def _gelu(x):
    return jax.nn.gelu(x, approximate=True)

def _silu(x):
    return jax.nn.silu(x)

def _sigmoid(x):
    return jax.nn.sigmoid(x)

def _layernorm(x, axis=-1, eps=1e-05):
    m = jnp.mean(x, axis=axis, keepdims=True)
    v = jnp.var(x, axis=axis, keepdims=True)
    return (x - m) / jnp.sqrt(v + eps)

def _scatter_add(tgt, idx, src, axis=0):
    return tgt.at[idx].add(src)

def _segment_sum(src, seg, n):
    return jax.ops.segment_sum(src, seg, n)
kernel_name = 'mk_gnn_ffn_d1_gnn_r8_ccfe3a'

def setup_inputs(seed: int=0):
    np.random.seed(seed)
    _w = jnp.asarray

    def _rec_inputs():
        import jax
        import jax.numpy as jnp
        _gk = jax.random.key(seed)
        x = -0.0003713 + 1 * jax.random.normal(jax.random.fold_in(_gk, 1), (6250, 256), jnp.float32)
        _s = jax.random.randint(jax.random.fold_in(_gk, 2), (100000,), 0, 6250, jnp.int32)
        _d = jax.random.randint(jax.random.fold_in(_gk, 3), (100000,), 0, 6250, jnp.int32)
        _loop = jnp.arange(6250, dtype=jnp.int32)
        src = jnp.concatenate([_s, _d, _loop])
        dst = jnp.concatenate([_d, _s, _loop])
        _o = jnp.argsort(dst, stable=True)
        src = src[_o]
        dst = dst[_o]
        return (x, src, dst)
    x, src, dst = _rec_inputs()

    def _L0_gnn_setup():
        import jax, jax.numpy as jnp
        import numpy as np
        N = 6250
        E = 100000
        D = 256
        EPS = 1e-05

        def _gcn_norm(row, col, n):
            ew = jnp.ones(row.shape[0], jnp.float32)
            deg = jax.ops.segment_sum(ew, col, num_segments=n)
            dis = jnp.where(deg > 0, jax.lax.rsqrt(deg), 0.0)
            return dis[row] * dis[col]

        def _gcn_conv(z, W, b, row, col, n):
            norm = _gcn_norm(row, col, n)
            h = z @ W
            msg = h[row] * norm[:, None]
            return jax.ops.segment_sum(msg, col, num_segments=n) + b

        def _batchnorm(z, g, bt):
            mu = z.mean(axis=0)
            var = ((z - mu) ** 2).mean(axis=0)
            return g * (z - mu) * jax.lax.rsqrt(var + EPS) + bt
        key = jax.random.key(seed)
        ks = jax.random.split(key, 12)
        x = jax.random.normal(ks[0], (N, D), dtype=jnp.float32)
        row = jax.random.randint(ks[1], (E,), 0, N)
        col = jax.random.randint(ks[2], (E,), 0, N)
        col = jnp.where(col == row, (col + 1) % N, col)
        edge_index = jnp.stack([row, col]).astype(jnp.int64)
        s = 1.0 / np.sqrt(D)
        return {'x': x, 'edge_index': edge_index, 'W0': jax.random.normal(ks[3], (D, D), dtype=jnp.float32) * s, 'b0': jnp.zeros((D,), jnp.float32), 'g0': jnp.ones((D,), jnp.float32), 'bt0': jnp.zeros((D,), jnp.float32), 'W1': jax.random.normal(ks[4], (D, D), dtype=jnp.float32) * s, 'b1': jnp.zeros((D,), jnp.float32), 'g1': jnp.ones((D,), jnp.float32), 'bt1': jnp.zeros((D,), jnp.float32)}
    _L0_gnn_all = _L0_gnn_setup()
    _L0_gnn_in = {k: v for k, v in _L0_gnn_all.items() if k in ('W0', 'b0', 'g0', 'bt0', 'W1', 'b1', 'g1', 'bt1')}
    del _L0_gnn_all

    def _L0_ffn_setup():
        import jax, jax.numpy as jnp
        import numpy as np
        B, S, H, F, E, K = (8, 512, 256, 512, 16, 2)
        EPS = 1e-05
        key = jax.random.key(seed)
        ks = jax.random.split(key, 9)
        sc = 0.02
        return {'x': jax.random.normal(ks[0], (B, S, H), dtype=jnp.float32), 'gate_w': jax.random.normal(ks[1], (H, E), dtype=jnp.float32) * sc, 'gate_b': jnp.zeros((E,), dtype=jnp.float32), 'w1': jax.random.normal(ks[2], (E, H, F), dtype=jnp.float32) * sc, 'b1': jnp.zeros((E, F), dtype=jnp.float32), 'w2': jax.random.normal(ks[3], (E, F, H), dtype=jnp.float32) * sc, 'b2': jnp.zeros((E, H), dtype=jnp.float32), 'gamma': jnp.ones((H,), dtype=jnp.float32), 'beta': jnp.zeros((H,), dtype=jnp.float32)}
    _L0_ffn_all = _L0_ffn_setup()
    _L0_ffn_in = {k: v for k, v in _L0_ffn_all.items() if k in ('gate_w', 'gate_b', 'w1', 'b1', 'w2', 'b2', 'gamma', 'beta')}
    del _L0_ffn_all
    return {'x': x, 'src': src, 'dst': dst, 'L0_gnn_W0': _L0_gnn_in['W0'], 'L0_gnn_b0': _L0_gnn_in['b0'], 'L0_gnn_g0': _L0_gnn_in['g0'], 'L0_gnn_bt0': _L0_gnn_in['bt0'], 'L0_gnn_W1': _L0_gnn_in['W1'], 'L0_gnn_b1': _L0_gnn_in['b1'], 'L0_gnn_g1': _L0_gnn_in['g1'], 'L0_gnn_bt1': _L0_gnn_in['bt1'], 'L0_ffn_gate_w': _L0_ffn_in['gate_w'], 'L0_ffn_gate_b': _L0_ffn_in['gate_b'], 'L0_ffn_w1': _L0_ffn_in['w1'], 'L0_ffn_b1': _L0_ffn_in['b1'], 'L0_ffn_w2': _L0_ffn_in['w2'], 'L0_ffn_b2': _L0_ffn_in['b2'], 'L0_ffn_gamma': _L0_ffn_in['gamma'], 'L0_ffn_beta': _L0_ffn_in['beta']}

def reference(x, src, dst, L0_gnn_W0, L0_gnn_b0, L0_gnn_g0, L0_gnn_bt0, L0_gnn_W1, L0_gnn_b1, L0_gnn_g1, L0_gnn_bt1, L0_ffn_gate_w, L0_ffn_gate_b, L0_ffn_w1, L0_ffn_b1, L0_ffn_w2, L0_ffn_b2, L0_ffn_gamma, L0_ffn_beta):
    import jax
    import jax.numpy as jnp

    def _L0_gnn_ref(x, edge_index, W0, b0, g0, bt0, W1, b1, g1, bt1):
        import jax, jax.numpy as jnp
        import numpy as np
        N = 6250
        E = 100000
        D = 256
        EPS = 1e-05

        def _gcn_norm(row, col, n):
            ew = jnp.ones(row.shape[0], jnp.float32)
            deg = jax.ops.segment_sum(ew, col, num_segments=n)
            dis = jnp.where(deg > 0, jax.lax.rsqrt(deg), 0.0)
            return dis[row] * dis[col]

        def _gcn_conv(z, W, b, row, col, n):
            norm = _gcn_norm(row, col, n)
            h = z @ W
            msg = h[row] * norm[:, None]
            return jax.ops.segment_sum(msg, col, num_segments=n) + b

        def _batchnorm(z, g, bt):
            mu = z.mean(axis=0)
            var = ((z - mu) ** 2).mean(axis=0)
            return g * (z - mu) * jax.lax.rsqrt(var + EPS) + bt
        n = x.shape[0]
        loops = jnp.arange(n, dtype=edge_index.dtype)
        row = jnp.concatenate([edge_index[0], loops])
        col = jnp.concatenate([edge_index[1], loops])
        z = _gcn_conv(x, W0, b0, row, col, n)
        z = _batchnorm(jax.nn.relu(z), g0, bt0)
        z = _gcn_conv(z, W1, b1, row, col, n)
        z = _batchnorm(jax.nn.relu(z), g1, bt1)
        return z

    def _L0_ffn_ref(x, gate_w, gate_b, w1, b1, w2, b2, gamma, beta):
        import jax, jax.numpy as jnp
        import numpy as np
        B, S, H, F, E, K = (8, 512, 256, 512, 16, 2)
        EPS = 1e-05
        gate_logits = x @ gate_w + gate_b
        topk_vals, topk_idx = jax.lax.top_k(gate_logits, K)
        topk_w = jax.nn.softmax(topk_vals, axis=-1)
        h = jax.nn.relu(jnp.einsum('bsh,ehf->bsef', x, w1) + b1)
        expert_out = jnp.einsum('bsef,efh->bseh', h, w2) + b2
        sel = jnp.take_along_axis(expert_out, topk_idx[:, :, :, None], axis=2)
        moe = jnp.sum(topk_w[..., None] * sel, axis=2)
        y = x + moe
        mu = jnp.mean(y, axis=-1, keepdims=True)
        var = jnp.var(y, axis=-1, keepdims=True)
        return (y - mu) / jnp.sqrt(var + EPS) * gamma + beta
    edge_index = jnp.stack([src, dst])
    x = x + _L0_gnn_ref(_layernorm(x, axis=-1), edge_index, L0_gnn_W0, L0_gnn_b0, L0_gnn_g0, L0_gnn_bt0, L0_gnn_W1, L0_gnn_b1, L0_gnn_g1, L0_gnn_bt1)
    x = x + _L0_ffn_ref(_layernorm(x, axis=-1)[None], L0_ffn_gate_w, L0_ffn_gate_b, L0_ffn_w1, L0_ffn_b1, L0_ffn_w2, L0_ffn_b2, L0_ffn_gamma, L0_ffn_beta)[0]
    return x

_drawn_inputs = setup_inputs


def setup_inputs(seed=0):
    import zlib

    import numpy as np

    out = dict(_drawn_inputs(seed))
    spreads = {'L0_gnn_b0': (0.0, 0.1),
     'L0_gnn_g0': (1.0, 0.2),
     'L0_gnn_bt0': (0.0, 0.1),
     'L0_gnn_b1': (0.0, 0.1),
     'L0_gnn_g1': (1.0, 0.2),
     'L0_gnn_bt1': (0.0, 0.1),
     'L0_ffn_gate_b': (0.0, 0.279),
     'L0_ffn_b1': (0.0, 0.8),
     'L0_ffn_b2': (0.0, 0.269),
     'L0_ffn_gamma': (1.0, 0.2),
     'L0_ffn_beta': (0.0, 0.1)}
    factors = {}
    for name, (base, spread) in spreads.items():
        noise = np.random.default_rng([zlib.crc32(name.encode()), seed]).standard_normal(out[name].shape)
        drawn = base * np.exp(spread * noise) if base else spread * noise
        out[name] = jnp.asarray(drawn.astype(out[name].dtype))
    for name, factor in factors.items():
        out[name] = (out[name] * factor).astype(out[name].dtype)
    return out
```

```python
from contextlib import ExitStack, contextmanager

import numpy as np
import concourse.bass as bass
from concourse import mybir

F32 = mybir.dt.float32
F32R = mybir.dt.float32r
BF16 = mybir.dt.bfloat16
FP16 = mybir.dt.float16
I32 = mybir.dt.int32
U32 = mybir.dt.uint32
U8 = mybir.dt.uint8
ALU = mybir.AluOpType
ACT = mybir.ActivationFunctionType
AX = mybir.AxisListType

P = 128
N = 6250
D = 256
NT = -(-N // P)
NPAD = NT * P
LAST = N - (NT - 1) * P
E = 206250
CH = -(-E // P) + 7
EPAD = CH * P
BD = 8
SLOTS = 3 * P
REAL = SLOTS - BD
WT = 7
NBLK = WT * P
KEYS = NT * BD
BPT = P // BD
UNITS = 3 * BPT
PAIRS = BPT // 2
NO_NODE = 8192.0
EPS = 1e-5
NE = 16
FF = 512
GOOD, BAD = 0, 1
MT = 114


class Names:
    pass


class Chain:

    def __init__(self, engine, sem):
        self.engine, self.sem, self.n = engine, sem, 0

    def __call__(self, ins):
        self.n += 1
        ins.then_inc(self.sem, 1)
        self.engine.wait_ge(self.sem, self.n)


def edge_stage(nc, m, src, dst):
    with ExitStack() as ctx:
        def sb(name, shape, dt):
            return ctx.enter_context(nc.sbuf_tensor(name, shape, dt))

        sem = m.sem

        iota_i = sb("iota_i", [P, 512], I32)
        pads = sb("pads", [2, (EPAD - E) // 2], I32)
        padd = sb("padd", [2, (EPAD - E) // 2], I32)
        slot_src = sb("slot_src", [P, WT, SLOTS], I32)
        slot_dst = sb("slot_dst", [P, WT, SLOTS], I32)
        heads_i = sb("heads_i", [P, CH], I32)
        heads = sb("heads", [P, CH], F32)
        below = sb("below", [P, CH], BF16)
        first_i = sb("first_i", [P, WT], I32)
        first = sb("first", [P, WT], F32)
        rowf = sb("rowf", [P, WT], F32)
        rowi = sb("rowi", [P, WT], I32)
        edge_row_i = sb("edge_row_i", [P, WT, P], I32)
        edge_row = sb("edge_row", [P, WT, P], F32)
        cnt = sb("cnt", [P, WT], F32)
        starti = sb("starti", [P, WT], I32)
        hi = sb("hi", [P, WT, SLOTS], I32)
        lo_i = sb("lo_i", [P, WT, SLOTS], I32)
        lo = sb("lo", [P, WT, SLOTS], F32)
        dl = sb("dl", [P, WT, SLOTS], F32)
        ok = sb("ok", [P, WT, SLOTS], F32)
        key = sb("key", [P, WT, SLOTS], F32)
        hit = sb("hit", [P, SLOTS], BF16)
        deg = sb("deg", [P, WT, BD], F32)
        over = sb("over", [P, WT * BD], BF16)
        sums = sb("sums", [P, 2], F32)
        bad = sb("bad", [P, 1], F32)
        pt = [ctx.enter_context(nc.psum_tensor(f"keys_ps{i}", [P, 2, 4, P], F32)) for i in range(2)]
        psum_sums = ctx.enter_context(nc.psum_tensor("sums_ps", [P, 2], F32))

        s_copy_src, s_copy_dst = sem("src_copied"), sem("dst_copied")
        s_pad_src, s_pad_dst = sem("src_padded"), sem("dst_padded")
        s_heads, s_heads_in = sem("heads_packed"), sem("heads_in")
        s_const = sem("constants_ready")
        s_pool = sem("pool_step")
        s_dve = sem("dve_step")
        s_memset = sem("pads_set")
        s_row = sem("row_index_ready")
        s_rows = sem("edge_rows_in")
        s_start = sem("block_starts_ready")
        s_src, s_dst = sem("slot_src_in"), sem("slot_dst_in")
        s_keys = sem("keys_ready")
        s_tr = sem("keys_transposed")
        s_ev = sem("keys_copied")
        s_ev2 = sem("los_copied")
        s_sums, s_total = sem("sums_ready"), sem("total_ready")
        s_deg, s_degd = sem("deg_ready"), sem("deg_stored")

        src_rows, dst_rows = m.src_pad.rearrange("(r c) -> r c", c=P), m.dst_pad.rearrange("(r c) -> r c", c=P)
        with nc.Block() as block:
            @block.sync
            def _(sp):
                sp.dma_start(m.dst_pad[0:E].rearrange("(r c) -> r c", r=150),
                             dst.rearrange("(r c) -> r c", r=150)).then_inc(s_copy_dst, 16)
                sp.dma_start(m.src_pad[0:E].rearrange("(r c) -> r c", r=150),
                             src.rearrange("(r c) -> r c", r=150)).then_inc(s_copy_src, 16)
                sp.wait_ge(s_memset, 2)
                sp.dma_start(m.dst_pad[E:EPAD].rearrange("(r c) -> r c", r=2), padd[:]).then_inc(s_pad_dst, 16)
                sp.dma_start(m.src_pad[E:EPAD].rearrange("(r c) -> r c", r=2), pads[:]).then_inc(s_pad_src, 16)
                sp.wait_ge(s_copy_dst, 16)
                sp.wait_ge(s_pad_dst, 16)
                with nc.allow_non_contiguous_dma(reason="one word of each row, 6.7 KB in all"):
                    sp.dma_start(m.heads[:].rearrange("(r c) -> r c", c=1), dst_rows[:, 0:1]).then_inc(s_heads, 16)
                sp.wait_ge(s_heads, 16)
                sp.dma_start(heads_i[:], m.heads.rearrange("(a r) -> a r", a=1).to_broadcast([P, CH])).then_inc(s_heads_in, 16)
                sp.wait_ge(s_deg, 1)
                sp.dma_start(m.deg.rearrange("(w p d) -> p w d", p=P, d=BD), deg[:]).then_inc(s_degd, 16)
                sp.wait_ge(s_degd, 16)

            @block.gpsimd
            def _(pool):
                step = Chain(pool, s_pool)
                pool.iota(first_i[:], pattern=[[P * BD, WT]], base=0, channel_multiplier=BD).then_inc(s_const, 1)
                pool.iota(slot_src[:, :, REAL:SLOTS], pattern=[[P * BD, WT], [1, BD]], base=0, channel_multiplier=BD).then_inc(s_const, 1)
                pool.iota(slot_dst[:, :, REAL:SLOTS], pattern=[[P * BD, WT], [1, BD]], base=0, channel_multiplier=BD).then_inc(s_const, 1)
                step(pool.iota(iota_i[:], pattern=[[1, 512]], base=0, channel_multiplier=0))
                pool.tensor_copy(m.iota16[:], iota_i[:]).then_inc(s_const, 1)
                step(pool.memset(m.ident[:], 0.0))
                pool.affine_select(out=m.ident[:], in_=m.ident[:], compare_op=ALU.not_equal, fill=1.0, base=0,
                                   pattern=[[-1, P]], channel_multiplier=1).then_inc(s_const, 1)
                pool.memset(m.ones[:], 1.0).then_inc(s_const, 1)
                pool.wait_ge(s_row, 1)
                for w in range(WT):
                    pool.indirect_dma_start(out=edge_row_i[:, w, :], out_offset=None, in_=dst_rows,
                                            in_offset=bass.IndirectOffsetOnAxis(ap=rowi[:, w:w + 1], axis=0)).then_inc(s_rows, 16)
                pool.wait_ge(s_start, 1)
                pool.wait_ge(s_copy_src, 16)
                pool.wait_ge(s_pad_src, 16)
                for w in range(WT):
                    start = bass.IndirectOffsetOnAxis(ap=starti[:, w:w + 1], axis=0)
                    pool.indirect_dma_start(out=slot_dst[:, w, 0:REAL], out_offset=None,
                                            in_=m.dst_pad.rearrange("(e o) -> e o", o=1), in_offset=start).then_inc(s_dst, 16)
                    pool.indirect_dma_start(out=slot_src[:, w, 0:REAL], out_offset=None,
                                            in_=m.src_pad.rearrange("(e o) -> e o", o=1), in_offset=start).then_inc(s_src, 16)

            @block.vector
            def _(dve):
                step = Chain(dve, s_dve)
                dve.memset(pads[:], 0).then_inc(s_memset, 1)
                dve.memset(padd[:], int(NO_NODE)).then_inc(s_memset, 1)
                dve.wait_ge(s_const, 6)
                step(dve.tensor_copy(first[:], first_i[:]))
                dve.wait_ge(s_heads_in, 16)
                step(dve.tensor_copy(heads[:], heads_i[:]))
                for w in range(WT):
                    step(dve.tensor_scalar(below[:], heads[:], first[:, w:w + 1], 0.0, ALU.is_lt, ALU.add,
                                           accum_out=rowf[:, w:w + 1]))
                step(dve.tensor_scalar(rowf[:], rowf[:], -1.0, 0.0, ALU.add, ALU.max))
                dve.tensor_copy(rowi[:], rowf[:]).then_inc(s_row, 1)
                dve.wait_ge(s_rows, 16 * WT)
                step(dve.tensor_copy(edge_row[:], edge_row_i[:]))
                for w in range(WT):
                    step(dve.tensor_scalar(below[:, 0:P], edge_row[:, w, :], first[:, w:w + 1], 0.0, ALU.is_lt, ALU.add,
                                           accum_out=cnt[:, w:w + 1]))
                step(dve.scalar_tensor_tensor(out=cnt[:], in0=rowf[:], scalar=float(P), in1=cnt[:], op0=ALU.mult, op1=ALU.add))
                dve.tensor_copy(starti[:], cnt[:]).then_inc(s_start, 1)
                dve.wait_ge(s_dst, 16 * WT)
                step(dve.tensor_tensor(dl[:], slot_dst[:], first[:].unsqueeze(2).to_broadcast([P, WT, SLOTS]), ALU.subtract))
                step(dve.tensor_scalar(ok[:], dl[:], 0.0, None, ALU.is_ge))
                step(dve.scalar_tensor_tensor(out=ok[:], in0=dl[:], scalar=float(BD), in1=ok[:], op0=ALU.is_lt, op1=ALU.mult))
                dve.wait_ge(s_src, 16 * WT)
                step(dve.tensor_scalar(hi[:], slot_src[:], 7, None, ALU.arith_shift_right))
                step(dve.tensor_scalar(lo_i[:], slot_src[:], P - 1, None, ALU.bitwise_and))
                step(dve.tensor_copy(lo[:], lo_i[:]))
                step(dve.scalar_tensor_tensor(out=key[:], in0=hi[:], scalar=float(BD), in1=dl[:], op0=ALU.mult, op1=ALU.add))
                step(dve.scalar_tensor_tensor(out=key[:], in0=key[:], scalar=1.0, in1=ok[:], op0=ALU.add, op1=ALU.mult))
                dve.sem_inc(s_keys, 1)
                for w in range(WT):
                    for d in range(BD):
                        step(dve.tensor_scalar(hit[:], dl[:, w, :], float(d), 0.0, ALU.is_equal, ALU.add,
                                               accum_out=deg[:, w, d:d + 1]))
                dve.sem_inc(s_deg, 1)
                step(dve.reduce_sum(sums[:, 0:1], deg[:].rearrange("p w d -> p (w d)"), AX.X))
                step(dve.tensor_scalar(over[:], deg[:].rearrange("p w d -> p (w d)"), 255.0, 0.0, ALU.is_gt, ALU.add,
                                       accum_out=sums[:, 1:2]))
                dve.sem_inc(s_sums, 1)
                for w in range(WT):
                    dve.wait_ge(s_tr, w + 1)
                    dve.tensor_scalar(m.keyT[:, w * P:(w + 1) * P, :].rearrange("p w j -> p j w"), pt[w % 2][:, 0, 0:3, :],
                                      -1.0, None, ALU.add).then_inc(s_ev, 1)
                dve.wait_ge(s_total, 1)
                step(dve.tensor_scalar(bad[:], psum_sums[:, 0:1], float(E + NBLK * BD), None, ALU.not_equal))
                step(dve.tensor_tensor(bad[:], bad[:], psum_sums[:, 1:2], ALU.add))
                step(dve.tensor_scalar(m.flags[:, BAD:BAD + 1], bad[:], 0.0, None, ALU.is_gt))
                step(dve.tensor_scalar(m.flags[:, GOOD:GOOD + 1], bad[:], 0.0, None, ALU.is_equal))

            @block.tensor
            def _(pe):
                pe.wait_ge(s_const, 6)
                pe.wait_ge(s_keys, 1)
                for w in range(WT):
                    if w >= 2:
                        pe.wait_ge(s_ev, w - 1)
                        pe.wait_ge(s_ev2, w - 1)
                    for k, t in enumerate((key, lo)):
                        for j in range(3):
                            last = pe.transpose(pt[w % 2][:, k, j, :], t[:, w, j * P:(j + 1) * P], m.ident[:])
                    last.then_inc(s_tr, 1)
                pe.wait_ge(s_sums, 1)
                pe.matmul(psum_sums[:], m.ones[:], sums[:], start=True, stop=True).then_inc(s_total, 1)

            @block.scalar
            def _(act):
                for w in range(WT):
                    act.wait_ge(s_tr, w + 1)
                    act.activation(m.loT[:, w * P:(w + 1) * P, :].rearrange("p w j -> p j w"), pt[w % 2][:, 1, 0:3, :],
                                   ACT.Copy).then_inc(s_ev2, 1)


class Semaphores:

    def __init__(self, nc):
        self.nc, self.live = nc, []

    def __call__(self, name):
        self.live.append(self.nc.alloc_semaphore(f"{name}_{len(self.live)}"))
        return self.live[-1]

    def renew(self):
        self.nc.clear_and_free_semaphores(self.live)
        self.nc.all_engine_barrier()
        self.live = []


def wait(engine, sem, value):
    if not isinstance(value, int) or value > 0:
        engine.wait_ge(sem, value)


def for_tiles(engine, body, total, unroll, first=None):
    first = unroll if first is None else first
    rounds = (total - first) // unroll
    for t in range(first):
        body(t, t % unroll)
    if rounds:
        with engine.Fori(0, rounds) as i:
            for k in range(unroll):
                body(first + k + i * unroll, (first + k) % unroll)
    for t in range(first + rounds * unroll, total):
        body(t, t % unroll)


def dis_stage(nc, m):
    with ExitStack() as ctx:
        deg = ctx.enter_context(nc.sbuf_tensor("deg_rows", [NT, P], F32))
        root = ctx.enter_context(nc.sbuf_tensor("deg_root", [NT, P], F32))
        pt = ctx.enter_context(nc.psum_tensor("dis_ps", [P, NT], F32))
        s_in, s_root, s_inv, s_t, s_done = (m.sem(n) for n in
                                            ("deg_in", "root_ready", "dis_ready", "dis_transposed", "dis_done"))
        with nc.Block() as block:
            @block.sync
            def _(sp):
                sp.dma_start(deg[:], m.deg[0:NPAD].rearrange("(t p) -> t p", p=P)).then_inc(s_in, 16)

            @block.scalar
            def _(act):
                act.wait_ge(s_in, 16)
                act.activation(root[:], deg[:], ACT.Sqrt).then_inc(s_root, 1)

            @block.vector
            def _(dve):
                dve.wait_ge(s_root, 1)
                dve.reciprocal(deg[:], root[:]).then_inc(s_inv, 1)
                dve.wait_ge(s_t, 1)
                dve.tensor_copy(m.dis[:], pt[:]).then_inc(s_done, 1)

            @block.tensor
            def _(pe):
                pe.wait_ge(s_inv, 1)
                pe.transpose(pt[:], deg[:], m.ident[0:NT, 0:NT]).then_inc(s_t, 1)


def project_pe(pe, t, r, m, s, w):
    pe.wait_ge(s.lhs, t + 1)
    wait(pe, s.hf, t - 1)
    for k in range(2):
        last = pe.matmul(s.hp_ps[r % 2][:, 0:D], s.lhs_t[r % 2][:, k, :], w[:, k, :], start=(k == 0), stop=(k == 1))
    last.then_inc(s.h, 1)


def project_scale(act, t, r, m, s):
    act.wait_ge(s.h, t + 1)
    wait(act, s.split, t - 1)
    act.activation(s.hf_t[r % 2][:], s.hp_ps[r % 2][:, 0:D], ACT.Copy, scale=m.dis[:, bass.ds(t, 1)]).then_inc(s.hf, 1)


def project_split(dve, t, r, m, s):
    dve.wait_ge(s.hf, t + 1)
    hi = m.h[:, bass.ds(t, 1), 0, :]
    lo = m.h[:, bass.ds(t, 1), 1, :]
    hf = s.hf_t[r % 2][:].unsqueeze(1)
    dve.tensor_copy(hi, hf).then_inc(s.hi, 1)
    dve.wait_ge(s.hi, t + 1)
    dve.tensor_tensor(lo, hf, hi.bitcast(F32), ALU.subtract).then_inc(s.split, 1)


def project_buffers(ctx, nc, m, tag):
    def sem(name):
        return m.sem(f"{name}{tag}")

    s = Names()
    s.lhs_t = [ctx.enter_context(nc.sbuf_tensor(f"lhs{tag}{i}", [P, 2, P], F32)) for i in range(2)]
    s.hf_t = [ctx.enter_context(nc.sbuf_tensor(f"hf{tag}{i}", [P, D], F32)) for i in range(2)]
    s.hp_ps = [ctx.enter_context(nc.psum_tensor(f"h_ps{tag}{i}", [P, 512], F32)) for i in range(2)]
    s.lhs = sem("lhs_ready")
    s.h = sem("h_ready")
    s.hf = sem("hf_ready")
    s.hi = sem("hi_ready")
    s.split = sem("h_split")
    return s


def input_stage(nc, m, x, w0):
    G = 8
    groups = (NT - 1) // G
    with ExitStack() as ctx:
        sem = m.sem

        s = project_buffers(ctx, nc, m, "0")
        xg = [ctx.enter_context(nc.sbuf_tensor(f"xg{i}", [P, G, D], F32)) for i in range(2)]
        w = ctx.enter_context(nc.sbuf_tensor("w0_sb", [P, 2, D], F32))
        st = ctx.enter_context(nc.sbuf_tensor("ln0_stats", [P, G, 6], F32))
        mv = ctx.enter_context(nc.sbuf_tensor("ln0_mv", [P, G, 2], F32))
        root = ctx.enter_context(nc.sbuf_tensor("ln0_root", [P, G], F32))
        rstd = ctx.enter_context(nc.sbuf_tensor("ln0_rstd", [P, G], F32))
        pt = [ctx.enter_context(nc.psum_tensor(f"xt_ps{i}", [P, 512], F32)) for i in range(2)]
        s_x = [sem(f"x_in{i}") for i in range(2)]
        s_w, s_st, s_mv, s_root, s_rstd, s_xn, s_tr, s_zero, s_seen = (sem(n) for n in (
            "w0_in", "ln0_stats_ready", "ln0_mv_ready", "ln0_root_ready", "ln0_rstd_ready", "xn_ready", "xt_ready", "x_tail_zeroed", "ln0_stats_seen"))

        with nc.Block() as block:
            @block.sync
            def _(sp):
                sp.dma_start(w[:], w0.rearrange("(k p) n -> p k n", p=P)).then_inc(s_w, 16)

                def load(g, r):
                    wait(sp, s_tr, (g - 1) * G)
                    sp.dma_start(xg[r][:], x[bass.ds(g * (G * P), G * P), :].rearrange("(k p) d -> p k d", p=P)).then_inc(s_x[r], 16)

                for_tiles(sp, load, groups, 2)
                sp.wait_ge(s_zero, 1)
                sp.dma_start(xg[groups % 2][0:LAST, 0, :], x[(NT - 1) * P:N, :]).then_inc(s_x[groups % 2], 16)

            @block.vector
            def _(dve):
                def normalize(g, q, n):
                    dve.wait_ge(s_x[q], (g - q) * 8 + 16)
                    for k in range(n):
                        dve.bn_stats(st[:, k, :], xg[q][:, k, :]).then_inc(s_st, 1)
                    dve.wait_ge(s_st, g * G + n)
                    dve.sem_inc(s_seen, 1)
                    for k in range(n):
                        last = dve.bn_aggr(mv[:, k, :], st[:, k, :])
                    last.then_inc(s_mv, 1)
                    dve.wait_ge(s_root, g + 1)
                    dve.reciprocal(rstd[:, 0:n], root[:, 0:n]).then_inc(s_rstd, 1)
                    dve.wait_ge(s_rstd, g + 1)
                    for k in range(n):
                        dve.tensor_scalar(xg[q][:, k, :], xg[q][:, k, :], mv[:, k, 0:1], rstd[:, k:k + 1],
                                          ALU.subtract, ALU.mult).then_inc(s_xn, 1)

                def group(g, r):
                    normalize(g, r, G)
                    if not isinstance(g, int) or g > 0:
                        for k in range(G):
                            project_split(dve, (g - 1) * G + k, k, m, s)

                for_tiles(dve, group, groups, 2)
                dve.wait_ge(s_tr, (groups - 1) * G)
                dve.memset(xg[groups % 2][96:P, 0, :], 0.0).then_inc(s_zero, 1)
                normalize(groups, groups % 2, 1)
                for k in range(G + 1):
                    project_split(dve, (groups - 1) * G + k, k, m, s)

            @block.tensor
            def _(pe):
                pe.wait_ge(s_w, 16)

                def group(g, r, n=G):
                    for k in range(n):
                        t = g * G + k
                        pe.wait_ge(s_xn, t + 1)
                        wait(pe, s.lhs, t - 1)
                        for c in range(2):
                            last = pe.transpose(pt[k % 2][:, c * P:(c + 1) * P], xg[r][:, k, c * P:(c + 1) * P], m.ident[:])
                        last.then_inc(s_tr, 1)
                        if not isinstance(t, int) or t > 0:
                            project_pe(pe, t - 1, k + 1, m, s, w)

                for_tiles(pe, group, groups, 2)
                group(groups, groups % 2, 1)
                project_pe(pe, NT - 1, NT - 1, m, s, w)

            @block.scalar
            def _(act):
                def root_of(g, n):
                    act.wait_ge(s_mv, g + 1)
                    act.activation(root[:, 0:n], mv[:, 0:n, 1], ACT.Sqrt, bias=m.eps[:, 0:1]).then_inc(s_root, 1)

                def tile(t, r):
                    act.wait_ge(s_tr, t + 1)
                    wait(act, s.h, t - 1)
                    act.activation(s.lhs_t[r % 2][:].rearrange("p k n -> p (k n)"), pt[r % 2][:, 0:D], ACT.Copy).then_inc(s.lhs, 1)
                    project_scale(act, t, r, m, s)

                def group(g, r):
                    root_of(g, G)
                    if not isinstance(g, int) or g > 0:
                        for k in range(G):
                            tile((g - 1) * G + k, k)

                for_tiles(act, group, groups, 2)
                root_of(groups, 1)
                for k in range(G + 1):
                    tile((groups - 1) * G + k, k)


def tail_buffers(ctx, nc, m, tag, bias):
    def sem(name):
        return m.sem(f"{name}{tag}")

    s = Names()
    s.sum_ps = [ctx.enter_context(nc.psum_tensor(f"sum_ps{tag}{i}", [P, 512], F32)) for i in range(2)]
    s.zt_ps = [ctx.enter_context(nc.psum_tensor(f"zt_ps{tag}{i}", [P, 512], F32)) for i in range(2)]
    s.low_t = [ctx.enter_context(nc.sbuf_tensor(f"low{tag}{i}", [P, D], F32)) for i in range(2)]
    s.z_t = [ctx.enter_context(nc.sbuf_tensor(f"z{tag}{i}", [P, D], F32)) for i in range(2)]
    s.zt_t = [ctx.enter_context(nc.sbuf_tensor(f"zt{tag}{i}", [P, 2, P], F32)) for i in range(2)]
    s.bias = bias
    s.sum = sem("sum_ready")
    s.low = sem("low_scaled")
    s.z = sem("z_ready")
    s.tr = sem("z_transposed")
    s.relu = sem("z_relu")
    s.stats = sem("z_stats_ready")
    s.store = [sem(f"z_stored{i}_") for i in range(2)]
    return s


def tail_low(act, t, r, m, s):
    act.wait_ge(s.sum, t + 1)
    wait(act, s.z, t - 1)
    act.activation(s.low_t[r][:], s.sum_ps[r][:, D:2 * D], ACT.Copy, scale=m.dis[:, bass.ds(t, 1)]).then_inc(s.low, 1)


def tail_add(dve, t, r, m, s):
    dve.wait_ge(s.low, t + 1)
    wait(dve, s.tr, t - 1)
    dve.scalar_tensor_tensor(out=s.z_t[r][:], in0=s.sum_ps[r][:, 0:D], scalar=m.dis[:, bass.ds(t, 1)], in1=s.low_t[r][:],
                             op0=ALU.mult, op1=ALU.add).then_inc(s.z, 1)


def tail_transpose(pe, t, r, m, s):
    pe.wait_ge(s.z, t + 1)
    wait(pe, s.relu, 2 * (t - 1))
    for c in range(2):
        last = pe.transpose(s.zt_ps[r][:, c * P:(c + 1) * P], s.z_t[r][:, c * P:(c + 1) * P], m.ident[:])
    last.then_inc(s.tr, 1)


def tail_relu(act, t, r, u, m, s):
    act.wait_ge(s.tr, t + 1)
    wait(act, s.stats, 2 * (t - 1))
    wait(act, s.store[r], 16 * u)
    for c in range(2):
        act.activation(s.zt_t[r][:, c, :], s.zt_ps[r][:, c * P:(c + 1) * P], ACT.Relu, bias=s.bias[:, c:c + 1]).then_inc(s.relu, 1)


def tail_stats(dve, t, r, m, s, n=P):
    dve.wait_ge(s.relu, 2 * (t + 1))
    for c in range(2):
        out = m.stats[:, c, t * 6:(t + 1) * 6] if isinstance(t, int) else m.stats[:, c, bass.ds(t * 6, 6)]
        dve.bn_stats(out, s.zt_t[r][:, c, 0:n]).then_inc(s.stats, 1)


def tile_at(engine, store, t, width, dt):
    size = P * width * (1 if dt == U8 else 4)
    at = t * size if isinstance(t, int) else engine.snap(engine.to_reg(t * size), min_val=0, max_val=store.shape[0] - size)
    flat = store[bass.ds(at, size)]
    return (flat if dt == U8 else flat.bitcast(dt)).rearrange("(p n) -> p n", p=P)


def tail_store(sp, t, r, m, s):
    at = tile_at(sp, m.zT, t, D, F32)
    sp.wait_ge(s.relu, 2 * (t + 1))
    sp.dma_start(at, s.zt_t[r][:].rearrange("p c n -> p (c n)")).then_inc(s.store[r], 16)


def tail_stored(sp, s):
    for r in range(2):
        sp.wait_ge(s.store[r], 16 * ((NT + 1 - r) // 2))


def build_stage(nc, m):
    RING = 2
    AHEAD = 4
    DVE_LO = 4
    with ExitStack() as ctx:
        sem = m.sem

        s = tail_buffers(ctx, nc, m, "_b", m.b0)
        key1 = [ctx.enter_context(nc.sbuf_tensor(f"key_onehot{i}", [P, 6, KEYS], BF16)) for i in range(AHEAD)]
        lo1 = [ctx.enter_context(nc.sbuf_tensor(f"lo_onehot{i}", [P, 6, P], BF16)) for i in range(AHEAD)]
        key_now = [ctx.enter_context(nc.sbuf_tensor(f"key_now{i}", [P, UNITS], F32)) for i in range(2)]
        lo_now = [ctx.enter_context(nc.sbuf_tensor(f"lo_now{i}", [P, UNITS], F32)) for i in range(2)]
        counts = [ctx.enter_context(nc.sbuf_tensor(f"counts{i}", [P, NT, P], F32R)) for i in range(2)]
        bytes_ = [ctx.enter_context(nc.sbuf_tensor(f"count_bytes{i}", [P, NT, P], U8)) for i in range(2)]
        pair_ps = [ctx.enter_context(nc.psum_tensor(f"pair_ps{i}", [P, 2, 512], F32)) for i in range(RING)]
        s_now, s_one, s_one_pool, s_seen, s_pair, s_ev, s_byte = (sem(n) for n in (
            "keys_now_ready", "onehots_ready", "pool_onehots_ready", "pool_may_write", "pair_ready", "pair_copied", "bytes_ready"))
        s_bst = [sem(f"bytes_stored{i}") for i in range(2)]
        key_flat = m.keyT[:].rearrange("p w j -> p (w j)")
        lo_flat = m.loT[:].rearrange("p w j -> p (w j)")

        def steps(engine, body):
            for t in range(4):
                body(t, t % 2, t // 2, True, t >= 1, t >= 2)
            with engine.Fori(0, (NT - 4) // 2) as i:
                for k in range(2):
                    body(i * 2 + (4 + k), k, i + 2, True, True, True)
            body(NT - 1, (NT - 1) % 2, (NT - 1) // 2, True, True, True)
            body(NT, NT % 2, NT // 2, False, True, True)
            body(NT + 1, (NT + 1) % 2, (NT + 1) // 2, False, False, True)

        with nc.Block() as block:
            @block.vector
            def _(dve):
                with when(dve, m, GOOD):
                    def now(t, r):
                        dve.tensor_copy(key_now[r][:], key_flat[:, bass.ds(t * UNITS, UNITS)]).then_inc(s_now, 1)
                        dve.tensor_copy(lo_now[r][:], lo_flat[:, bass.ds(t * UNITS, UNITS)]).then_inc(s_now, 1)

                    def step(t, r, u, build, prod, tail):
                        if build:
                            if isinstance(t, int) and t == 0:
                                now(0, 0)
                            else:
                                dve.wait_ge(s_one, t * PAIRS)
                                dve.wait_ge(s_one_pool, t * PAIRS)
                            now(t + 1, 1 - r)
                            dve.wait_ge(s_now, 2 * (t + 1))
                            for q in range(PAIRS):
                                wait(dve, s_pair, t * PAIRS + (q - AHEAD + 1))
                                for j in range(6):
                                    c = q * 6 + j
                                    last = dve.tensor_scalar(key1[q % AHEAD][:, j, :], m.iota16[:, 0:KEYS], key_now[r][:, c:c + 1], None, ALU.is_equal)
                                    if j < DVE_LO:
                                        last = dve.tensor_scalar(lo1[q % AHEAD][:, j, :], m.iota16[:, 0:P], lo_now[r][:, c:c + 1], None, ALU.is_equal)
                                last.then_inc(s_one, 1)
                                if tail and q == 0:
                                    tail_add(dve, t - 2, r, m, s)
                                if tail and q == 5:
                                    tail_stats(dve, t - 2, r, m, s)
                        elif tail:
                            tail_add(dve, t - 2, r, m, s)
                            tail_stats(dve, t - 2, r, m, s, LAST if t - 2 == NT - 1 else P)

                    steps(dve, step)

            @block.tensor
            def _(pe):
                with when(pe, m, GOOD):
                    def product(t, r, first, end):
                        for h in range(first, end):
                            last = pe.matmul(s.sum_ps[r][:], counts[r][:, h, :], m.h[:, h, :, :].rearrange("p a d -> p (a d)"),
                                             start=(h == 0), stop=(h == NT - 1))
                        if end == NT:
                            last.then_inc(s.sum, 1)

                    def product_ready(t):
                        pe.wait_ge(s_ev, (t + 1) * PAIRS)
                        wait(pe, s.z, t - 1)

                    def step(t, r, u, build, prod, tail):
                        for q in range(PAIRS):
                            if build:
                                pe.wait_ge(s_one, t * PAIRS + (q + 1))
                                pe.wait_ge(s_one_pool, t * PAIRS + (q + 1))
                                wait(pe, s_ev, t * PAIRS + (q - RING + 1))
                                for b in range(2):
                                    for j in range(3):
                                        last = pe.matmul(pair_ps[q % RING][:, b, 0:KEYS], lo1[q % AHEAD][:, b * 3 + j, :],
                                                         key1[q % AHEAD][:, b * 3 + j, :], start=(j == 0), stop=(j == 2))
                                last.then_inc(s_pair, 1)
                            if prod:
                                if q == 0:
                                    product_ready(t - 1)
                                product(t - 1, 1 - r, q * 6, (q + 1) * 6 if q < PAIRS - 1 else NT)
                            if tail and q == 2:
                                tail_transpose(pe, t - 2, r, m, s)

                    steps(pe, step)

            @block.scalar
            def _(act):
                with when(act, m, GOOD):
                    def step(t, r, u, build, prod, tail):
                        for q in range(PAIRS):
                            if tail and q == 1:
                                tail_low(act, t - 2, r, m, s)
                            if build:
                                if q == 0:
                                    wait(act, s.sum, t - 1)
                                    wait(act, s_byte, (t - 1) * PAIRS)
                                act.wait_ge(s_pair, t * PAIRS + (q + 1))
                                act.activation(counts[r][:, :, q * 16:(q + 1) * 16].rearrange("p h (b d) -> p b h d", b=2),
                                               pair_ps[q % RING][:, :, 0:KEYS].rearrange("p b (h d) -> p b h d", d=BD),
                                               ACT.Copy).then_inc(s_ev, 1)
                            if prod:
                                if q == 0:
                                    act.wait_ge(s_ev, t * PAIRS)
                                    wait(act, s_bst[1 - r], 16 * (u + (r - 1)))
                                end = (q + 1) * 6 if q < PAIRS - 1 else NT
                                act.activation(bytes_[1 - r][:, q * 6:end, :], counts[1 - r][:, q * 6:end, :].bitcast(F32),
                                               ACT.Copy).then_inc(s_byte, 1)
                            if tail and q == 4:
                                tail_relu(act, t - 2, r, u - 1, m, s)

                    steps(act, step)

            @block.gpsimd
            def _(pool):
                with when(pool, m, GOOD):
                    def step(t, r, u, build, prod, tail):
                        if build:
                            pool.wait_ge(s_now, 2 * (t + 1))
                            for q in range(PAIRS):
                                wait(pool, s_pair, t * PAIRS + (q - AHEAD + 1))
                                pool.sem_inc(s_seen, 1)
                                for j in range(DVE_LO, 6):
                                    c = q * 6 + j
                                    last = pool.tensor_scalar(lo1[q % AHEAD][:, j, :], m.iota16[:, 0:P], lo_now[r][:, c:c + 1], None, ALU.is_equal)
                                last.then_inc(s_one_pool, 1)

                    steps(pool, step)

            @block.sync
            def _(sp):
                with when(sp, m, GOOD):
                    def step(t, r, u, build, prod, tail):
                        if tail:
                            tail_store(sp, t - 2, r, m, s)
                        if prod:
                            at = tile_at(sp, m.counts, t - 1, NPAD, U8)
                            sp.wait_ge(s_byte, t * PAIRS)
                            sp.dma_start(at, bytes_[1 - r][:].rearrange("p h n -> p (h n)")).then_inc(s_bst[1 - r], 16)

                    steps(sp, step)
                    tail_stored(sp, s)
                    for r in range(2):
                        sp.wait_ge(s_bst[r], 16 * ((NT + 1 - r) // 2))


@contextmanager
def when(engine, m, flag):
    value = engine.value_load(m.flags[0:1, flag:flag + 1], min_val=0, max_val=1)
    with engine.If(value):
        yield


def any_degrees(nc, m):
    RING = 4
    with ExitStack() as ctx:
        def sb(name, shape, dt):
            return ctx.enter_context(nc.sbuf_tensor(name, shape, dt))

        dst_i, part_i = sb("any_dst", [P, CH], I32), sb("any_dst_part", [P, CH], I32)
        lo, hi = sb("any_lo", [P, CH], F32), sb("any_hi", [P, CH], F32)
        lo1 = [sb(f"any_lo_onehot{i}", [P, P], BF16) for i in range(RING)]
        hi1 = [sb(f"any_hi_onehot{i}", [P, NT], BF16) for i in range(RING)]
        root = sb("any_root", [P, NT], F32)
        total = ctx.enter_context(nc.psum_tensor("any_degree_ps", [P, NT], F32))
        s_in, s_step, s_one, s_used, s_root, s_dis = (m.sem(n) for n in (
            "any_dst_in", "any_degree_step", "any_onehots_ready", "any_onehots_used", "any_root_ready", "any_dis_ready"))
        with nc.Block() as block:
            @block.sync
            def _(sp):
                with when(sp, m, BAD):
                    sp.dma_start(dst_i[:], m.dst_pad.rearrange("(p c) -> p c", p=P)).then_inc(s_in, 16)

            @block.vector
            def _(dve):
                with when(dve, m, BAD):
                    step = Chain(dve, s_step)
                    dve.wait_ge(s_in, 16)
                    step(dve.tensor_scalar(part_i[:], dst_i[:], P - 1, None, ALU.bitwise_and))
                    step(dve.tensor_copy(lo[:], part_i[:]))
                    step(dve.tensor_scalar(part_i[:], dst_i[:], 7, None, ALU.arith_shift_right))
                    step(dve.tensor_copy(hi[:], part_i[:]))

                    def onehots(t, r, u):
                        wait(dve, s_used, t - RING + 1)
                        dve.tensor_scalar(lo1[r][:], m.iota16[:, 0:P], lo[:, at_tile(t, 0)], None, ALU.is_equal)
                        dve.tensor_scalar(hi1[r][:], m.iota16[:, 0:NT], hi[:, at_tile(t, 0)], None, ALU.is_equal).then_inc(s_one, 1)

                    for_slots(dve, onehots, CH, RING)
                    dve.wait_ge(s_root, 1)
                    dve.reciprocal(m.dis[:], root[:]).then_inc(s_dis, 1)

            @block.tensor
            def _(pe):
                with when(pe, m, BAD):
                    def count(t, r, u):
                        pe.wait_ge(s_one, t + 1)
                        pe.matmul(total[:], lo1[r][:], hi1[r][:], start=isinstance(t, int) and t == 0,
                                  stop=isinstance(t, int) and t == CH - 1).then_inc(s_used, 1)

                    for_slots(pe, count, CH, RING)

            @block.scalar
            def _(act):
                with when(act, m, BAD):
                    act.wait_ge(s_used, CH)
                    act.activation(root[:], total[:], ACT.Sqrt, bias=m.ones[:, 0:1]).then_inc(s_root, 1)


def any_sums(nc, m, tag, bias):
    RING = 4
    with ExitStack() as ctx:
        def sb(name, shape, n, dt=F32):
            return [ctx.enter_context(nc.sbuf_tensor(f"{name}{tag}{i}", shape, dt)) for i in range(n)]

        def sem(name):
            return m.sem(f"{name}{tag}")

        s = tail_buffers(ctx, nc, m, tag, bias)
        edges = sb("any_edges", [P, CH], 2, I32)
        row = sb("any_h_row", [P, D], 2)
        src_now, dst_now, dst_f = sb("any_src_now", [P, 1], RING, I32), sb("any_dst_now", [P, 1], RING, I32), sb("any_dst_f", [P, 1], RING)
        diag, equal = sb("any_diag", [P, P], 2), sb("any_equal", [P, P], 2)
        h_rows, sums, new = sb("any_h_rows", [P, D], RING), sb("any_sums", [P, D], RING), sb("any_new", [P, D], RING)
        final = sb("any_final", [P, D], 2)
        dst_ps = [ctx.enter_context(nc.psum_tensor(f"any_dst_ps{tag}{i}", [P, 512], F32)) for i in range(2)]
        part_ps = s.sum_ps
        s_edges, s_row, s_now, s_diag, s_dst, s_equal, s_part, s_new, s_seen, s_seen2 = (sem(n) for n in (
            "any_edges_in", "any_row_ready", "any_now_ready", "any_diag_ready", "any_dst_rows_ready", "any_equal_ready",
            "any_part_ready", "any_new_ready", "any_rows_may_load", "any_sums_may_load"))
        s_stored = [sem(f"any_row_stored{i}_") for i in range(2)]
        s_h, s_old, s_sent = ([sem(f"{n}{i}_") for i in range(RING)] for n in ("any_h_rows_in", "any_sums_in", "any_sums_stored"))
        s_final = [sem(f"any_final_in{i}_") for i in range(2)]
        h_at, sum_at = m.any_h.rearrange("(n d) -> n d", d=4 * D).bitcast(F32), m.any_sum.rearrange("(n d) -> n d", d=4 * D).bitcast(F32)

        with nc.Block() as block:
            @block.sync
            def _(sp):
                with when(sp, m, BAD):
                    sp.dma_start(edges[0][:], m.src_pad.rearrange("(p c) -> p c", p=P)).then_inc(s_edges, 16)
                    sp.dma_start(edges[1][:], m.dst_pad.rearrange("(p c) -> p c", p=P)).then_inc(s_edges, 16)

                    def store(t, r, u):
                        h_to, sum_to = tile_at(sp, m.any_h, t, D, F32), tile_at(sp, m.any_sum, t, D, F32)
                        sp.wait_ge(s_row, t + 1)
                        sp.dma_start(h_to, row[r][:]).then_inc(s_stored[r], 16)
                        sp.dma_start(sum_to, row[r][:]).then_inc(s_stored[r], 16)

                    for_slots(sp, store, NT + 1, 2)

                    def load(t, r, u):
                        at = tile_at(sp, m.any_sum, t, D, F32)
                        wait(sp, s.z, t - 1)
                        sp.dma_start(final[r][:], at).then_inc(s_final[r], 16)
                        if not isinstance(t, int) or t >= 1:
                            tail_store(sp, t - 1, 1 - r, m, s)

                    for r in range(RING):
                        sp.wait_ge(s_sent[r], 16 * ((CH + RING - 1 - r) // RING))
                    for_slots(sp, load, NT, 2)
                    tail_store(sp, NT - 1, (NT - 1) % 2, m, s)
                    tail_stored(sp, s)

            @block.vector
            def _(dve):
                with when(dve, m, BAD):
                    def whole(t, r, u):
                        wait(dve, s_stored[r], 32 * u)
                        dve.tensor_tensor(row[r][:].unsqueeze(1), m.h[:, at_tile(t, 0), 0, :].bitcast(F32),
                                          m.h[:, at_tile(t, 0), 1, :].bitcast(F32), ALU.add).then_inc(s_row, 1)

                    for_slots(dve, whole, NT, 2)
                    dve.wait_ge(s_stored[NT % 2], 32 * (NT // 2))
                    dve.memset(row[NT % 2][:], 0.0).then_inc(s_row, 1)
                    dve.wait_ge(s_edges, 32)

                    def now(t, r, u):
                        wait(dve, s_sent[r], 16 * u)
                        dve.tensor_copy(src_now[r][:], edges[0][:, at_tile(t, 0)]).then_inc(s_now, 1)
                        dve.tensor_scalar(dst_now[r][:], edges[1][:, at_tile(t, 0)], float(NPAD), None, ALU.min).then_inc(s_now, 1)
                        dve.tensor_scalar(dst_f[r][:], edges[1][:, at_tile(t, 0)], float(NPAD), None, ALU.min).then_inc(s_now, 1)
                        dve.wait_ge(s_now, 3 * (t + 1))
                        wait(dve, s_dst, t - 1)
                        dve.tensor_scalar(diag[r % 2][:], m.ident[:], dst_f[r][:], None, ALU.mult).then_inc(s_diag, 1)

                    def add(t, r, u):
                        now(t, r, u)
                        dve.wait_ge(s_dst, t + 1)
                        wait(dve, s_part, t - 1)
                        dve.tensor_scalar(equal[r % 2][:], dst_ps[r % 2][:, 0:P], dst_f[r][:], None, ALU.is_equal).then_inc(s_equal, 1)
                        dve.wait_ge(s_part, t + 1)
                        dve.wait_ge(s_old[r], 16 * (u + 1))
                        dve.tensor_tensor(new[r][:], sums[r][:], part_ps[r % 2][:, 0:D], ALU.add).then_inc(s_new, 1)

                    for_slots(dve, add, CH, RING)

                    def scale(t, r, u):
                        dve.wait_ge(s_final[r], 16 * (u + 1))
                        wait(dve, s.tr, t - 1)
                        dve.tensor_scalar(s.z_t[r][:], final[r][:], m.dis[:, at_tile(t, 0)], None, ALU.mult).then_inc(s.z, 1)
                        if not isinstance(t, int) or t >= 1:
                            tail_stats(dve, t - 1, 1 - r, m, s)

                    for_slots(dve, scale, NT, 2)
                    tail_stats(dve, NT - 1, (NT - 1) % 2, m, s, LAST)

            @block.tensor
            def _(pe):
                with when(pe, m, BAD):
                    def add(t, r, u):
                        pe.wait_ge(s_diag, t + 1)
                        wait(pe, s_equal, t - 1)
                        pe.matmul(dst_ps[r % 2][:, 0:P], m.ones[:], diag[r % 2][:], start=True, stop=True).then_inc(s_dst, 1)
                        pe.wait_ge(s_equal, t + 1)
                        pe.wait_ge(s_h[r], 16 * (u + 1))
                        wait(pe, s_new, t - 1)
                        pe.matmul(part_ps[r % 2][:, 0:D], equal[r % 2][:], h_rows[r][:], start=True, stop=True).then_inc(s_part, 1)

                    for_slots(pe, add, CH, RING)
                    for_slots(pe, lambda t, r, u: tail_transpose(pe, t, r, m, s), NT, 2)

            @block.scalar
            def _(act):
                with when(act, m, BAD):
                    for_slots(act, lambda t, r, u: tail_relu(act, t, r, u, m, s), NT, 2)

            @block.gpsimd
            def _(pool):
                with when(pool, m, BAD):
                    for r in range(2):
                        pool.wait_ge(s_stored[r], 32 * ((NT + 2 - r) // 2))

                    def add(t, r, u):
                        pool.wait_ge(s_now, 3 * (t + 1))
                        wait(pool, s_part, t - RING + 1)
                        wait(pool, s_sent[(r + 3) % RING], 16 * (u + 1 if r > 0 else u))
                        wait(pool, s_new, t - RING + 1)
                        pool.sem_inc(s_seen, 1)
                        pool.indirect_dma_start(out=sums[r][:], out_offset=None, in_=sum_at,
                                                in_offset=bass.IndirectOffsetOnAxis(ap=dst_now[r][:], axis=0)).then_inc(s_old[r], 16)
                        pool.indirect_dma_start(out=h_rows[r][:], out_offset=None, in_=h_at,
                                                in_offset=bass.IndirectOffsetOnAxis(ap=src_now[r][:], axis=0)).then_inc(s_h[r], 16)
                        pool.wait_ge(s_new, t + 1)
                        pool.sem_inc(s_seen2, 1)
                        pool.indirect_dma_start(out=sum_at, out_offset=bass.IndirectOffsetOnAxis(ap=dst_now[r][:], axis=0),
                                                in_=new[r][:], in_offset=None).then_inc(s_sent[r], 16)

                    for_slots(pool, add, CH, RING)


def norm_stage(nc, m, tag, gain, shift):
    with ExitStack() as ctx:
        mv = ctx.enter_context(nc.sbuf_tensor("bn_mv" + tag, [P, 2, 2], F32))
        root = ctx.enter_context(nc.sbuf_tensor("bn_root" + tag, [P, 2], F32))
        inv = ctx.enter_context(nc.sbuf_tensor("bn_inv" + tag, [P, 2], F32))
        off = ctx.enter_context(nc.sbuf_tensor("bn_off" + tag, [P, 2], F32))
        s_mv, s_root, s_dve = (m.sem(n + tag) for n in ("bn_mv_ready", "bn_root_ready", "bn_step"))
        with nc.Block() as block:
            @block.vector
            def _(dve):
                for c in range(2):
                    last = dve.bn_aggr(mv[:, c, :], m.stats[:, c, :])
                last.then_inc(s_mv, 1)
                dve.wait_ge(s_root, 1)
                step = Chain(dve, s_dve)
                step(dve.reciprocal(inv[:], root[:]))
                step(dve.tensor_tensor(m.scale[:], inv[:], gain[:], ALU.mult))
                step(dve.tensor_tensor(off[:], mv[:, :, 0], m.scale[:], ALU.mult))
                step(dve.tensor_tensor(m.offset[:], shift[:], off[:], ALU.subtract))

            @block.scalar
            def _(act):
                act.wait_ge(s_mv, 1)
                act.activation(root[:], mv[:, :, 1], ACT.Sqrt, bias=m.eps[:, 0:1]).then_inc(s_root, 1)


def load_zt(sp, t, r, u, m, zt, s_in, s_free, free):
    at = tile_at(sp, m.zT, t, D, F32)
    wait(sp, s_free, free)
    sp.dma_start(zt[r][:].rearrange("p c n -> p (c n)"), at).then_inc(s_in[r], 16)


def project_stage(nc, m, w_dram):
    RING = 4
    with ExitStack() as ctx:
        s = project_buffers(ctx, nc, m, "1")
        zt = [ctx.enter_context(nc.sbuf_tensor(f"zt_in{i}", [P, 2, P], F32)) for i in range(RING)]
        w = ctx.enter_context(nc.sbuf_tensor("w1_sb", [P, 2, D], F32))
        s_in = [m.sem(f"zt_loaded{i}") for i in range(RING)]
        s_w = m.sem("w1_in")

        with nc.Block() as block:
            @block.sync
            def _(sp):
                sp.dma_start(w[:], w_dram.rearrange("(k p) n -> p k n", p=P)).then_inc(s_w, 16)
                for_slots(sp, lambda t, r, u: load_zt(sp, t, r, u, m, zt, s_in, s.lhs, 2 * (t - RING + 1)), NT, RING)

            @block.scalar
            def _(act):
                def tile(t, r, u):
                    act.wait_ge(s_in[r], 16 * (u + 1))
                    wait(act, s.h, t - 1)
                    for c in range(2):
                        act.activation(s.lhs_t[r % 2][:, c, :], zt[r][:, c, :], ACT.Identity, bias=m.offset[:, c:c + 1],
                                       scale=m.scale[:, c:c + 1]).then_inc(s.lhs, 1)
                    if not isinstance(t, int) or t > 0:
                        project_scale(act, t - 1, r + 1, m, s)

                for_slots(act, tile, NT, RING)
                project_scale(act, NT - 1, NT - 1, m, s)

            @block.tensor
            def _(pe):
                pe.wait_ge(s_w, 16)

                def tile(t, r, u):
                    pe.wait_ge(s.lhs, 2 * (t + 1))
                    project_pe(pe, t, r, m, s, w)

                for_slots(pe, tile, NT, RING)

            @block.vector
            def _(dve):
                for_slots(dve, lambda t, r, u: project_split(dve, t, r, m, s), NT, RING)


def for_slots(engine, body, total, ring):
    rounds = total // ring - 1
    for t in range(ring):
        body(t, t, 0)
    if rounds > 0:
        with engine.Fori(0, rounds) as i:
            for k in range(ring):
                body(i * ring + (ring + k), k, i + 1)
    for t in range(ring * (1 + max(rounds, 0)), total):
        body(t, t % ring, t // ring)


def product_stage(nc, m):
    SPLIT = 30
    with ExitStack() as ctx:
        sem = m.sem

        s = tail_buffers(ctx, nc, m, "_p", m.b1)
        counts = [ctx.enter_context(nc.sbuf_tensor(f"wide{i}", [P, NT, P], F32R)) for i in range(2)]
        bytes_ = [ctx.enter_context(nc.sbuf_tensor(f"bytes_in{i}", [P, NT, P], U8)) for i in range(2)]
        s_in = [sem(f"bytes_loaded{i}") for i in range(2)]
        s_v, s_a = sem("wide_by_vector"), sem("wide_by_scalar")

        def steps(engine, body):
            for t in range(4):
                body(t, t % 2, t // 2, True, t >= 1)
            with engine.Fori(0, (NT - 7) // 2) as i:
                for k in range(2):
                    body(i * 2 + (4 + k), k, i + 2, True, True)
            for t in range(NT - 3, NT):
                body(t, t % 2, t // 2, True, True)
            body(NT, NT % 2, NT // 2, False, True)

        def widen(engine, t, r, u, first, end, s_done):
            engine.wait_ge(s_in[r], 16 * (u + 1))
            wait(engine, s.sum, t - 1)
            if s_done is s_v:
                engine.tensor_copy(counts[r][:, first:end, :], bytes_[r][:, first:end, :]).then_inc(s_done, 1)
            else:
                engine.activation(counts[r][:, first:end, :], bytes_[r][:, first:end, :], ACT.Copy).then_inc(s_done, 1)

        with nc.Block() as block:
            @block.sync
            def _(sp):
                with when(sp, m, GOOD):
                    def load(t, r):
                        at = tile_at(sp, m.counts, t, NPAD, U8)
                        wait(sp, s_v, t - 1)
                        wait(sp, s_a, t - 1)
                        sp.dma_start(bytes_[r][:].rearrange("p h n -> p (h n)"), at).then_inc(s_in[r], 16)

                    def step(t, r, u, prod, tail):
                        if not isinstance(t, int) or t + 2 < NT:
                            load(t + 2, r)
                        if tail:
                            tail_store(sp, t - 1, 1 - r, m, s)

                    load(0, 0)
                    load(1, 1)
                    steps(sp, step)
                    tail_stored(sp, s)

            @block.vector
            def _(dve):
                with when(dve, m, GOOD):
                    def step(t, r, u, prod, tail):
                        if tail:
                            tail_add(dve, t - 1, 1 - r, m, s)
                        if not isinstance(t, int) or t + 1 < NT:
                            widen(dve, t + 1, 1 - r, u + r, 0, SPLIT, s_v)
                        if tail:
                            tail_stats(dve, t - 1, 1 - r, m, s, LAST if isinstance(t, int) and t - 1 == NT - 1 else P)

                    widen(dve, 0, 0, 0, 0, SPLIT, s_v)
                    steps(dve, step)

            @block.scalar
            def _(act):
                with when(act, m, GOOD):
                    def step(t, r, u, prod, tail):
                        if tail:
                            tail_low(act, t - 1, 1 - r, m, s)
                        if not isinstance(t, int) or t + 1 < NT:
                            widen(act, t + 1, 1 - r, u + r, SPLIT, NT, s_a)
                        if tail:
                            tail_relu(act, t - 1, 1 - r, u + (r - 1), m, s)

                    widen(act, 0, 0, 0, SPLIT, NT, s_a)
                    steps(act, step)

            @block.tensor
            def _(pe):
                with when(pe, m, GOOD):
                    def step(t, r, u, prod, tail):
                        if prod:
                            pe.wait_ge(s_v, t + 1)
                            wait(pe, s.z, t - 1)
                        for h in range(NT):
                            if h == 16 and tail:
                                tail_transpose(pe, t - 1, 1 - r, m, s)
                            if h == SPLIT and prod:
                                pe.wait_ge(s_a, t + 1)
                            if prod:
                                last = pe.matmul(s.sum_ps[r][:], counts[r][:, h, :], m.h[:, h, :, :].rearrange("p a d -> p (a d)"),
                                                 start=(h == 0), stop=(h == NT - 1))
                        if prod:
                            last.then_inc(s.sum, 1)

                    steps(pe, step)


def gate_stage(nc, m, x, gate_w, gate_b):
    RING = 4
    with ExitStack() as ctx:
        sem = m.sem

        def sb(name, shape, dt=F32):
            return ctx.enter_context(nc.sbuf_tensor(name, shape, dt))

        def ps(name, n):
            return [ctx.enter_context(nc.psum_tensor(f"{name}{i}", [P, 512], F32)) for i in range(n)]

        zt = [sb(f"zt_gate{i}", [P, 2, P]) for i in range(RING)]
        xin = [sb(f"x_gate{i}", [P, D]) for i in range(RING)]
        zn = [sb(f"zn{i}", [P, 2, P]) for i in range(2)]
        x1 = [sb(f"x1_{i}", [P, D]) for i in range(RING)]
        xn = [sb(f"xn{i}", [P, D]) for i in range(RING)]
        xnT = [sb(f"xnT{i}", [P, 2, P]) for i in range(2)]
        st = [sb(f"ln1_stats{i}", [P, 6]) for i in range(2)]
        mv = [sb(f"ln1_mv{i}", [P, 2]) for i in range(2)]
        root = [sb(f"ln1_root{i}", [P, 1]) for i in range(2)]
        rstd = [sb(f"ln1_rstd{i}", [P, 1]) for i in range(2)]
        gw = sb("gate_w_sb", [P, 2, NE])
        gb = sb("gate_b_sb", [P, NE])
        zps, xps, gps = ps("z_back_ps", 2), ps("xn_t_ps", 2), ps("gate_ps", 2)
        s_zt = [sem(f"zt_gate_in{i}") for i in range(RING)]
        s_x = [sem(f"x_gate_in{i}") for i in range(RING)]
        s_x1o = [sem(f"x1_stored{i}") for i in range(RING)]
        s_xno = [sem(f"xn_stored{i}") for i in range(RING)]
        (s_w, s_zero, s_zn, s_zb, s_x1, s_st, s_seen, s_mv, s_root, s_rstd, s_xn, s_xt, s_xc, s_g, s_lg) = (sem(n) for n in (
            "gate_w_in", "x_gate_tail_zeroed", "zn_ready", "z_back", "x1_ready", "ln1_stats_ready", "ln1_stats_seen", "ln1_mv_ready",
            "ln1_root_ready", "ln1_rstd_ready", "xn1_ready", "xn1_transposed", "xn1_t_copied", "gate_ready", "logit_ready"))

        def steps(engine, body):
            for t in range(8):
                body(t, t % RING, t // RING)
            with engine.Fori(0, 10) as i:
                for k in range(4):
                    body(i * 4 + (8 + k), k, i + 2)
            for t in range(48, NT + 3):
                body(t, t % RING, t // RING)

        def has(t, lag):
            return not isinstance(t, int) or 0 <= t - lag < NT

        with nc.Block() as block:
            @block.sync
            def _(sp):
                sp.dma_start(gw[:], gate_w.rearrange("(k p) n -> p k n", p=P)).then_inc(s_w, 16)
                sp.dma_start(gb[:], gate_b.rearrange("(a n) -> a n", a=1).to_broadcast([P, NE])).then_inc(s_w, 16)

                def step(t, r, u):
                    if has(t, 0):
                        load_zt(sp, t, r, u, m, zt, s_zt, s_zn, 2 * (t - RING + 1))
                        at = None if isinstance(t, int) and t == NT - 1 else tile_at(sp, x.rearrange("n d -> (n d)").bitcast(U8), t, D, F32)
                        wait(sp, s_x1, t - RING + 1)
                        if at is None:
                            sp.wait_ge(s_zero, 1)
                            sp.dma_start(xin[r][0:LAST, :], x[(NT - 1) * P:N, :]).then_inc(s_x[r], 16)
                        else:
                            sp.dma_start(xin[r][:], at).then_inc(s_x[r], 16)
                    if has(t, 2):
                        q = (r + 2) % 4
                        at = tile_at(sp, m.x1, t - 2, D, F32)
                        sp.wait_ge(s_x1, t - 1)
                        sp.dma_start(at, x1[q][:]).then_inc(s_x1o[q], 16)
                    if has(t, 3):
                        q = (r + 1) % 4
                        at = tile_at(sp, m.xn, t - 3, D, F32)
                        sp.wait_ge(s_xn, t - 2)
                        sp.dma_start(at, xn[q][:]).then_inc(s_xno[q], 16)

                steps(sp, step)
                for r in range(RING):
                    sp.wait_ge(s_x1o[r], 16 * ((NT + RING - 1 - r) // RING))
                    sp.wait_ge(s_xno[r], 16 * ((NT + RING - 1 - r) // RING))

            @block.scalar
            def _(act):
                def step(t, r, u):
                    if has(t, 0):
                        act.wait_ge(s_zt[r], 16 * (u + 1))
                        wait(act, s_zb, t - 1)
                        for c in range(2):
                            act.activation(zn[r % 2][:, c, :], zt[r][:, c, :], ACT.Identity, bias=m.offset[:, c:c + 1],
                                           scale=m.scale[:, c:c + 1]).then_inc(s_zn, 1)
                    if has(t, 1):
                        q = (r + 1) % 2
                        act.wait_ge(s_mv, t)
                        wait(act, s_rstd, t - 2)
                        act.activation(root[q][:], mv[q][:, 1:2], ACT.Sqrt, bias=m.eps[:, 0:1]).then_inc(s_root, 1)
                    if has(t, 2):
                        act.wait_ge(s_xt, t - 1)
                        wait(act, s_g, t - 3)
                        act.activation(xnT[r % 2][:].rearrange("p c n -> p (c n)"), xps[r % 2][:, 0:D], ACT.Copy).then_inc(s_xc, 1)

                steps(act, step)

            @block.tensor
            def _(pe):
                pe.wait_ge(s_w, 32)

                def step(t, r, u):
                    if has(t, 0):
                        pe.wait_ge(s_zn, 2 * (t + 1))
                        wait(pe, s_x1, t - 1)
                        for c in range(2):
                            last = pe.transpose(zps[r % 2][:, c * P:(c + 1) * P], zn[r % 2][:, c, :], m.ident[:])
                        last.then_inc(s_zb, 1)
                    if has(t, 2):
                        pe.wait_ge(s_xn, t - 1)
                        wait(pe, s_xc, t - 3)
                        for c in range(2):
                            last = pe.transpose(xps[r % 2][:, c * P:(c + 1) * P], xn[(r + 2) % 4][:, c * P:(c + 1) * P], m.ident[:])
                        last.then_inc(s_xt, 1)
                    if has(t, 3):
                        q = (r + 1) % 2
                        pe.wait_ge(s_xc, t - 2)
                        wait(pe, s_lg, t - 4)
                        for c in range(2):
                            last = pe.matmul(gps[q][:, 0:NE], xnT[q][:, c, :], gw[:, c, :], start=(c == 0), stop=(c == 1))
                        last.then_inc(s_g, 1)

                steps(pe, step)

            @block.vector
            def _(dve):
                def step(t, r, u):
                    if isinstance(t, int) and t == NT - 1:
                        dve.wait_ge(s_x1, t - RING + 1)
                        dve.memset(xin[r][96:P, :], 0.0).then_inc(s_zero, 1)
                    if has(t, 0):
                        dve.wait_ge(s_zb, t + 1)
                        dve.wait_ge(s_x[r], 16 * (u + 1))
                        wait(dve, s_x1o[r], 16 * u)
                        dve.tensor_tensor(x1[r][:], zps[r % 2][:, 0:D], xin[r][:], ALU.add).then_inc(s_x1, 1)
                        dve.wait_ge(s_x1, t + 1)
                        wait(dve, s_mv, t - 1)
                        dve.bn_stats(st[r % 2][:], x1[r][:]).then_inc(s_st, 1)
                    if has(t, 1):
                        p, q = (r + 3) % 4, (r + 1) % 2
                        dve.wait_ge(s_root, t)
                        dve.reciprocal(rstd[q][:], root[q][:]).then_inc(s_rstd, 1)
                        dve.wait_ge(s_rstd, t)
                        wait(dve, s_xno[p], 16 * (u if r > 0 else u - 1))
                        wait(dve, s_xt, t - RING)
                        dve.tensor_scalar(xn[p][:], x1[p][:], mv[q][:, 0:1], rstd[q][:], ALU.subtract, ALU.mult).then_inc(s_xn, 1)
                    if has(t, 0):
                        dve.wait_ge(s_st, t + 1)
                        wait(dve, s_root, t - 1)
                        wait(dve, s_xn, t - 1)
                        dve.sem_inc(s_seen, 1)
                        dve.bn_aggr(mv[r % 2][:], st[r % 2][:]).then_inc(s_mv, 1)
                    if has(t, 3):
                        q = (r + 1) % 2
                        dve.wait_ge(s_g, t - 2)
                        dve.tensor_tensor(m.logits[:, at_tile(t, -3), :], gps[q][:, 0:NE].unsqueeze(1), gb[:].unsqueeze(1),
                                          ALU.add).then_inc(s_lg, 1)

                steps(dve, step)


def at_tile(t, lag):
    return slice(t + lag, t + lag + 1) if isinstance(t, int) else bass.ds(t + lag, 1)


def route_stage(nc, m):
    TE = NT * NE
    HALF = TE // 2
    with ExitStack() as ctx:
        sem = m.sem

        def sb(name, shape, dt=F32):
            return ctx.enter_context(nc.sbuf_tensor(name, shape, dt))

        rank_i, rank = sb("rank_i", [P, NE], I32), sb("rank", [P, NE])
        tile_i, tile_f = sb("tile_i", [1, MT], I32), sb("tile_f", [1, MT])
        below = sb("below_diag", [P, P])
        valid = sb("valid", [P, NT])
        rest, score = sb("rest", [P, NT, NE]), sb("score", [P, NT, NE])
        one = [sb(f"one{i}", [P, NT, NE]) for i in range(2)]
        both, place = sb("both", [P, NT, NE]), sb("place", [P, NT, NE])
        run = [sb(f"run{i}", [P, NT, NE]) for i in range(2)]
        top = [sb(f"top{i}", [P, NT]) for i in range(2)]
        most, total = sb("most", [P, NT]), sb("weight_sum", [P, NT])
        ntile_i = sb("ntile_i", [P, NE], I32)
        end = [sb(f"end{i}", [P, NE]) for i in range(2)]
        start = sb("expert_start", [P, NE])
        done = sb("done", [1, MT, NE])
        slot_f = sb("slot_f", [P, NT])
        exp_f = sb("expert_f", [1, MT])
        pre = ctx.enter_context(nc.psum_tensor("prefix_ps", [P, 2, 512], F32))
        tot = ctx.enter_context(nc.psum_tensor("total_ps", [P, 2, 512], F32))
        s_pool, s_ready, s_dve, s_oh, s_mm, s_diff, s_e = (sem(n) for n in (
            "route_pool_step", "route_constants", "route_step", "one_hots_ready", "ranks_ready", "gap_ready", "exp_ready"))

        with nc.Block() as block:
            @block.gpsimd
            def _(pool):
                step = Chain(pool, s_pool)
                pool.iota(rank_i[:], pattern=[[-1, NE]], base=NE, channel_multiplier=0).then_inc(s_ready, 1)
                pool.iota(tile_i[:], pattern=[[1, MT]], base=0, channel_multiplier=0).then_inc(s_ready, 1)
                step(pool.memset(below[:], 1.0))
                pool.affine_select(out=below[:], in_=below[:], compare_op=ALU.is_gt, fill=0.0, base=0,
                                   pattern=[[1, P]], channel_multiplier=-1).then_inc(s_ready, 1)
                step(pool.memset(valid[:], 1.0))
                pool.affine_select(out=valid[:, NT - 1:NT], in_=valid[:, NT - 1:NT], compare_op=ALU.is_gt, fill=0.0, base=LAST,
                                   pattern=[[0, 1]], channel_multiplier=-1).then_inc(s_ready, 1)

            @block.vector
            def _(dve):
                step = Chain(dve, s_dve)
                wide = [P, NT, NE]
                dve.wait_ge(s_ready, 4)
                step(dve.tensor_copy(rank[:], rank_i[:]))
                step(dve.tensor_copy(tile_f[:], tile_i[:]))
                for k, values in enumerate((m.logits, rest)):
                    step(dve.reduce_max(top[k][:], values[:], AX.X))
                    step(dve.tensor_tensor(score[:], values[:], top[k][:].unsqueeze(2).to_broadcast(wide), ALU.is_equal))
                    step(dve.tensor_tensor(score[:], score[:], rank[:].unsqueeze(1).to_broadcast(wide), ALU.mult))
                    step(dve.reduce_max(most[:], score[:], AX.X))
                    step(dve.tensor_tensor(one[k][:], score[:], most[:].unsqueeze(2).to_broadcast(wide), ALU.is_equal))
                    if k == 0:
                        step(dve.scalar_tensor_tensor(out=rest[:].rearrange("p t e -> p (t e)"), in0=one[0][:].rearrange("p t e -> p (t e)"),
                                                      scalar=-3.0e38, in1=m.logits[:].rearrange("p t e -> p (t e)"),
                                                      op0=ALU.mult, op1=ALU.add))
                for k in range(2):
                    step(dve.tensor_tensor(one[k][:], one[k][:], valid[:].unsqueeze(2).to_broadcast(wide), ALU.mult))
                step(dve.tensor_tensor(both[:], one[0][:], one[1][:], ALU.add))
                dve.sem_inc(s_oh, 1)
                dve.tensor_tensor(m.weight[1][:], top[1][:], top[0][:], ALU.subtract).then_inc(s_diff, 1)
                dve.wait_ge(s_e, 1)
                step(dve.tensor_scalar(total[:], m.weight[1][:], 1.0, None, ALU.add))
                step(dve.reciprocal(m.weight[0][:], total[:]))
                step(dve.tensor_tensor(m.weight[1][:], m.weight[1][:], m.weight[0][:], ALU.mult))
                dve.wait_ge(s_mm, 1)
                for c in range(2):
                    flat = run[0][:].rearrange("p t e -> p (t e)")
                    step(dve.tensor_copy(flat[:, c * HALF:(c + 1) * HALF], tot[:, c, 0:HALF]))
                a, b, d = 0, 1, 1
                while d < NT:
                    step(dve.tensor_copy(run[b][:, 0:d, :], run[a][:, 0:d, :]))
                    step(dve.tensor_tensor(run[b][:, d:NT, :], run[a][:, d:NT, :], run[a][:, 0:NT - d, :], ALU.add))
                    a, b, d = b, a, 2 * d
                step(dve.tensor_scalar(start[:], run[a][:, NT - 1, :], float(P - 1), None, ALU.add))
                step(dve.tensor_copy(ntile_i[:], start[:]))
                step(dve.tensor_scalar(ntile_i[:], ntile_i[:], 7, None, ALU.arith_shift_right))
                step(dve.tensor_copy(end[0][:], ntile_i[:]))
                step(dve.tensor_copy(start[:], end[0][:]))
                x, y, d = 0, 1, 1
                while d < NE:
                    step(dve.tensor_copy(end[y][:, 0:d], end[x][:, 0:d]))
                    step(dve.tensor_tensor(end[y][:, d:NE], end[x][:, d:NE], end[x][:, 0:NE - d], ALU.add))
                    x, y, d = y, x, 2 * d
                step(dve.tensor_tensor(start[:], end[x][:], start[:], ALU.subtract))
                step(dve.tensor_scalar(start[:], start[:], float(P), None, ALU.mult))
                for c in range(2):
                    flat, place_f = run[a][:].rearrange("p t e -> p (t e)"), place[:].rearrange("p t e -> p (t e)")
                    span = slice(c * HALF, (c + 1) * HALF)
                    step(dve.tensor_tensor(place_f[:, span], flat[:, span], tot[:, c, 0:HALF], ALU.subtract))
                    step(dve.tensor_tensor(place_f[:, span], place_f[:, span], pre[:, c, 0:HALF], ALU.add))
                step(dve.tensor_tensor(place[:], place[:], start[:].unsqueeze(1).to_broadcast(wide), ALU.add))
                for k in range(2):
                    step(dve.tensor_tensor(score[:], place[:], one[k][:], ALU.mult))
                    step(dve.reduce_sum(slot_f[:], score[:], AX.X))
                    step(dve.tensor_copy(m.slot[k][:], slot_f[:]))
                step(dve.tensor_tensor(done[:], end[x][0:1, :].unsqueeze(1).to_broadcast([1, MT, NE]),
                                       tile_f[:].unsqueeze(2).to_broadcast([1, MT, NE]), ALU.is_le))
                step(dve.reduce_sum(exp_f[:], done[:], AX.X))
                step(dve.tensor_scalar(m.expert[:], exp_f[:], float(NE - 1), None, ALU.min))

            @block.scalar
            def _(act):
                act.wait_ge(s_diff, 1)
                act.activation(m.weight[1][:], m.weight[1][:], ACT.Exp).then_inc(s_e, 1)

            @block.tensor
            def _(pe):
                pe.wait_ge(s_oh, 1)
                for c in range(2):
                    part = both[:].rearrange("p t e -> p (t e)")[:, c * HALF:(c + 1) * HALF]
                    pe.matmul(pre[:, c, 0:HALF], below[:], part, start=True, stop=True)
                    last = pe.matmul(tot[:, c, 0:HALF], m.ones[:], part, start=True, stop=True)
                last.then_inc(s_mm, 1)


def scatter_stage(nc, m, ew1, eb1, ew2, eb2):
    RING = 4
    ROUND = MT // 6
    with ExitStack() as ctx:
        sem = m.sem

        zero = ctx.enter_context(nc.sbuf_tensor("zero_rows", [P, ROUND * D], F32))
        xn = [ctx.enter_context(nc.sbuf_tensor(f"xn_s{i}", [P, D], F32)) for i in range(RING)]
        at = [[ctx.enter_context(nc.sbuf_tensor(f"at{k}_{i}", [P, 1], I32)) for i in range(RING)] for k in range(2)]
        brow = ctx.enter_context(nc.sbuf_tensor("bias_rows", [P, 96], F32))
        bres = ctx.enter_context(nc.sbuf_tensor("bias_rest", [P, 96], F32))
        bpart = ctx.enter_context(nc.sbuf_tensor("bias_parts", [P, 3, 96], BF16))
        s_w, s_b, s_zero, s_zeroed, s_dve, s_parts, s_pst, s_pin = (sem(n) for n in (
            "expert_weights_in", "expert_bias_in", "zero_set", "slots_zeroed", "bias_step", "bias_parts_ready", "bias_parts_stored", "bias_parts_in"))
        s_in = [sem(f"xn_s_in{i}") for i in range(RING)]
        s_seen = sem("send_may_start")
        s_at, s_sent = sem("at_ready"), [sem(f"rows_sent{i}") for i in range(RING)]

        with nc.Block() as block:
            @block.sync
            def _(sp):
                sp.dma_start(brow[:, 0:64], eb1.rearrange("e f -> (e f)").rearrange("(p n) -> p n", p=P)).then_inc(s_b, 16)
                sp.dma_start(brow[:, 64:96], eb2.rearrange("e f -> (e f)").rearrange("(p n) -> p n", p=P)).then_inc(s_b, 16)
                sp.wait_ge(s_zero, 1)
                for g in range(MT // ROUND):
                    sp.dma_start(m.rows[g * ROUND * P:(g + 1) * ROUND * P, :].rearrange("(p n) d -> p (n d)", p=P), zero[:]).then_inc(s_zeroed, 16)

                def load(t, r, u):
                    src = tile_at(sp, m.xn, t, D, F32)
                    wait(sp, s_sent[r], 32 * u)
                    sp.dma_start(xn[r][:], src).then_inc(s_in[r], 16)

                for_slots(sp, load, NT, RING)
                sp.wait_ge(s_parts, 1)
                for k in range(3):
                    sp.dma_start(m.b1_parts[k, :].rearrange("(p n) -> p n", p=P), bpart[:, k, 0:64]).then_inc(s_pst, 16)
                    sp.dma_start(m.b2_parts[k, :].rearrange("(p n) -> p n", p=P), bpart[:, k, 64:96]).then_inc(s_pst, 16)
                sp.wait_ge(s_pst, 96)
                sp.dma_start(m.eb1[:].rearrange("k e f -> k (e f)"), m.b1_parts).then_inc(s_pin, 16)
                sp.dma_start(m.eb2[:].rearrange("k e f -> k (e f)"), m.b2_parts).then_inc(s_pin, 16)
                sp.wait_ge(s_pin, 32)

            @block.scalar
            def _(act):
                for k in range(2):
                    act.dma_start(m.ew1[:, k, :, :], ew1[:, k * P:(k + 1) * P, :].rearrange("e p f -> p e f")).then_inc(s_w, 16)
                for k in range(4):
                    act.dma_start(m.ew2[:, k, :, :], ew2[:, k * P:(k + 1) * P, :].rearrange("e p f -> p e f")).then_inc(s_w, 16)
                act.wait_ge(s_w, 96)

            @block.vector
            def _(dve):
                dve.memset(zero[:], 0.0).then_inc(s_zero, 1)
                step = Chain(dve, s_dve)
                step(dve.memset(m.ones_bf[:], 1.0))
                dve.wait_ge(s_b, 32)
                step(dve.tensor_copy(bpart[:, 0, :], brow[:]))
                step(dve.tensor_tensor(bres[:], brow[:], bpart[:, 0, :], ALU.subtract))
                step(dve.tensor_copy(bpart[:, 1, :], bres[:]))
                step(dve.tensor_tensor(brow[:], bres[:], bpart[:, 1, :], ALU.subtract))
                step(dve.tensor_copy(bpart[:, 2, :], brow[:]))
                dve.sem_inc(s_parts, 1)

                def index(t, r, u):
                    wait(dve, s_sent[r], 32 * u)
                    for k in range(2):
                        dve.tensor_copy(at[k][r][:], m.slot[k][:, at_tile(t, 0)]).then_inc(s_at, 1)

                for_slots(dve, index, NT, RING)

            @block.gpsimd
            def _(pool):
                pool.wait_ge(s_zeroed, 16 * (MT // ROUND))

                def send(t, r, u):
                    n = LAST if isinstance(t, int) and t == NT - 1 else P
                    pool.wait_ge(s_in[r], 16 * (u + 1))
                    pool.wait_ge(s_at, 2 * (t + 1))
                    pool.sem_inc(s_seen, 1)
                    for k in range(2):
                        pool.indirect_dma_start(out=m.rows, out_offset=bass.IndirectOffsetOnAxis(ap=at[k][r][0:n, :], axis=0),
                                                in_=xn[r][0:n, :], in_offset=None).then_inc(s_sent[r], 16)

                for_slots(pool, send, NT, RING)
                for r in range(RING):
                    pool.wait_ge(s_sent[r], 32 * ((NT + RING - 1 - r) // RING))


def expert_stage(nc, m):
    RING = 2
    with ExitStack() as ctx:
        sem = m.sem

        def sb(name, shape, n, dt=F32):
            return [ctx.enter_context(nc.sbuf_tensor(f"{name}{i}", shape, dt)) for i in range(n)]

        def ps(name):
            return [ctx.enter_context(nc.psum_tensor(f"{name}{i}", [P, 512], F32)) for i in range(2)]

        xe, xT, hid, hT, ye = sb("xe", [P, D], 4), sb("xeT", [P, 2, P], 2), sb("hid", [P, FF], 2), sb("hidT", [P, 4, P], 2), sb("ye", [P, D], 4)
        xps, hps, tps, yps = ps("xe_ps"), ps("hid_ps"), ps("hidT_ps"), ps("ye_ps")
        s_in, s_out = [sem(f"xe_in{i}") for i in range(4)], [sem(f"ye_stored{i}") for i in range(4)]
        s_xt, s_xc, s_h, s_relu, s_ht, s_hc, s_y, s_yc = (sem(n) for n in (
            "xe_transposed", "xeT_copied", "hid_ready", "hid_relu", "hid_transposed", "hidT_copied", "ye_ready", "ye_copied"))

        def steps(engine, body):
            for t in range(8):
                body(t, t % 4, t // 4)
            rounds = (MT - 8) // 4
            with engine.Fori(0, rounds) as i:
                for k in range(4):
                    body(i * 4 + (8 + k), k, i + 2)
            for t in range(8 + 4 * rounds, MT + 3):
                body(t, t % 4, t // 4)

        def has(t, lag):
            return not isinstance(t, int) or 0 <= t - lag < MT

        with nc.Block() as block:
            @block.sync
            def _(sp):
                rows, ys = m.rows.rearrange("n d -> (n d)").bitcast(U8), m.ys.rearrange("n d -> (n d)").bitcast(U8)

                def step(t, r, u):
                    if has(t, 0):
                        at = tile_at(sp, rows, t, D, F32)
                        wait(sp, s_xt, t - 3)
                        sp.dma_start(xe[r][:], at).then_inc(s_in[r], 16)
                    if has(t, 3):
                        q = (r + 1) % 4
                        at = tile_at(sp, ys, t - 3, D, F32)
                        sp.wait_ge(s_yc, t - 2)
                        sp.dma_start(at, ye[q][:]).then_inc(s_out[q], 16)

                steps(sp, step)
                for r in range(4):
                    sp.wait_ge(s_out[r], 16 * ((MT + 3 - r) // 4))

            @block.tensor
            def _(pe):
                def step(t, r, u):
                    if has(t, 0):
                        pe.wait_ge(s_in[r], 16 * (u + 1))
                        wait(pe, s_xc, t - 1)
                        for c in range(2):
                            last = pe.transpose(xps[r % 2][:, c * P:(c + 1) * P], xe[r][:, c * P:(c + 1) * P], m.ident[:])
                        last.then_inc(s_xt, 1)
                    if has(t, 2):
                        pe.wait_ge(s_relu, t - 1)
                        wait(pe, s_hc, t - 3)
                        for c in range(4):
                            last = pe.transpose(tps[r % 2][:, c * P:(c + 1) * P], hid[r % 2][:, c * P:(c + 1) * P], m.ident[:])
                        last.then_inc(s_ht, 1)
                    if has(t, 1):
                        q = (r + 1) % 2
                        e = pe.value_load(m.expert[0:1, at_tile(t, -1)], min_val=0, max_val=NE - 1)
                        pe.wait_ge(s_xc, t)
                        wait(pe, s_relu, t - 2)
                        pe.matmul(hps[q][:], m.ones_bf[:], m.eb1[:, bass.ds(e, 1), :].rearrange("k o f -> k (o f)"), start=True, stop=False)
                        for k in range(2):
                            last = pe.matmul(hps[q][:], xT[q][:, k, :], m.ew1[:, k, bass.ds(e, 1), :].rearrange("p o f -> p (o f)"),
                                             start=False, stop=(k == 1))
                        last.then_inc(s_h, 1)
                    if has(t, 3):
                        q = (r + 1) % 2
                        e = pe.value_load(m.expert[0:1, at_tile(t, -3)], min_val=0, max_val=NE - 1)
                        pe.wait_ge(s_hc, t - 2)
                        wait(pe, s_yc, t - 4)
                        pe.matmul(yps[q][:, 0:D], m.ones_bf[:], m.eb2[:, bass.ds(e, 1), :].rearrange("k o f -> k (o f)"), start=True, stop=False)
                        for k in range(4):
                            last = pe.matmul(yps[q][:, 0:D], hT[q][:, k, :], m.ew2[:, k, bass.ds(e, 1), :].rearrange("p o f -> p (o f)"),
                                             start=False, stop=(k == 3))
                        last.then_inc(s_y, 1)

                steps(pe, step)

            @block.scalar
            def _(act):
                def step(t, r, u):
                    if has(t, 0):
                        act.wait_ge(s_xt, t + 1)
                        wait(act, s_h, t - 1)
                        act.activation(xT[r % 2][:].rearrange("p c n -> p (c n)"), xps[r % 2][:, 0:D], ACT.Copy).then_inc(s_xc, 1)
                    if has(t, 1):
                        q = (r + 1) % 2
                        act.wait_ge(s_h, t)
                        wait(act, s_ht, t - 2)
                        act.activation(hid[q][:], hps[q][:], ACT.Relu).then_inc(s_relu, 1)

                steps(act, step)

            @block.vector
            def _(dve):
                def step(t, r, u):
                    if has(t, 2):
                        dve.wait_ge(s_ht, t - 1)
                        wait(dve, s_y, t - 3)
                        dve.tensor_copy(hT[r % 2][:].rearrange("p c n -> p (c n)"), tps[r % 2][:]).then_inc(s_hc, 1)
                    if has(t, 3):
                        q = (r + 1) % 4
                        dve.wait_ge(s_y, t - 2)
                        wait(dve, s_out[q], 16 * (u if r == 3 else u - 1))
                        dve.tensor_copy(ye[q][:], yps[q % 2][:, 0:D]).then_inc(s_yc, 1)

                steps(dve, step)


def combine_stage(nc, m, gamma, beta, out):
    RING = 4
    with ExitStack() as ctx:
        sem = m.sem

        def sb(name, shape, n, dt=F32):
            return [ctx.enter_context(nc.sbuf_tensor(f"{name}{i}", shape, dt)) for i in range(n)]

        gam = ctx.enter_context(nc.sbuf_tensor("gamma_sb", [P, D], F32))
        bet = ctx.enter_context(nc.sbuf_tensor("beta_sb", [P, D], F32))
        y1, y2, xn, x1, res = sb("y1_", [P, D], RING), sb("y2_", [P, D], RING), sb("xn_c", [P, D], RING), sb("x1_c", [P, D], RING), sb("res", [P, D], RING)
        at = [sb(f"from{k}_", [P, 1], RING, I32) for k in range(2)]
        part, yv, nrm = sb("part", [P, D], 2), sb("yv", [P, D], 2), sb("nrm", [P, D], 2)
        shifted = sb("shifted", [P, D], 2)
        st, mv, root, rstd = sb("ln2_stats", [P, 6], 2), sb("ln2_mv", [P, 2], 2), sb("ln2_root", [P, 1], 2), sb("ln2_rstd", [P, 1], 2)
        s_gb = sem("gamma_beta_in")
        s_in, s_got, s_out = ([sem(f"{n}{i}") for i in range(RING)] for n in ("c_rows_in", "expert_rows_in", "out_stored"))
        (s_at, s_seen, s_part, s_y, s_st, s_seen2, s_mv, s_root, s_rstd, s_nrm, s_gam, s_sh, s_res) = (sem(n) for n in (
            "from_ready", "from_seen", "c_part", "c_y", "c_stats", "c_stats_seen", "c_mv", "c_root", "c_rstd", "c_normed", "c_gamma", "c_shifted", "c_result"))

        def steps(engine, body):
            for t in range(8):
                body(t, t % RING, t // RING)
            with engine.Fori(0, 9) as i:
                for k in range(4):
                    body(i * 4 + (8 + k), k, i + 2)
            for t in range(44, NT + 1):
                body(t, t % RING, t // RING)

        def has(t, lag):
            return not isinstance(t, int) or 0 <= t - lag < NT

        with nc.Block() as block:
            @block.sync
            def _(sp):
                sp.dma_start(gam[:], gamma.rearrange("(a n) -> a n", a=1).to_broadcast([P, D])).then_inc(s_gb, 16)
                sp.dma_start(bet[:], beta.rearrange("(a n) -> a n", a=1).to_broadcast([P, D])).then_inc(s_gb, 16)
                out_bytes = out.rearrange("n d -> (n d)").bitcast(U8)

                def step(t, r, u):
                    if has(t, 0):
                        a, b = tile_at(sp, m.xn, t, D, F32), tile_at(sp, m.x1, t, D, F32)
                        wait(sp, s_res, t - RING + 1)
                        sp.dma_start(xn[r][:], a).then_inc(s_in[r], 16)
                        sp.dma_start(x1[r][:], b).then_inc(s_in[r], 16)
                    if has(t, 1):
                        q = (r + 3) % 4
                        if isinstance(t, int) and t == NT:
                            sp.wait_ge(s_res, t)
                            sp.dma_start(out[(NT - 1) * P:N, :], res[q][0:LAST, :]).then_inc(s_out[q], 16)
                        else:
                            to = tile_at(sp, out_bytes, t - 1, D, F32)
                            sp.wait_ge(s_res, t)
                            sp.dma_start(to, res[q][:]).then_inc(s_out[q], 16)

                steps(sp, step)
                for r in range(RING):
                    sp.wait_ge(s_out[r], 16 * ((NT + RING - 1 - r) // RING))

            @block.gpsimd
            def _(pool):
                def step(t, r, u):
                    if has(t, 0):
                        pool.wait_ge(s_at, 2 * (t + 1))
                        wait(pool, s_y, t - RING + 1)
                        pool.sem_inc(s_seen, 1)
                        for k, y in enumerate((y1, y2)):
                            pool.indirect_dma_start(out=y[r][:], out_offset=None, in_=m.ys,
                                                    in_offset=bass.IndirectOffsetOnAxis(ap=at[k][r][:], axis=0)).then_inc(s_got[r], 16)

                steps(pool, step)

            @block.vector
            def _(dve):
                def index(t, r, u):
                    wait(dve, s_got[r], 32 * u)
                    for k in range(2):
                        dve.tensor_copy(at[k][r][:], m.slot[k][:, at_tile(t, 0)]).then_inc(s_at, 1)

                index(0, 0, 0)
                index(1, 1, 0)
                dve.wait_ge(s_gb, 32)

                def step(t, r, u):
                    if not isinstance(t, int) or t + 2 < NT:
                        index(t + 2, (r + 2) % 4, u if r < 2 else u + 1)
                    if has(t, 0):
                        q = r % 2
                        dve.wait_ge(s_in[r], 32 * (u + 1))
                        dve.wait_ge(s_got[r], 32 * (u + 1))
                        wait(dve, s_y, t - 1)
                        dve.scalar_tensor_tensor(out=part[q][:], in0=y1[r][:], scalar=m.weight[0][:, at_tile(t, 0)], in1=xn[r][:],
                                                 op0=ALU.mult, op1=ALU.add).then_inc(s_part, 1)
                        dve.wait_ge(s_part, t + 1)
                        wait(dve, s_nrm, t - 1)
                        dve.scalar_tensor_tensor(out=yv[q][:], in0=y2[r][:], scalar=m.weight[1][:, at_tile(t, 0)], in1=part[q][:],
                                                 op0=ALU.mult, op1=ALU.add).then_inc(s_y, 1)
                        dve.wait_ge(s_y, t + 1)
                        wait(dve, s_mv, t - 1)
                        dve.bn_stats(st[q][:], yv[q][:]).then_inc(s_st, 1)
                    if has(t, 1):
                        q = (r + 1) % 2
                        dve.wait_ge(s_root, t)
                        wait(dve, s_nrm, t - 2)
                        dve.reciprocal(rstd[q][:], root[q][:]).then_inc(s_rstd, 1)
                        dve.wait_ge(s_rstd, t)
                        wait(dve, s_gam, t - 2)
                        dve.tensor_scalar(nrm[q][:], yv[q][:], mv[q][:, 0:1], rstd[q][:], ALU.subtract, ALU.mult).then_inc(s_nrm, 1)
                    if has(t, 0):
                        q = r % 2
                        dve.wait_ge(s_st, t + 1)
                        wait(dve, s_root, t - 1)
                        wait(dve, s_nrm, t - 1)
                        dve.sem_inc(s_seen2, 1)
                        dve.bn_aggr(mv[q][:], st[q][:]).then_inc(s_mv, 1)
                    if has(t, 1):
                        q, p = (r + 1) % 2, (r + 3) % 4
                        dve.wait_ge(s_nrm, t)
                        wait(dve, s_res, t - 2)
                        dve.tensor_tensor(shifted[q][:], nrm[q][:], gam[:], ALU.mult).then_inc(s_gam, 1)
                        dve.wait_ge(s_gam, t)
                        dve.tensor_tensor(shifted[q][:], shifted[q][:], bet[:], ALU.add).then_inc(s_sh, 1)
                        dve.wait_ge(s_sh, t)
                        wait(dve, s_out[p], 16 * (u if r > 0 else u - 1))
                        dve.tensor_tensor(res[p][:], shifted[q][:], x1[p][:], ALU.add).then_inc(s_res, 1)

                steps(dve, step)

            @block.scalar
            def _(act):
                def step(t, r, u):
                    if has(t, 0):
                        q = r % 2
                        act.wait_ge(s_mv, t + 1)
                        wait(act, s_rstd, t - 1)
                        act.activation(root[q][:], mv[q][:, 1:2], ACT.Sqrt, bias=m.eps[:, 0:1]).then_inc(s_root, 1)

                steps(act, step)


def program(nc, x, src, dst, w0, b0, g0, bt0, w1, b1, g1, bt1, gate_w, gate_b, ew1, eb1, ew2, eb2, gamma, beta, out):
    def dram(name, shape, dt):
        return nc.dram_tensor(name, shape, dt).ap()

    m = Names()
    m.src_pad = dram("src_pad", [EPAD], I32)
    m.dst_pad = dram("dst_pad", [EPAD], I32)
    m.heads = dram("heads_dram", [CH], I32)
    m.deg = dram("degrees", [NBLK * BD], F32)
    m.counts = dram("counts", [NT * P * NT * P], U8)
    m.zT = dram("z_t", [NT * P * D * 4], U8)
    m.x1 = dram("x1_dram", [NT * P * D * 4], U8)
    m.xn = dram("xn_dram", [NT * P * D * 4], U8)
    m.any_h = dram("any_h_dram", [(NT + 1) * P * D * 4], U8)
    m.any_sum = dram("any_sum_dram", [(NT + 1) * P * D * 4], U8)
    m.rows = dram("expert_rows", [MT * P, D], F32)
    m.ys = dram("expert_out", [MT * P, D], F32)
    m.b1_parts = dram("b1_parts", [3, NE * FF], BF16)
    m.b2_parts = dram("b2_parts", [3, NE * D], BF16)
    m.sem = Semaphores(nc)
    with ExitStack() as ctx:
        def sb(name, shape, dt):
            return ctx.enter_context(nc.sbuf_tensor(name, shape, dt))

        m.iota16 = sb("iota16", [P, 512], FP16)
        m.ident, m.ones = sb("ident", [P, P], F32), sb("ones", [P, P], F32)
        m.flags = sb("flags", [P, 2], I32)
        m.dis = sb("dis", [P, NT], F32)
        m.eps = sb("eps", [P, 1], F32)
        m.stats = sb("z_stats", [P, 2, NT * 6], F32)
        m.b0, m.b1, m.g0, m.g1, m.bt0, m.bt1 = (sb(n, [P, 2], F32) for n in ("b0_sb", "b1_sb", "g0_sb", "g1_sb", "bt0_sb", "bt1_sb"))
        m.scale, m.offset = sb("bn_scale", [P, 2], F32), sb("bn_offset", [P, 2], F32)
        with nc.sbuf_tensor("keyT", [P, NBLK, 3], FP16) as m.keyT, nc.sbuf_tensor("loT", [P, NBLK, 3], FP16) as m.loT:
            edge_stage(nc, m, src, dst)
            parameter_stage(nc, m, [(m.b0, b0), (m.g0, g0), (m.bt0, bt0), (m.b1, b1), (m.g1, g1), (m.bt1, bt1)])
            dis_stage(nc, m)
            any_degrees(nc, m)
            with nc.sbuf_tensor("h", [P, NT, 2, D], F32R) as m.h:
                input_stage(nc, m, x, w0)
                build_stage(nc, m)
                m.sem.renew()
                any_sums(nc, m, "_any0", m.b0)
                norm_stage(nc, m, "0", m.g0, m.bt0)
                project_stage(nc, m, w1)
                product_stage(nc, m)
                m.sem.renew()
                any_sums(nc, m, "_any1", m.b1)
                norm_stage(nc, m, "1", m.g1, m.bt1)
        m.sem.renew()
        m.weight = [sb(f"weight{k}", [P, NT], F32) for k in range(2)]
        m.slot = [sb(f"slot{k}", [P, NT], I32) for k in range(2)]
        m.expert = sb("tile_expert", [1, MT], I32)
        with nc.sbuf_tensor("logits", [P, NT, NE], F32) as m.logits:
            gate_stage(nc, m, x, gate_w, gate_b)
            route_stage(nc, m)
        with ExitStack() as big:
            def big_sb(name, shape, dt):
                return big.enter_context(nc.sbuf_tensor(name, shape, dt))

            m.ew1, m.ew2 = big_sb("ew1", [P, 2, NE, FF], F32), big_sb("ew2", [P, 4, NE, D], F32)
            m.eb1, m.eb2 = big_sb("eb1", [3, NE, FF], BF16), big_sb("eb2", [3, NE, D], BF16)
            m.ones_bf = big_sb("ones_bf", [3, P], BF16)
            m.sem.renew()
            scatter_stage(nc, m, ew1, eb1, ew2, eb2)
            expert_stage(nc, m)
        combine_stage(nc, m, gamma, beta, out)


def parameter_stage(nc, m, columns):
    s_in, s_eps = m.sem("parameters_in"), m.sem("eps_set")
    with nc.Block() as block:
        @block.sync
        def _(sp):
            with nc.allow_non_contiguous_dma(reason="six vectors of 256 words"):
                for t, v in columns:
                    sp.dma_start(t[:], v.rearrange("(c p) -> p c", p=P)).then_inc(s_in, 16)
            sp.wait_ge(s_in, 16 * len(columns))

        @block.vector
        def _(dve):
            dve.memset(m.eps[:], EPS).then_inc(s_eps, 1)


_INS = ["x", "src", "dst", "L0_gnn_W0", "L0_gnn_b0", "L0_gnn_g0", "L0_gnn_bt0", "L0_gnn_W1", "L0_gnn_b1", "L0_gnn_g1", "L0_gnn_bt1",
        "L0_ffn_gate_w", "L0_ffn_gate_b", "L0_ffn_w1", "L0_ffn_b1", "L0_ffn_w2", "L0_ffn_b2", "L0_ffn_gamma", "L0_ffn_beta"]


def kernel(**inputs):
    import concourse.bacc as bacc
    from concourse.bass_utils import run_bass_kernel_spmd

    nc = bacc.Bacc("TRN2", target_bir_lowering=False, num_devices=1)
    arrays, args = {}, []
    for name in _INS:
        a = np.ascontiguousarray(inputs[name])
        arrays["in_" + name] = a
        args.append(nc.dram_tensor("in_" + name, a.shape, mybir.dt.from_np(a.dtype), kind="ExternalInput").ap())
    args.append(nc.dram_tensor("out", (N, D), F32, kind="ExternalOutput").ap())
    program(nc, *args)
    return run_bass_kernel_spmd(nc, [arrays], core_ids=[0]).results[0]["out"]
```

```python
from contextlib import ExitStack, contextmanager

import numpy as np
import concourse.bass as bass
from concourse import mybir

F32 = mybir.dt.float32
F32R = mybir.dt.float32r
BF16 = mybir.dt.bfloat16
FP16 = mybir.dt.float16
I32 = mybir.dt.int32
U32 = mybir.dt.uint32
U8 = mybir.dt.uint8
ALU = mybir.AluOpType
ACT = mybir.ActivationFunctionType
AX = mybir.AxisListType

P = 128
N = 6250
D = 256
NT = -(-N // P)
NPAD = NT * P
LAST = N - (NT - 1) * P
E = 206250
ROWS = -(-E // (P * P))
CH = ROWS * P
EPAD = P * CH
CODE = 13
BD = 2
SLOTS = P
REAL = SLOTS - BD
WIN = 8
BW = WIN // BD
WSLOTS = 3 * P
WT = 7
NBLK = WT * P * BW
KEYS = NT * BD
UNITS = P // BD
GROUPS = UNITS // 8
NO_NODE = (1 << CODE) - 1
EPS = 1e-5
NE = 16
FF = 512
GOOD, BAD = 0, 1
MT = 114


class Names:
    pass


class Chain:

    def __init__(self, engine, sem):
        self.engine, self.sem, self.n = engine, sem, 0

    def __call__(self, ins):
        self.later(ins)
        self.engine.wait_ge(self.sem, self.n)

    def later(self, ins):
        self.n += 1
        ins.then_inc(self.sem, 1)


def edge_stage(nc, m, src, dst):
    with ExitStack() as ctx:
        def sb(name, shape, dt):
            return ctx.enter_context(nc.sbuf_tensor(name, shape, dt))

        def ps(name, shape):
            return ctx.enter_context(nc.psum_tensor(name, shape, F32))

        sem = m.sem

        iota_i = sb("iota_i", [P, P], I32)
        src_i, dst_i = sb("src_i", [P, CH], I32), sb("dst_i", [P, CH], I32)
        head_i, head = sb("head_i", [P, ROWS], I32), sb("head", [P, ROWS], F32)
        head_diag = sb("head_diag", [P, ROWS, P], F32)
        first_i, first = sb("first_i", [P, WT, BW], I32), sb("first", [P, WT, WIN // BD], F32)
        below = sb("below", [P, ROWS * P], BF16)
        rowf, rowi = sb("rowf", [P, WT], F32), sb("rowi", [P, WT], I32)
        row_i = sb("row_i", [P, WT, P], I32)
        cnt = sb("cnt", [P, WT], F32)
        win_start, win_start_i = sb("win_start", [P, WT], F32), sb("win_start_i", [P, WT], I32)
        win_i = sb("win_i", [P, WT, WSLOTS], I32)
        sub = sb("sub", [P, WT, BW], F32)
        start_i = sb("start_i", [P, WT, BW], I32)
        code = sb("code", [P, WT, BW, SLOTS], I32)
        slot_dst, hi, lo_i = (sb(n, [P, WT, BW, SLOTS], I32) for n in ("slot_dst", "hi", "lo_i"))
        dl, no_dst, key, lo = (sb(n, [P, 2, BW, SLOTS], F32) for n in ("dl", "no_dst", "key", "lo"))
        hit = sb("hit", [P, SLOTS], BF16)
        deg = sb("deg", [P, WT, WIN], F32)
        over = sb("over", [P, WT * WIN], BF16)
        sums, bad = sb("sums", [P, 2], F32), sb("bad", [P, 1], F32)
        head_ps = ps("head_ps", [P, 4, 512])
        pt = [ps(f"keys_ps{i}", [P, 512]) for i in range(2)]
        lt = [ps(f"los_ps{i}", [P, 512]) for i in range(2)]

        (s_pads, s_src_in, s_dst_in, s_code, s_codes, s_const, s_pool, s_dve, s_diag, s_heads, s_row, s_rows, s_win, s_start, s_lo_i, s_lo,
         s_keys, s_key_t, s_lo_t, s_ev, s_ev2, s_deg, s_degd, s_sums, s_total) = (sem(n) for n in (
             "pads_set", "src_in", "dst_in", "codes_packed", "codes_stored", "constants_ready", "pool_step", "dve_step",
             "head_diagonals_ready", "heads_ready", "row_index_ready", "rows_in", "window_starts_ready", "block_starts_ready",
             "los_ready", "los_widened", "keys_ready", "keys_transposed", "los_transposed", "keys_copied", "los_copied",
             "degrees_ready", "degrees_stored", "sums_ready", "total_ready"))
        s_window = [sem(f"window_in{w}") for w in range(WT)]
        s_slots = [sem(f"slots_in{w}") for w in range(WT)]
        full = E // CH
        heads = head_ps[:].rearrange("p a b -> p (a b)")[:, 0:ROWS * P]

        with nc.Block() as block:
            @block.sync
            def _(sp):
                sp.wait_ge(s_pads, 2)
                sp.dma_start(dst_i[0:full, :], dst[0:full * CH].rearrange("(p c) -> p c", p=full)).then_inc(s_dst_in, 16)
                sp.dma_start(dst_i[full:full + 1, 0:E - full * CH], dst[full * CH:E].rearrange("(a c) -> a c", a=1)).then_inc(s_dst_in, 16)
                sp.wait_ge(s_code, 1)
                sp.dma_start(m.codes.rearrange("(p c) -> p c", p=P), dst_i[:]).then_inc(s_codes, 16)
                sp.wait_ge(s_deg, 1)
                sp.dma_start(m.deg.rearrange("(w p d) -> p w d", p=P, d=WIN), deg[:]).then_inc(s_degd, 16)
                sp.wait_ge(s_degd, 16)

            @block.scalar
            def _(act):
                act.wait_ge(s_pads, 2)
                act.dma_start(src_i[0:full, :], src[0:full * CH].rearrange("(p c) -> p c", p=full)).then_inc(s_src_in, 16)
                act.dma_start(src_i[full:full + 1, 0:E - full * CH], src[full * CH:E].rearrange("(a c) -> a c", a=1)).then_inc(s_src_in, 16)
                for w in range(WT):
                    act.wait_ge(s_lo_i, w + 1)
                    if w >= 2:
                        act.wait_ge(s_lo_t, w - 1)
                    act.activation(lo[:, w % 2, :, :], lo_i[:, w, :, :], ACT.Copy).then_inc(s_lo, 1)
                    if w >= 1:
                        act.wait_ge(s_lo_t, w)
                        act.activation(block_columns(m.loT, w - 1), lt[(w - 1) % 2][:].rearrange("p (j b) -> p j b", j=BW), ACT.Copy).then_inc(s_ev2, 1)
                act.wait_ge(s_lo_t, WT)
                act.activation(block_columns(m.loT, WT - 1), lt[(WT - 1) % 2][:].rearrange("p (j b) -> p j b", j=BW), ACT.Copy).then_inc(s_ev2, 1)

            @block.gpsimd
            def _(pool):
                step = Chain(pool, s_pool)
                step(pool.memset(m.ident[:], 0.0))
                pool.affine_select(out=m.ident[:], in_=m.ident[:], compare_op=ALU.not_equal, fill=1.0, base=0,
                                   pattern=[[-1, P]], channel_multiplier=1).then_inc(s_const, 1)
                pool.memset(m.ones[:], 1.0).then_inc(s_const, 1)
                pool.iota(first_i[:], pattern=[[P * WIN, WT], [BD, BW]], base=0, channel_multiplier=WIN).then_inc(s_const, 1)
                step(pool.iota(iota_i[:], pattern=[[1, P]], base=0, channel_multiplier=0))
                pool.tensor_copy(m.iota16[:], iota_i[:]).then_inc(s_const, 1)
                loop = (1 << CODE) + 1
                for w in range(WT):
                    pool.iota(code[:, w, :, REAL:SLOTS], pattern=[[loop * BD, BW], [loop, BD]], base=loop * P * WIN * w,
                              channel_multiplier=loop * WIN).then_inc(s_const, 1)
                rows = m.codes.rearrange("(r c) -> r c", c=P)
                edges = m.codes.rearrange("(e o) -> e o", o=1)
                pool.wait_ge(s_codes, 16)
                pool.wait_ge(s_row, 1)
                for w in range(WT):
                    pool.indirect_dma_start(out=row_i[:, w, :], out_offset=None, in_=rows,
                                            in_offset=bass.IndirectOffsetOnAxis(ap=rowi[:, w:w + 1], axis=0)).then_inc(s_rows, 16)
                pool.wait_ge(s_win, 1)
                for w in range(WT):
                    pool.indirect_dma_start(out=win_i[:, w, :], out_offset=None, in_=edges,
                                            in_offset=bass.IndirectOffsetOnAxis(ap=win_start_i[:, w:w + 1], axis=0)).then_inc(s_window[w], 16)
                for w in range(WT):
                    pool.wait_ge(s_start, w + 1)
                    for j in range(BW):
                        pool.indirect_dma_start(out=code[:, w, j, 0:REAL], out_offset=None, in_=edges,
                                                in_offset=bass.IndirectOffsetOnAxis(ap=start_i[:, w, j:j + 1], axis=0)).then_inc(s_slots[w], 16)

            @block.vector
            def _(dve):
                step = Chain(dve, s_dve)
                dve.memset(dst_i[96:P, :], NO_NODE).then_inc(s_pads, 1)
                dve.memset(src_i[96:P, :], 0).then_inc(s_pads, 1)
                dve.wait_ge(s_const, 4 + WT)
                step.later(dve.tensor_copy(first[:], first_i[:]))
                step.later(dve.tensor_copy(m.iota4[:], m.iota16[:].unsqueeze(2).to_broadcast([P, P, 4])))
                dve.wait_ge(s_dst_in, 32)
                step(dve.tensor_copy(head[:], dst_i[:].rearrange("p (r c) -> p r c", c=P)[:, :, 0]))
                dve.tensor_tensor(head_diag[:], m.ident[:].unsqueeze(1).to_broadcast([P, ROWS, P]),
                                  head[:].unsqueeze(2).to_broadcast([P, ROWS, P]), ALU.mult).then_inc(s_diag, 1)
                dve.wait_ge(s_src_in, 32)
                dve.scalar_tensor_tensor(out=dst_i[:], in0=dst_i[:], scalar=CODE, in1=src_i[:], op0=ALU.logical_shift_left,
                                         op1=ALU.bitwise_or).then_inc(s_code, 1)
                dve.wait_ge(s_heads, 1)
                for w in range(WT):
                    step(dve.tensor_scalar(below[:], heads, first[:, w, 0:1], 0.0, ALU.is_lt, ALU.add, accum_out=rowf[:, w:w + 1]))
                step(dve.tensor_scalar(rowf[:], rowf[:], -1.0, 0.0, ALU.add, ALU.max))
                dve.tensor_copy(rowi[:], rowf[:]).then_inc(s_row, 1)
                dve.wait_ge(s_rows, 16 * WT)
                step(dve.tensor_scalar(row_i[:], row_i[:], CODE, None, ALU.arith_shift_right))
                for w in range(WT):
                    step(dve.tensor_scalar(below[:, 0:P], row_i[:, w, :], first[:, w, 0:1], 0.0, ALU.is_lt, ALU.add,
                                           accum_out=cnt[:, w:w + 1]))
                step(dve.scalar_tensor_tensor(out=win_start[:], in0=rowf[:], scalar=float(P), in1=cnt[:], op0=ALU.mult, op1=ALU.add))
                dve.tensor_copy(win_start_i[:], win_start[:]).then_inc(s_win, 1)
                step(dve.memset(sub[:], 0.0))
                for w in range(WT):
                    dve.wait_ge(s_window[w], 16)
                    step(dve.tensor_scalar(win_i[:, w, :], win_i[:, w, :], CODE, None, ALU.arith_shift_right))
                    for j in range(1, BW):
                        step(dve.tensor_scalar(below[:, 0:WSLOTS], win_i[:, w, :], first[:, w, j:j + 1], 0.0, ALU.is_lt, ALU.add,
                                               accum_out=sub[:, w, j:j + 1]))
                    step(dve.tensor_scalar(sub[:, w, :], sub[:, w, :], win_start[:, w:w + 1], None, ALU.add))
                    dve.tensor_copy(start_i[:, w, :], sub[:, w, :]).then_inc(s_start, 1)

                def copy_keys(w):
                    dve.wait_ge(s_key_t, w + 1)
                    dve.tensor_scalar(block_columns(m.keyT, w), pt[w % 2][:].rearrange("p (j b) -> p j b", j=BW), 500.0, None,
                                      ALU.min).then_inc(s_ev, 1)

                for w in range(WT):
                    q = w % 2
                    dve.wait_ge(s_slots[w], 16 * BW)
                    dve.tensor_scalar(lo_i[:, w, :, :], code[:, w, :, :], P - 1, None, ALU.bitwise_and).then_inc(s_lo_i, 1)
                    step.later(dve.tensor_scalar(hi[:, w, :, :], code[:, w, :, :], 7, (1 << CODE - 7) - 1, ALU.arith_shift_right, ALU.bitwise_and))
                    step(dve.tensor_scalar(slot_dst[:, w, :, :], code[:, w, :, :], CODE, None, ALU.arith_shift_right))
                    step(dve.tensor_tensor(dl[:, q, :, :], slot_dst[:, w, :, :], first[:, w, :].unsqueeze(2).to_broadcast([P, BW, SLOTS]), ALU.subtract))
                    step.later(dve.tensor_scalar(no_dst[:, q, :, :], dl[:, q, :, :], 1.0, 128.0, ALU.is_gt, ALU.mult))
                    if w >= 2:
                        dve.wait_ge(s_key_t, w - 1)
                    step(dve.scalar_tensor_tensor(out=key[:, q, :, :], in0=hi[:, w, :, :], scalar=float(BD), in1=dl[:, q, :, :],
                                                  op0=ALU.mult, op1=ALU.add))
                    dve.tensor_tensor(key[:, q, :, :], key[:, q, :, :], no_dst[:, q, :, :], ALU.add).then_inc(s_keys, 1)
                    for j in range(BW):
                        for d in range(BD):
                            step(dve.tensor_scalar(hit[:], dl[:, q, j, :], float(d), 0.0, ALU.is_equal, ALU.add,
                                                   accum_out=deg[:, w, j * BD + d:j * BD + d + 1]))
                    if w >= 1:
                        copy_keys(w - 1)
                dve.sem_inc(s_deg, 1)
                step(dve.reduce_sum(sums[:, 0:1], deg[:].rearrange("p w d -> p (w d)"), AX.X))
                step(dve.tensor_scalar(over[:], deg[:].rearrange("p w d -> p (w d)"), 255.0, 0.0, ALU.is_gt, ALU.add,
                                       accum_out=sums[:, 1:2]))
                dve.sem_inc(s_sums, 1)
                copy_keys(WT - 1)
                dve.wait_ge(s_total, 1)
                step(dve.tensor_scalar(bad[:], heads[:, 0:1], float(E + NBLK * BD), None, ALU.not_equal))
                step(dve.tensor_tensor(bad[:], bad[:], heads[:, 1:2], ALU.add))
                step(dve.tensor_scalar(m.flags[:, BAD:BAD + 1], bad[:], 0.0, None, ALU.is_gt))
                step(dve.tensor_scalar(m.flags[:, GOOD:GOOD + 1], bad[:], 0.0, None, ALU.is_equal))

            @block.tensor
            def _(pe):
                pe.wait_ge(s_const, 4 + WT)
                pe.wait_ge(s_diag, 1)
                diag = head_diag[:].rearrange("p r c -> p (r c)")
                for a in range(0, ROWS * P, 512):
                    end = min(a + 512, ROWS * P)
                    last = pe.matmul(heads[:, a:end], m.ones[:], diag[:, a:end], start=True, stop=True)
                last.then_inc(s_heads, 1)
                for w in range(WT):
                    pe.wait_ge(s_lo, w + 1)
                    if w >= 2:
                        pe.wait_ge(s_ev2, w - 1)
                    for j in range(BW):
                        last = pe.transpose(lt[w % 2][:, j * P:(j + 1) * P], lo[:, w % 2, j, :], m.ident[:])
                    last.then_inc(s_lo_t, 1)
                    pe.wait_ge(s_keys, w + 1)
                    if w >= 2:
                        pe.wait_ge(s_ev, w - 1)
                    for j in range(BW):
                        last = pe.transpose(pt[w % 2][:, j * P:(j + 1) * P], key[:, w % 2, j, :], m.ident[:])
                    last.then_inc(s_key_t, 1)
                pe.wait_ge(s_sums, 1)
                pe.matmul(heads[:, 0:2], m.ones[:], sums[:], start=True, stop=True).then_inc(s_total, 1)


def block_columns(t, w):
    return t[:, w * P * BW:(w + 1) * P * BW].rearrange("p (b j) -> p j b", j=BW)


class Semaphores:

    def __init__(self, nc):
        self.nc, self.live = nc, []

    def __call__(self, name):
        self.live.append(self.nc.alloc_semaphore(f"{name}_{len(self.live)}"))
        return self.live[-1]

    def renew(self):
        self.nc.clear_and_free_semaphores(self.live)
        self.nc.all_engine_barrier()
        self.live = []


def wait(engine, sem, value):
    if not isinstance(value, int) or value > 0:
        engine.wait_ge(sem, value)


def for_tiles(engine, body, total, unroll, first=None):
    first = unroll if first is None else first
    rounds = (total - first) // unroll
    for t in range(first):
        body(t, t % unroll)
    if rounds:
        with engine.Fori(0, rounds) as i:
            for k in range(unroll):
                body(first + k + i * unroll, (first + k) % unroll)
    for t in range(first + rounds * unroll, total):
        body(t, t % unroll)


def dis_stage(nc, m):
    with ExitStack() as ctx:
        deg = ctx.enter_context(nc.sbuf_tensor("deg_rows", [NT, P], F32))
        root = ctx.enter_context(nc.sbuf_tensor("deg_root", [NT, P], F32))
        pt = ctx.enter_context(nc.psum_tensor("dis_ps", [P, NT], F32))
        s_in, s_root, s_inv, s_t, s_done = (m.sem(n) for n in
                                            ("deg_in", "root_ready", "dis_ready", "dis_transposed", "dis_done"))
        with nc.Block() as block:
            @block.sync
            def _(sp):
                sp.dma_start(deg[:], m.deg[0:NPAD].rearrange("(t p) -> t p", p=P)).then_inc(s_in, 16)

            @block.scalar
            def _(act):
                act.wait_ge(s_in, 16)
                act.activation(root[:], deg[:], ACT.Sqrt).then_inc(s_root, 1)

            @block.vector
            def _(dve):
                dve.wait_ge(s_root, 1)
                dve.reciprocal(deg[:], root[:]).then_inc(s_inv, 1)
                dve.wait_ge(s_t, 1)
                dve.tensor_copy(m.dis[:], pt[:]).then_inc(s_done, 1)

            @block.tensor
            def _(pe):
                pe.wait_ge(s_inv, 1)
                pe.transpose(pt[:], deg[:], m.ident[0:NT, 0:NT]).then_inc(s_t, 1)


def project_pe(pe, t, r, m, s, w):
    pe.wait_ge(s.lhs, t + 1)
    wait(pe, s.hf, t - 1)
    for k in range(2):
        last = pe.matmul(s.hp_ps[r % 2][:, 0:D], s.lhs_t[r % 2][:, k, :], w[:, k, :], start=(k == 0), stop=(k == 1))
    last.then_inc(s.h, 1)


def project_scale(act, t, r, m, s):
    act.wait_ge(s.h, t + 1)
    wait(act, s.split, t - 1)
    act.activation(s.hf_t[r % 2][:], s.hp_ps[r % 2][:, 0:D], ACT.Copy, scale=m.dis[:, bass.ds(t, 1)]).then_inc(s.hf, 1)


def project_split(dve, t, r, m, s):
    dve.wait_ge(s.hf, t + 1)
    hi = m.h[:, bass.ds(t, 1), 0, :]
    lo = m.h[:, bass.ds(t, 1), 1, :]
    hf = s.hf_t[r % 2][:].unsqueeze(1)
    dve.tensor_copy(hi, hf).then_inc(s.hi, 1)
    dve.wait_ge(s.hi, t + 1)
    dve.tensor_tensor(lo, hf, hi.bitcast(F32), ALU.subtract).then_inc(s.split, 1)


def project_buffers(ctx, nc, m, tag):
    def sem(name):
        return m.sem(f"{name}{tag}")

    s = Names()
    s.lhs_t = [ctx.enter_context(nc.sbuf_tensor(f"lhs{tag}{i}", [P, 2, P], F32)) for i in range(2)]
    s.hf_t = [ctx.enter_context(nc.sbuf_tensor(f"hf{tag}{i}", [P, D], F32)) for i in range(2)]
    s.hp_ps = [ctx.enter_context(nc.psum_tensor(f"h_ps{tag}{i}", [P, 512], F32)) for i in range(2)]
    s.lhs = sem("lhs_ready")
    s.h = sem("h_ready")
    s.hf = sem("hf_ready")
    s.hi = sem("hi_ready")
    s.split = sem("h_split")
    return s


def input_stage(nc, m, x, w0):
    G = 8
    groups = (NT - 1) // G
    with ExitStack() as ctx:
        sem = m.sem

        s = project_buffers(ctx, nc, m, "0")
        xg = [ctx.enter_context(nc.sbuf_tensor(f"xg{i}", [P, G, D], F32)) for i in range(2)]
        w = ctx.enter_context(nc.sbuf_tensor("w0_sb", [P, 2, D], F32))
        st = ctx.enter_context(nc.sbuf_tensor("ln0_stats", [P, G, 6], F32))
        mv = ctx.enter_context(nc.sbuf_tensor("ln0_mv", [P, G, 2], F32))
        root = ctx.enter_context(nc.sbuf_tensor("ln0_root", [P, G], F32))
        rstd = ctx.enter_context(nc.sbuf_tensor("ln0_rstd", [P, G], F32))
        pt = [ctx.enter_context(nc.psum_tensor(f"xt_ps{i}", [P, 512], F32)) for i in range(2)]
        s_x = [sem(f"x_in{i}") for i in range(2)]
        s_w, s_st, s_mv, s_root, s_rstd, s_xn, s_tr, s_zero, s_seen = (sem(n) for n in (
            "w0_in", "ln0_stats_ready", "ln0_mv_ready", "ln0_root_ready", "ln0_rstd_ready", "xn_ready", "xt_ready", "x_tail_zeroed", "ln0_stats_seen"))

        with nc.Block() as block:
            @block.sync
            def _(sp):
                sp.dma_start(w[:], w0.rearrange("(k p) n -> p k n", p=P)).then_inc(s_w, 16)

                def load(g, r):
                    wait(sp, s_tr, (g - 1) * G)
                    sp.dma_start(xg[r][:], x[bass.ds(g * (G * P), G * P), :].rearrange("(k p) d -> p k d", p=P)).then_inc(s_x[r], 16)

                for_tiles(sp, load, groups, 2)
                sp.wait_ge(s_zero, 1)
                sp.dma_start(xg[groups % 2][0:LAST, 0, :], x[(NT - 1) * P:N, :]).then_inc(s_x[groups % 2], 16)

            @block.vector
            def _(dve):
                def normalize(g, q, n):
                    dve.wait_ge(s_x[q], (g - q) * 8 + 16)
                    for k in range(n):
                        dve.bn_stats(st[:, k, :], xg[q][:, k, :]).then_inc(s_st, 1)
                    dve.wait_ge(s_st, g * G + n)
                    dve.sem_inc(s_seen, 1)
                    for k in range(n):
                        last = dve.bn_aggr(mv[:, k, :], st[:, k, :])
                    last.then_inc(s_mv, 1)
                    dve.wait_ge(s_root, g + 1)
                    dve.reciprocal(rstd[:, 0:n], root[:, 0:n]).then_inc(s_rstd, 1)
                    dve.wait_ge(s_rstd, g + 1)
                    for k in range(n):
                        dve.tensor_scalar(xg[q][:, k, :], xg[q][:, k, :], mv[:, k, 0:1], rstd[:, k:k + 1],
                                          ALU.subtract, ALU.mult).then_inc(s_xn, 1)

                def group(g, r):
                    normalize(g, r, G)
                    if not isinstance(g, int) or g > 0:
                        for k in range(G):
                            project_split(dve, (g - 1) * G + k, k, m, s)

                for_tiles(dve, group, groups, 2)
                dve.wait_ge(s_tr, (groups - 1) * G)
                dve.memset(xg[groups % 2][96:P, 0, :], 0.0).then_inc(s_zero, 1)
                normalize(groups, groups % 2, 1)
                for k in range(G + 1):
                    project_split(dve, (groups - 1) * G + k, k, m, s)

            @block.tensor
            def _(pe):
                pe.wait_ge(s_w, 16)

                def group(g, r, n=G):
                    for k in range(n):
                        t = g * G + k
                        pe.wait_ge(s_xn, t + 1)
                        wait(pe, s.lhs, t - 1)
                        for c in range(2):
                            last = pe.transpose(pt[k % 2][:, c * P:(c + 1) * P], xg[r][:, k, c * P:(c + 1) * P], m.ident[:])
                        last.then_inc(s_tr, 1)
                        if not isinstance(t, int) or t > 0:
                            project_pe(pe, t - 1, k + 1, m, s, w)

                for_tiles(pe, group, groups, 2)
                group(groups, groups % 2, 1)
                project_pe(pe, NT - 1, NT - 1, m, s, w)

            @block.scalar
            def _(act):
                def root_of(g, n):
                    act.wait_ge(s_mv, g + 1)
                    act.activation(root[:, 0:n], mv[:, 0:n, 1], ACT.Sqrt, bias=m.eps[:, 0:1]).then_inc(s_root, 1)

                def tile(t, r):
                    act.wait_ge(s_tr, t + 1)
                    wait(act, s.h, t - 1)
                    act.activation(s.lhs_t[r % 2][:].rearrange("p k n -> p (k n)"), pt[r % 2][:, 0:D], ACT.Copy).then_inc(s.lhs, 1)
                    project_scale(act, t, r, m, s)

                def group(g, r):
                    root_of(g, G)
                    if not isinstance(g, int) or g > 0:
                        for k in range(G):
                            tile((g - 1) * G + k, k)

                for_tiles(act, group, groups, 2)
                root_of(groups, 1)
                for k in range(G + 1):
                    tile((groups - 1) * G + k, k)


def tail_buffers(ctx, nc, m, tag, bias):
    def sem(name):
        return m.sem(f"{name}{tag}")

    s = Names()
    s.sum_ps = [ctx.enter_context(nc.psum_tensor(f"sum_ps{tag}{i}", [P, 512], F32)) for i in range(2)]
    s.zt_ps = [ctx.enter_context(nc.psum_tensor(f"zt_ps{tag}{i}", [P, 512], F32)) for i in range(2)]
    s.low_t = [ctx.enter_context(nc.sbuf_tensor(f"low{tag}{i}", [P, D], F32)) for i in range(2)]
    s.z_t = [ctx.enter_context(nc.sbuf_tensor(f"z{tag}{i}", [P, D], F32)) for i in range(2)]
    s.zt_t = [ctx.enter_context(nc.sbuf_tensor(f"zt{tag}{i}", [P, 2, P], F32)) for i in range(2)]
    s.bias = bias
    s.sum = sem("sum_ready")
    s.low = sem("low_scaled")
    s.z = sem("z_ready")
    s.tr = sem("z_transposed")
    s.relu = sem("z_relu")
    s.stats = sem("z_stats_ready")
    s.store = [sem(f"z_stored{i}_") for i in range(2)]
    return s


def tail_low(act, t, r, m, s):
    act.wait_ge(s.sum, t + 1)
    wait(act, s.z, t - 1)
    act.activation(s.low_t[r][:], s.sum_ps[r][:, D:2 * D], ACT.Copy, scale=m.dis[:, bass.ds(t, 1)]).then_inc(s.low, 1)


def tail_add(dve, t, r, m, s):
    dve.wait_ge(s.low, t + 1)
    wait(dve, s.tr, t - 1)
    dve.scalar_tensor_tensor(out=s.z_t[r][:], in0=s.sum_ps[r][:, 0:D], scalar=m.dis[:, bass.ds(t, 1)], in1=s.low_t[r][:],
                             op0=ALU.mult, op1=ALU.add).then_inc(s.z, 1)


def tail_transpose(pe, t, r, m, s):
    pe.wait_ge(s.z, t + 1)
    wait(pe, s.relu, 2 * (t - 1))
    for c in range(2):
        last = pe.transpose(s.zt_ps[r][:, c * P:(c + 1) * P], s.z_t[r][:, c * P:(c + 1) * P], m.ident[:])
    last.then_inc(s.tr, 1)


def tail_relu(act, t, r, u, m, s):
    act.wait_ge(s.tr, t + 1)
    wait(act, s.stats, 2 * (t - 1))
    wait(act, s.store[r], 16 * u)
    for c in range(2):
        act.activation(s.zt_t[r][:, c, :], s.zt_ps[r][:, c * P:(c + 1) * P], ACT.Relu, bias=s.bias[:, c:c + 1]).then_inc(s.relu, 1)


def tail_stats(dve, t, r, m, s, n=P):
    dve.wait_ge(s.relu, 2 * (t + 1))
    for c in range(2):
        out = m.stats[:, c, t * 6:(t + 1) * 6] if isinstance(t, int) else m.stats[:, c, bass.ds(t * 6, 6)]
        dve.bn_stats(out, s.zt_t[r][:, c, 0:n]).then_inc(s.stats, 1)


def tile_at(engine, store, t, width, dt):
    size = P * width * (1 if dt == U8 else 4)
    at = t * size if isinstance(t, int) else engine.snap(engine.to_reg(t * size), min_val=0, max_val=store.shape[0] - size)
    flat = store[bass.ds(at, size)]
    return (flat if dt == U8 else flat.bitcast(dt)).rearrange("(p n) -> p n", p=P)


def before_wait(engine, value):
    return value if isinstance(value, int) else engine.snap(engine.to_reg(value), min_val=0, max_val=1 << 20)


def tail_store(sp, t, r, m, s):
    at = tile_at(sp, m.zT, t, D, F32)
    sp.wait_ge(s.relu, 2 * (t + 1))
    sp.dma_start(at, s.zt_t[r][:].rearrange("p c n -> p (c n)")).then_inc(s.store[r], 16)


def tail_stored(sp, s):
    for r in range(2):
        sp.wait_ge(s.store[r], 16 * ((NT + 1 - r) // 2))


def build_stage(nc, m):
    RING = 2
    AHEAD = 4
    ROUND = MT // 6
    BY_VECTOR = (2, 4, 6)
    with ExitStack() as ctx:
        sem = m.sem

        s = tail_buffers(ctx, nc, m, "_b", m.b0)
        key1 = [ctx.enter_context(nc.sbuf_tensor(f"key_onehot{i}", [P, 2, KEYS, 4], BF16)) for i in range(AHEAD)]
        lo1 = [ctx.enter_context(nc.sbuf_tensor(f"lo_onehot{i}", [P, 2, P, 4], BF16)) for i in range(AHEAD)]
        counts = [ctx.enter_context(nc.sbuf_tensor(f"counts{i}", [P, NT, P], F32R)) for i in range(2)]
        bytes_ = [ctx.enter_context(nc.sbuf_tensor(f"count_bytes{i}", [P, NT, P], U8)) for i in range(2)]
        zero = ctx.enter_context(nc.sbuf_tensor("zero_row", [P, D], F32))
        group_ps = [ctx.enter_context(nc.psum_tensor(f"group_ps{i}", [P, 8, P], F32)) for i in range(RING)]
        s_one, s_group, s_ev, s_byte, s_byte_v = (sem(n) for n in (
            "onehots_ready", "group_ready", "group_copied", "bytes_by_scalar", "bytes_by_vector"))
        s_bst = [sem(f"bytes_stored{i}") for i in range(2)]
        s_zero, s_zeroed = sem("zero_set"), sem("slots_zeroed")
        by_scalar = GROUPS - len(BY_VECTOR)

        def steps(engine, body):
            for t in range(4):
                body(t, t % 2, t // 2, True, t >= 1, t >= 2)
            with engine.Fori(0, (NT - 4) // 2) as i:
                for k in range(2):
                    body(i * 2 + (4 + k), k, i + 2, True, True, True)
            body(NT - 1, (NT - 1) % 2, (NT - 1) // 2, True, True, True)
            body(NT, NT % 2, NT // 2, False, True, True)
            body(NT + 1, (NT + 1) % 2, (NT + 1) // 2, False, False, True)

        def eighth(q):
            return q * 6, (q + 1) * 6 if q < GROUPS - 1 else NT

        def one_hots(dve, out, width, column):
            dve.tensor_tensor(out[:], m.iota4[:, 0:width, :].unsqueeze(1).to_broadcast([P, 2, width, 4]),
                              column.rearrange("p (g c) -> p g c", g=2).unsqueeze(2).to_broadcast([P, 2, width, 4]),
                              ALU.is_equal).then_inc(s_one, 1)

        with nc.Block() as block:
            @block.vector
            def _(dve):
                with when(dve, m, GOOD):
                    def step(t, r, u, build, prod, tail):
                        for q in range(GROUPS):
                            if build:
                                wait(dve, s_group, t * GROUPS + (q - AHEAD + 1))
                                blocks = slice(t * UNITS + q * 8, t * UNITS + q * 8 + 8) if isinstance(t, int) else bass.ds(t * UNITS + q * 8, 8)
                                one_hots(dve, key1[q % AHEAD], KEYS, m.keyT[:, blocks])
                                one_hots(dve, lo1[q % AHEAD], P, m.loT[:, blocks])
                            if prod and q in BY_VECTOR:
                                if q == BY_VECTOR[0]:
                                    dve.wait_ge(s_ev, t * GROUPS)
                                    wait(dve, s_bst[1 - r], 16 * (u + (r - 1)))
                                first, end = eighth(q)
                                dve.tensor_copy(bytes_[1 - r][:, first:end, :], counts[1 - r][:, first:end, :].bitcast(F32)).then_inc(s_byte_v, 1)
                            if tail and q == 1:
                                tail_add(dve, t - 2, r, m, s)
                            if tail and q == 5:
                                tail_stats(dve, t - 2, r, m, s, LAST if isinstance(t, int) and t - 2 == NT - 1 else P)

                    steps(dve, step)

            @block.tensor
            def _(pe):
                with when(pe, m, GOOD):
                    def step(t, r, u, build, prod, tail):
                        for q in range(GROUPS):
                            if build:
                                pe.wait_ge(s_one, t * (2 * GROUPS) + 2 * (q + 1))
                                wait(pe, s_ev, t * GROUPS + (q - RING + 1))
                                for g in range(2):
                                    for c in range(4):
                                        last = pe.matmul(group_ps[q % RING][:, 4 * g + c, 0:KEYS], lo1[q % AHEAD][:, g, :, c],
                                                         key1[q % AHEAD][:, g, :, c], start=True, stop=True)
                                last.then_inc(s_group, 1)
                            if prod:
                                first, end = eighth(q)
                                if q == 0:
                                    pe.wait_ge(s_ev, t * GROUPS)
                                    wait(pe, s.z, t - 2)
                                for h in range(first, end):
                                    last = pe.matmul(s.sum_ps[1 - r][:], counts[1 - r][:, h, :], m.h[:, h, :, :].rearrange("p a d -> p (a d)"),
                                                     start=(h == 0), stop=(h == NT - 1))
                                if end == NT:
                                    last.then_inc(s.sum, 1)
                            if tail and q == 3:
                                tail_transpose(pe, t - 2, r, m, s)

                    steps(pe, step)

            @block.scalar
            def _(act):
                with when(act, m, GOOD):
                    def step(t, r, u, build, prod, tail):
                        for q in range(GROUPS):
                            if tail and q == 0:
                                tail_low(act, t - 2, r, m, s)
                            if build:
                                if q == 0:
                                    wait(act, s.sum, t - 1)
                                    wait(act, s_byte, (t - 1) * by_scalar)
                                    wait(act, s_byte_v, (t - 1) * len(BY_VECTOR))
                                act.wait_ge(s_group, t * GROUPS + (q + 1))
                                act.activation(counts[r][:, :, q * 16:(q + 1) * 16].rearrange("p h (v d) -> p h v d", d=BD),
                                               group_ps[q % RING][:, :, 0:KEYS].rearrange("p v (h d) -> p h v d", d=BD),
                                               ACT.Copy).then_inc(s_ev, 1)
                            if prod and q not in BY_VECTOR:
                                if q == 0:
                                    act.wait_ge(s_ev, t * GROUPS)
                                    wait(act, s_bst[1 - r], 16 * (u + (r - 1)))
                                first, end = eighth(q)
                                act.activation(bytes_[1 - r][:, first:end, :], counts[1 - r][:, first:end, :].bitcast(F32),
                                               ACT.Copy).then_inc(s_byte, 1)
                            if tail and q == 4:
                                tail_relu(act, t - 2, r, u - 1, m, s)

                    steps(act, step)

            @block.sync
            def _(sp):
                with when(sp, m, GOOD):
                    def step(t, r, u, build, prod, tail):
                        if tail:
                            tail_store(sp, t - 2, r, m, s)
                        if prod:
                            at, done = tile_at(sp, m.counts, t - 1, NPAD, U8), before_wait(sp, t * by_scalar)
                            sp.wait_ge(s_byte_v, t * len(BY_VECTOR))
                            sp.wait_ge(s_byte, done)
                            sp.dma_start(at, bytes_[1 - r][:].rearrange("p h n -> p (h n)")).then_inc(s_bst[1 - r], 16)

                    steps(sp, step)
                    tail_stored(sp, s)
                    for r in range(2):
                        sp.wait_ge(s_bst[r], 16 * ((NT + 1 - r) // 2))

            @block.gpsimd
            def _(pool):
                pool.memset(zero[:], 0.0).then_inc(s_zero, 1)
                pool.wait_ge(s_zero, 1)
                for g in range(MT // ROUND):
                    pool.dma_start(m.rows[g * ROUND * P:(g + 1) * ROUND * P, :].rearrange("(p n) d -> p n d", p=P),
                                   zero[:].unsqueeze(1).to_broadcast([P, ROUND, D])).then_inc(s_zeroed, 16)
                pool.wait_ge(s_zeroed, 16 * (MT // ROUND))


@contextmanager
def when(engine, m, flag):
    value = engine.value_load(m.flags[0:1, flag:flag + 1], min_val=0, max_val=1)
    with engine.If(value):
        yield


def any_degrees(nc, m):
    RING = 4
    with ExitStack() as ctx:
        def sb(name, shape, dt):
            return ctx.enter_context(nc.sbuf_tensor(name, shape, dt))

        code, part_i = sb("any_codes", [P, CH], I32), sb("any_dst_part", [P, CH], I32)
        lo, hi = sb("any_lo", [P, CH], F32), sb("any_hi", [P, CH], F32)
        lo1 = [sb(f"any_lo_onehot{i}", [P, P], BF16) for i in range(RING)]
        hi1 = [sb(f"any_hi_onehot{i}", [P, NT], BF16) for i in range(RING)]
        root = sb("any_root", [P, NT], F32)
        total = ctx.enter_context(nc.psum_tensor("any_degree_ps", [P, NT], F32))
        s_in, s_step, s_one, s_used, s_root, s_dis = (m.sem(n) for n in (
            "any_dst_in", "any_degree_step", "any_onehots_ready", "any_onehots_used", "any_root_ready", "any_dis_ready"))
        with nc.Block() as block:
            @block.sync
            def _(sp):
                with when(sp, m, BAD):
                    sp.dma_start(code[:], m.codes.rearrange("(p c) -> p c", p=P)).then_inc(s_in, 16)

            @block.vector
            def _(dve):
                with when(dve, m, BAD):
                    step = Chain(dve, s_step)
                    dve.wait_ge(s_in, 16)
                    step(dve.tensor_scalar(part_i[:], code[:], CODE, P - 1, ALU.arith_shift_right, ALU.bitwise_and))
                    step(dve.tensor_copy(lo[:], part_i[:]))
                    step(dve.tensor_scalar(part_i[:], code[:], CODE + 7, None, ALU.arith_shift_right))
                    step(dve.tensor_copy(hi[:], part_i[:]))

                    def onehots(t, r, u):
                        wait(dve, s_used, t - RING + 1)
                        dve.tensor_scalar(lo1[r][:], m.iota16[:, 0:P], lo[:, at_tile(t, 0)], None, ALU.is_equal)
                        dve.tensor_scalar(hi1[r][:], m.iota16[:, 0:NT], hi[:, at_tile(t, 0)], None, ALU.is_equal).then_inc(s_one, 1)

                    for_slots(dve, onehots, CH, RING)
                    dve.wait_ge(s_root, 1)
                    dve.reciprocal(m.dis[:], root[:]).then_inc(s_dis, 1)

            @block.tensor
            def _(pe):
                with when(pe, m, BAD):
                    def count(t, r, u):
                        pe.wait_ge(s_one, t + 1)
                        pe.matmul(total[:], lo1[r][:], hi1[r][:], start=isinstance(t, int) and t == 0,
                                  stop=isinstance(t, int) and t == CH - 1).then_inc(s_used, 1)

                    for_slots(pe, count, CH, RING)

            @block.scalar
            def _(act):
                with when(act, m, BAD):
                    act.wait_ge(s_used, CH)
                    act.activation(root[:], total[:], ACT.Sqrt, bias=m.ones[:, 0:1]).then_inc(s_root, 1)


def any_sums(nc, m, tag, bias):
    RING = 4
    with ExitStack() as ctx:
        def sb(name, shape, n, dt=F32):
            return [ctx.enter_context(nc.sbuf_tensor(f"{name}{tag}{i}", shape, dt)) for i in range(n)]

        def sem(name):
            return m.sem(f"{name}{tag}")

        s = tail_buffers(ctx, nc, m, tag, bias)
        edges = sb("any_edges", [P, CH], 2, I32)
        row = sb("any_h_row", [P, D], 2)
        src_now, dst_now, dst_f = sb("any_src_now", [P, 1], RING, I32), sb("any_dst_now", [P, 1], RING, I32), sb("any_dst_f", [P, 1], RING)
        diag, equal = sb("any_diag", [P, P], 2), sb("any_equal", [P, P], 2)
        h_rows, sums, new = sb("any_h_rows", [P, D], RING), sb("any_sums", [P, D], RING), sb("any_new", [P, D], RING)
        final = sb("any_final", [P, D], 2)
        dst_ps = [ctx.enter_context(nc.psum_tensor(f"any_dst_ps{tag}{i}", [P, 512], F32)) for i in range(2)]
        part_ps = s.sum_ps
        s_edges, s_split, s_row, s_now, s_diag, s_dst, s_equal, s_part, s_new, s_seen, s_seen2 = (sem(n) for n in (
            "any_edges_in", "any_edges_split", "any_row_ready", "any_now_ready", "any_diag_ready", "any_dst_rows_ready", "any_equal_ready",
            "any_part_ready", "any_new_ready", "any_rows_may_load", "any_sums_may_load"))
        s_stored = [sem(f"any_row_stored{i}_") for i in range(2)]
        s_h, s_old, s_sent = ([sem(f"{n}{i}_") for i in range(RING)] for n in ("any_h_rows_in", "any_sums_in", "any_sums_stored"))
        s_final = [sem(f"any_final_in{i}_") for i in range(2)]
        h_at, sum_at = m.any_h.rearrange("(n d) -> n d", d=4 * D).bitcast(F32), m.any_sum.rearrange("(n d) -> n d", d=4 * D).bitcast(F32)

        with nc.Block() as block:
            @block.sync
            def _(sp):
                with when(sp, m, BAD):
                    sp.dma_start(edges[0][:], m.codes.rearrange("(p c) -> p c", p=P)).then_inc(s_edges, 16)

                    def store(t, r, u):
                        h_to, sum_to = tile_at(sp, m.any_h, t, D, F32), tile_at(sp, m.any_sum, t, D, F32)
                        sp.wait_ge(s_row, t + 1)
                        sp.dma_start(h_to, row[r][:]).then_inc(s_stored[r], 16)
                        sp.dma_start(sum_to, row[r][:]).then_inc(s_stored[r], 16)

                    for_slots(sp, store, NT + 1, 2)

                    def load(t, r, u):
                        at = tile_at(sp, m.any_sum, t, D, F32)
                        wait(sp, s.z, t - 1)
                        sp.dma_start(final[r][:], at).then_inc(s_final[r], 16)
                        if not isinstance(t, int) or t >= 1:
                            tail_store(sp, t - 1, 1 - r, m, s)

                    for r in range(RING):
                        sp.wait_ge(s_sent[r], 16 * ((CH + RING - 1 - r) // RING))
                    for_slots(sp, load, NT, 2)
                    tail_store(sp, NT - 1, (NT - 1) % 2, m, s)
                    tail_stored(sp, s)

            @block.vector
            def _(dve):
                with when(dve, m, BAD):
                    def whole(t, r, u):
                        wait(dve, s_stored[r], 32 * u)
                        dve.tensor_tensor(row[r][:].unsqueeze(1), m.h[:, at_tile(t, 0), 0, :].bitcast(F32),
                                          m.h[:, at_tile(t, 0), 1, :].bitcast(F32), ALU.add).then_inc(s_row, 1)

                    for_slots(dve, whole, NT, 2)
                    dve.wait_ge(s_stored[NT % 2], 32 * (NT // 2))
                    dve.memset(row[NT % 2][:], 0.0).then_inc(s_row, 1)
                    dve.wait_ge(s_edges, 16)
                    dve.tensor_scalar(edges[1][:], edges[0][:], CODE, None, ALU.arith_shift_right).then_inc(s_split, 1)
                    dve.wait_ge(s_split, 1)
                    dve.tensor_scalar(edges[0][:], edges[0][:], (1 << CODE) - 1, None, ALU.bitwise_and).then_inc(s_split, 1)
                    dve.wait_ge(s_split, 2)

                    def now(t, r, u):
                        wait(dve, s_sent[r], 16 * u)
                        dve.tensor_copy(src_now[r][:], edges[0][:, at_tile(t, 0)]).then_inc(s_now, 1)
                        dve.tensor_scalar(dst_now[r][:], edges[1][:, at_tile(t, 0)], float(NPAD), None, ALU.min).then_inc(s_now, 1)
                        dve.tensor_scalar(dst_f[r][:], edges[1][:, at_tile(t, 0)], float(NPAD), None, ALU.min).then_inc(s_now, 1)
                        dve.wait_ge(s_now, 3 * (t + 1))
                        wait(dve, s_dst, t - 1)
                        dve.tensor_scalar(diag[r % 2][:], m.ident[:], dst_f[r][:], None, ALU.mult).then_inc(s_diag, 1)

                    def add(t, r, u):
                        now(t, r, u)
                        dve.wait_ge(s_dst, t + 1)
                        wait(dve, s_part, t - 1)
                        dve.tensor_scalar(equal[r % 2][:], dst_ps[r % 2][:, 0:P], dst_f[r][:], None, ALU.is_equal).then_inc(s_equal, 1)
                        dve.wait_ge(s_part, t + 1)
                        dve.wait_ge(s_old[r], 16 * (u + 1))
                        dve.tensor_tensor(new[r][:], sums[r][:], part_ps[r % 2][:, 0:D], ALU.add).then_inc(s_new, 1)

                    for_slots(dve, add, CH, RING)

                    def scale(t, r, u):
                        dve.wait_ge(s_final[r], 16 * (u + 1))
                        wait(dve, s.tr, t - 1)
                        dve.tensor_scalar(s.z_t[r][:], final[r][:], m.dis[:, at_tile(t, 0)], None, ALU.mult).then_inc(s.z, 1)
                        if not isinstance(t, int) or t >= 1:
                            tail_stats(dve, t - 1, 1 - r, m, s)

                    for_slots(dve, scale, NT, 2)
                    tail_stats(dve, NT - 1, (NT - 1) % 2, m, s, LAST)

            @block.tensor
            def _(pe):
                with when(pe, m, BAD):
                    def add(t, r, u):
                        pe.wait_ge(s_diag, t + 1)
                        wait(pe, s_equal, t - 1)
                        pe.matmul(dst_ps[r % 2][:, 0:P], m.ones[:], diag[r % 2][:], start=True, stop=True).then_inc(s_dst, 1)
                        pe.wait_ge(s_equal, t + 1)
                        pe.wait_ge(s_h[r], 16 * (u + 1))
                        wait(pe, s_new, t - 1)
                        pe.matmul(part_ps[r % 2][:, 0:D], equal[r % 2][:], h_rows[r][:], start=True, stop=True).then_inc(s_part, 1)

                    for_slots(pe, add, CH, RING)
                    for_slots(pe, lambda t, r, u: tail_transpose(pe, t, r, m, s), NT, 2)

            @block.scalar
            def _(act):
                with when(act, m, BAD):
                    for_slots(act, lambda t, r, u: tail_relu(act, t, r, u, m, s), NT, 2)

            @block.gpsimd
            def _(pool):
                with when(pool, m, BAD):
                    for r in range(2):
                        pool.wait_ge(s_stored[r], 32 * ((NT + 2 - r) // 2))

                    def add(t, r, u):
                        pool.wait_ge(s_now, 3 * (t + 1))
                        wait(pool, s_part, t - RING + 1)
                        wait(pool, s_sent[(r + 3) % RING], 16 * (u + 1 if r > 0 else u))
                        wait(pool, s_new, t - RING + 1)
                        pool.sem_inc(s_seen, 1)
                        pool.indirect_dma_start(out=sums[r][:], out_offset=None, in_=sum_at,
                                                in_offset=bass.IndirectOffsetOnAxis(ap=dst_now[r][:], axis=0)).then_inc(s_old[r], 16)
                        pool.indirect_dma_start(out=h_rows[r][:], out_offset=None, in_=h_at,
                                                in_offset=bass.IndirectOffsetOnAxis(ap=src_now[r][:], axis=0)).then_inc(s_h[r], 16)
                        pool.wait_ge(s_new, t + 1)
                        pool.sem_inc(s_seen2, 1)
                        pool.indirect_dma_start(out=sum_at, out_offset=bass.IndirectOffsetOnAxis(ap=dst_now[r][:], axis=0),
                                                in_=new[r][:], in_offset=None).then_inc(s_sent[r], 16)

                    for_slots(pool, add, CH, RING)


def norm_stage(nc, m, tag, gain, shift):
    with ExitStack() as ctx:
        mv = ctx.enter_context(nc.sbuf_tensor("bn_mv" + tag, [P, 2, 2], F32))
        root = ctx.enter_context(nc.sbuf_tensor("bn_root" + tag, [P, 2], F32))
        inv = ctx.enter_context(nc.sbuf_tensor("bn_inv" + tag, [P, 2], F32))
        off = ctx.enter_context(nc.sbuf_tensor("bn_off" + tag, [P, 2], F32))
        s_mv, s_root, s_dve = (m.sem(n + tag) for n in ("bn_mv_ready", "bn_root_ready", "bn_step"))
        with nc.Block() as block:
            @block.vector
            def _(dve):
                for c in range(2):
                    last = dve.bn_aggr(mv[:, c, :], m.stats[:, c, :])
                last.then_inc(s_mv, 1)
                dve.wait_ge(s_root, 1)
                step = Chain(dve, s_dve)
                step(dve.reciprocal(inv[:], root[:]))
                step(dve.tensor_tensor(m.scale[:], inv[:], gain[:], ALU.mult))
                step(dve.tensor_tensor(off[:], mv[:, :, 0], m.scale[:], ALU.mult))
                step(dve.tensor_tensor(m.offset[:], shift[:], off[:], ALU.subtract))

            @block.scalar
            def _(act):
                act.wait_ge(s_mv, 1)
                act.activation(root[:], mv[:, :, 1], ACT.Sqrt, bias=m.eps[:, 0:1]).then_inc(s_root, 1)


def load_zt(sp, t, r, u, m, zt, s_in, s_free, free):
    at = tile_at(sp, m.zT, t, D, F32)
    wait(sp, s_free, free)
    sp.dma_start(zt[r][:].rearrange("p c n -> p (c n)"), at).then_inc(s_in[r], 16)


def project_stage(nc, m, w_dram):
    RING = 4
    with ExitStack() as ctx:
        s = project_buffers(ctx, nc, m, "1")
        zt = [ctx.enter_context(nc.sbuf_tensor(f"zt_in{i}", [P, 2, P], F32)) for i in range(RING)]
        w = ctx.enter_context(nc.sbuf_tensor("w1_sb", [P, 2, D], F32))
        s_in = [m.sem(f"zt_loaded{i}") for i in range(RING)]
        s_w = m.sem("w1_in")

        with nc.Block() as block:
            @block.sync
            def _(sp):
                sp.dma_start(w[:], w_dram.rearrange("(k p) n -> p k n", p=P)).then_inc(s_w, 16)
                for_slots(sp, lambda t, r, u: load_zt(sp, t, r, u, m, zt, s_in, s.lhs, 2 * (t - RING + 1)), NT, RING)

            @block.scalar
            def _(act):
                def tile(t, r, u):
                    act.wait_ge(s_in[r], 16 * (u + 1))
                    wait(act, s.h, t - 1)
                    for c in range(2):
                        act.activation(s.lhs_t[r % 2][:, c, :], zt[r][:, c, :], ACT.Identity, bias=m.offset[:, c:c + 1],
                                       scale=m.scale[:, c:c + 1]).then_inc(s.lhs, 1)
                    if not isinstance(t, int) or t > 0:
                        project_scale(act, t - 1, r + 1, m, s)

                for_slots(act, tile, NT, RING)
                project_scale(act, NT - 1, NT - 1, m, s)

            @block.tensor
            def _(pe):
                pe.wait_ge(s_w, 16)

                def tile(t, r, u):
                    pe.wait_ge(s.lhs, 2 * (t + 1))
                    project_pe(pe, t, r, m, s, w)

                for_slots(pe, tile, NT, RING)

            @block.vector
            def _(dve):
                for_slots(dve, lambda t, r, u: project_split(dve, t, r, m, s), NT, RING)


def for_slots(engine, body, total, ring):
    rounds = (total - 1) // ring - 1
    for t in range(ring):
        body(t, t, 0)
    if rounds > 0:
        with engine.Fori(0, rounds) as i:
            for k in range(ring):
                body(i * ring + (ring + k), k, i + 1)
    for t in range(ring * (1 + max(rounds, 0)), total):
        body(t, t % ring, t // ring)


def product_stage(nc, m):
    SPLIT = 30
    with ExitStack() as ctx:
        sem = m.sem

        s = tail_buffers(ctx, nc, m, "_p", m.b1)
        counts = [ctx.enter_context(nc.sbuf_tensor(f"wide{i}", [P, NT, P], F32R)) for i in range(2)]
        bytes_ = [ctx.enter_context(nc.sbuf_tensor(f"bytes_in{i}", [P, NT, P], U8)) for i in range(2)]
        s_in = [sem(f"bytes_loaded{i}") for i in range(2)]
        s_v, s_a = sem("wide_by_vector"), sem("wide_by_scalar")

        def steps(engine, body):
            for t in range(4):
                body(t, t % 2, t // 2, True, t >= 1)
            with engine.Fori(0, (NT - 7) // 2) as i:
                for k in range(2):
                    body(i * 2 + (4 + k), k, i + 2, True, True)
            for t in range(NT - 3, NT):
                body(t, t % 2, t // 2, True, True)
            body(NT, NT % 2, NT // 2, False, True)

        def widen(engine, t, r, u, first, end, s_done):
            engine.wait_ge(s_in[r], 16 * (u + 1))
            wait(engine, s.sum, t - 1)
            if s_done is s_v:
                engine.tensor_copy(counts[r][:, first:end, :], bytes_[r][:, first:end, :]).then_inc(s_done, 1)
            else:
                engine.activation(counts[r][:, first:end, :], bytes_[r][:, first:end, :], ACT.Copy).then_inc(s_done, 1)

        with nc.Block() as block:
            @block.sync
            def _(sp):
                with when(sp, m, GOOD):
                    def load(t, r):
                        at = tile_at(sp, m.counts, t, NPAD, U8)
                        wait(sp, s_v, t - 1)
                        wait(sp, s_a, t - 1)
                        sp.dma_start(bytes_[r][:].rearrange("p h n -> p (h n)"), at).then_inc(s_in[r], 16)

                    def step(t, r, u, prod, tail):
                        if not isinstance(t, int) or t + 2 < NT:
                            load(t + 2, r)
                        if tail:
                            tail_store(sp, t - 1, 1 - r, m, s)

                    load(0, 0)
                    load(1, 1)
                    steps(sp, step)
                    tail_stored(sp, s)

            @block.vector
            def _(dve):
                with when(dve, m, GOOD):
                    def step(t, r, u, prod, tail):
                        if tail:
                            tail_add(dve, t - 1, 1 - r, m, s)
                        if not isinstance(t, int) or t + 1 < NT:
                            widen(dve, t + 1, 1 - r, u + r, 0, SPLIT, s_v)
                        if tail:
                            tail_stats(dve, t - 1, 1 - r, m, s, LAST if isinstance(t, int) and t - 1 == NT - 1 else P)

                    widen(dve, 0, 0, 0, 0, SPLIT, s_v)
                    steps(dve, step)

            @block.scalar
            def _(act):
                with when(act, m, GOOD):
                    def step(t, r, u, prod, tail):
                        if tail:
                            tail_low(act, t - 1, 1 - r, m, s)
                        if not isinstance(t, int) or t + 1 < NT:
                            widen(act, t + 1, 1 - r, u + r, SPLIT, NT, s_a)
                        if tail:
                            tail_relu(act, t - 1, 1 - r, u + (r - 1), m, s)

                    widen(act, 0, 0, 0, SPLIT, NT, s_a)
                    steps(act, step)

            @block.tensor
            def _(pe):
                with when(pe, m, GOOD):
                    def step(t, r, u, prod, tail):
                        if prod:
                            pe.wait_ge(s_v, t + 1)
                            wait(pe, s.z, t - 1)
                        for h in range(NT):
                            if h == 16 and tail:
                                tail_transpose(pe, t - 1, 1 - r, m, s)
                            if h == SPLIT and prod:
                                pe.wait_ge(s_a, t + 1)
                            if prod:
                                last = pe.matmul(s.sum_ps[r][:], counts[r][:, h, :], m.h[:, h, :, :].rearrange("p a d -> p (a d)"),
                                                 start=(h == 0), stop=(h == NT - 1))
                        if prod:
                            last.then_inc(s.sum, 1)

                    steps(pe, step)


def gate_stage(nc, m, x, gate_w, gate_b, ew1):
    RING = 4
    with ExitStack() as ctx:
        sem = m.sem

        def sb(name, shape, dt=F32):
            return ctx.enter_context(nc.sbuf_tensor(name, shape, dt))

        def ps(name, n):
            return [ctx.enter_context(nc.psum_tensor(f"{name}{i}", [P, 512], F32)) for i in range(n)]

        zt = [sb(f"zt_gate{i}", [P, 2, P]) for i in range(RING)]
        xin = [sb(f"x_gate{i}", [P, D]) for i in range(RING)]
        zn = [sb(f"zn{i}", [P, 2, P]) for i in range(2)]
        x1 = [sb(f"x1_{i}", [P, D]) for i in range(RING)]
        xn = [sb(f"xn{i}", [P, D]) for i in range(RING)]
        xnT = [sb(f"xnT{i}", [P, 2, P]) for i in range(2)]
        st = [sb(f"ln1_stats{i}", [P, 6]) for i in range(2)]
        mv = [sb(f"ln1_mv{i}", [P, 2]) for i in range(2)]
        root = [sb(f"ln1_root{i}", [P, 1]) for i in range(2)]
        rstd = [sb(f"ln1_rstd{i}", [P, 1]) for i in range(2)]
        gw = sb("gate_w_sb", [P, 2, NE])
        gb = sb("gate_b_sb", [P, NE])
        zps, xps, gps = ps("z_back_ps", 2), ps("xn_t_ps", 2), ps("gate_ps", 2)
        s_zt = [sem(f"zt_gate_in{i}") for i in range(RING)]
        s_x = [sem(f"x_gate_in{i}") for i in range(RING)]
        s_x1o = [sem(f"x1_stored{i}") for i in range(RING)]
        s_kept = sem("xn_kept")
        (s_w, s_zero, s_zn, s_zb, s_x1, s_st, s_seen, s_mv, s_root, s_rstd, s_xn, s_xt, s_xc, s_g, s_lg) = (sem(n) for n in (
            "gate_w_in", "x_gate_tail_zeroed", "zn_ready", "z_back", "x1_ready", "ln1_stats_ready", "ln1_stats_seen", "ln1_mv_ready",
            "ln1_root_ready", "ln1_rstd_ready", "xn1_ready", "xn1_transposed", "xn1_t_copied", "gate_ready", "logit_ready"))

        def steps(engine, body):
            for t in range(8):
                body(t, t % RING, t // RING)
            with engine.Fori(0, 9) as i:
                for k in range(4):
                    body(i * 4 + (8 + k), k, i + 2)
            for t in range(44, NT + 3):
                body(t, t % RING, t // RING)

        def has(t, lag):
            return not isinstance(t, int) or 0 <= t - lag < NT

        with nc.Block() as block:
            @block.sync
            def _(sp):
                sp.dma_start(gw[:], gate_w.rearrange("(k p) n -> p k n", p=P)).then_inc(s_w, 16)
                sp.dma_start(gb[:], gate_b.rearrange("(a n) -> a n", a=1).to_broadcast([P, NE])).then_inc(s_w, 16)

                def load(t, r, u):
                    load_zt(sp, t, r, u, m, zt, s_zt, s_zn, 2 * (t - RING + 1))
                    at = None if isinstance(t, int) and t == NT - 1 else tile_at(sp, x.rearrange("n d -> (n d)").bitcast(U8), t, D, F32)
                    wait(sp, s_x1, t - RING + 1)
                    if at is None:
                        sp.wait_ge(s_zero, 1)
                        sp.dma_start(xin[r][0:LAST, :], x[(NT - 1) * P:N, :]).then_inc(s_x[r], 16)
                    else:
                        sp.dma_start(xin[r][:], at).then_inc(s_x[r], 16)

                def step(t, r, u):
                    if not isinstance(t, int) or t + 2 < NT:
                        load(t + 2, (r + 2) % 4, u)
                    if has(t, 2):
                        q = (r + 2) % 4
                        at = tile_at(sp, m.x1, t - 2, D, F32)
                        sp.wait_ge(s_x1, t - 1)
                        sp.dma_start(at, x1[q][:]).then_inc(s_x1o[q], 16)

                load(0, 0, 0)
                load(1, 1, 0)
                steps(sp, step)
                for r in range(RING):
                    sp.wait_ge(s_x1o[r], 16 * ((NT + RING - 1 - r) // RING))

            @block.scalar
            def _(act):
                def step(t, r, u):
                    if has(t, 0):
                        act.wait_ge(s_zt[r], 16 * (u + 1))
                        wait(act, s_zb, t - 1)
                        for c in range(2):
                            act.activation(zn[r % 2][:, c, :], zt[r][:, c, :], ACT.Identity, bias=m.offset[:, c:c + 1],
                                           scale=m.scale[:, c:c + 1]).then_inc(s_zn, 1)
                    if has(t, 1):
                        q = (r + 1) % 2
                        act.wait_ge(s_mv, t)
                        wait(act, s_rstd, t - 2)
                        act.activation(root[q][:], mv[q][:, 1:2], ACT.Sqrt, bias=m.eps[:, 0:1]).then_inc(s_root, 1)
                    if has(t, 2):
                        act.wait_ge(s_xt, t - 1)
                        wait(act, s_g, t - 3)
                        act.activation(xnT[r % 2][:].rearrange("p c n -> p (c n)"), xps[r % 2][:, 0:D], ACT.Copy).then_inc(s_xc, 1)
                        act.activation(m.xn[:, at_tile(t, -2), :], xn[(r + 2) % 4][:].unsqueeze(1), ACT.Copy).then_inc(s_kept, 1)

                for k in range(2):
                    act.dma_start(m.ew1[:, k, :, :], ew1[:, k * P:(k + 1) * P, :].rearrange("e p f -> p e f")).then_inc(m.s_weights, 16)
                steps(act, step)

            @block.tensor
            def _(pe):
                pe.wait_ge(s_w, 32)

                def step(t, r, u):
                    if has(t, 0):
                        pe.wait_ge(s_zn, 2 * (t + 1))
                        wait(pe, s_x1, t - 1)
                        for c in range(2):
                            last = pe.transpose(zps[r % 2][:, c * P:(c + 1) * P], zn[r % 2][:, c, :], m.ident[:])
                        last.then_inc(s_zb, 1)
                    if has(t, 2):
                        pe.wait_ge(s_xn, t - 1)
                        wait(pe, s_xc, t - 3)
                        for c in range(2):
                            last = pe.transpose(xps[r % 2][:, c * P:(c + 1) * P], xn[(r + 2) % 4][:, c * P:(c + 1) * P], m.ident[:])
                        last.then_inc(s_xt, 1)
                    if has(t, 3):
                        q = (r + 1) % 2
                        pe.wait_ge(s_xc, t - 2)
                        wait(pe, s_lg, t - 4)
                        for c in range(2):
                            last = pe.matmul(gps[q][:, 0:NE], xnT[q][:, c, :], gw[:, c, :], start=(c == 0), stop=(c == 1))
                        last.then_inc(s_g, 1)

                steps(pe, step)

            @block.vector
            def _(dve):
                def step(t, r, u):
                    if isinstance(t, int) and t == NT - 3:
                        dve.wait_ge(s_x1, NT - RING)
                        dve.memset(xin[(NT - 1) % RING][96:P, :], 0.0).then_inc(s_zero, 1)
                    if has(t, 0):
                        dve.wait_ge(s_zb, t + 1)
                        dve.wait_ge(s_x[r], 16 * (u + 1))
                        wait(dve, s_x1o[r], 16 * u)
                        dve.tensor_tensor(x1[r][:], zps[r % 2][:, 0:D], xin[r][:], ALU.add).then_inc(s_x1, 1)
                        dve.wait_ge(s_x1, t + 1)
                        wait(dve, s_mv, t - 1)
                        dve.bn_stats(st[r % 2][:], x1[r][:]).then_inc(s_st, 1)
                    if has(t, 1):
                        p, q = (r + 3) % 4, (r + 1) % 2
                        dve.wait_ge(s_root, t)
                        dve.reciprocal(rstd[q][:], root[q][:]).then_inc(s_rstd, 1)
                        dve.wait_ge(s_rstd, t)
                        wait(dve, s_xt, t - RING)
                        wait(dve, s_kept, t - RING)
                        dve.tensor_scalar(xn[p][:], x1[p][:], mv[q][:, 0:1], rstd[q][:], ALU.subtract, ALU.mult).then_inc(s_xn, 1)
                    if has(t, 0):
                        dve.wait_ge(s_st, t + 1)
                        wait(dve, s_root, t - 1)
                        wait(dve, s_xn, t - 1)
                        dve.sem_inc(s_seen, 1)
                        dve.bn_aggr(mv[r % 2][:], st[r % 2][:]).then_inc(s_mv, 1)
                    if has(t, 3):
                        q = (r + 1) % 2
                        dve.wait_ge(s_g, t - 2)
                        dve.tensor_tensor(m.logits[:, at_tile(t, -3), :], gps[q][:, 0:NE].unsqueeze(1), gb[:].unsqueeze(1),
                                          ALU.add).then_inc(s_lg, 1)

                steps(dve, step)


def at_tile(t, lag):
    return slice(t + lag, t + lag + 1) if isinstance(t, int) else bass.ds(t + lag, 1)


def route_stage(nc, m):
    TE = NT * NE
    HALF = TE // 2
    with ExitStack() as ctx:
        sem = m.sem

        def sb(name, shape, dt=F32):
            return ctx.enter_context(nc.sbuf_tensor(name, shape, dt))

        rank_i, rank = sb("rank_i", [P, NE], I32), sb("rank", [P, NE])
        tile_i, tile_f = sb("tile_i", [1, MT], I32), sb("tile_f", [1, MT])
        below = sb("below_diag", [P, P])
        valid = sb("valid", [P, NT])
        rest, score = sb("rest", [P, NT, NE]), sb("score", [P, NT, NE])
        one = [sb(f"one{i}", [P, NT, NE]) for i in range(2)]
        both, place = sb("both", [P, NT, NE]), sb("place", [P, NT, NE])
        run = [sb(f"run{i}", [P, NT, NE]) for i in range(2)]
        top = [sb(f"top{i}", [P, NT]) for i in range(2)]
        most, total = sb("most", [P, NT]), sb("weight_sum", [P, NT])
        ntile_i = sb("ntile_i", [P, NE], I32)
        end = [sb(f"end{i}", [P, NE]) for i in range(2)]
        start = sb("expert_start", [P, NE])
        done = sb("done", [1, MT, NE])
        slot_f = sb("slot_f", [P, NT])
        exp_f = sb("expert_f", [1, MT])
        pre = ctx.enter_context(nc.psum_tensor("prefix_ps", [P, 2, 512], F32))
        tot = ctx.enter_context(nc.psum_tensor("total_ps", [P, 2, 512], F32))
        s_pool, s_ready, s_dve, s_oh, s_mm, s_diff, s_e = (sem(n) for n in (
            "route_pool_step", "route_constants", "route_step", "one_hots_ready", "ranks_ready", "gap_ready", "exp_ready"))

        with nc.Block() as block:
            @block.gpsimd
            def _(pool):
                step = Chain(pool, s_pool)
                pool.iota(rank_i[:], pattern=[[-1, NE]], base=NE, channel_multiplier=0).then_inc(s_ready, 1)
                pool.iota(tile_i[:], pattern=[[1, MT]], base=0, channel_multiplier=0).then_inc(s_ready, 1)
                step(pool.memset(below[:], 1.0))
                pool.affine_select(out=below[:], in_=below[:], compare_op=ALU.is_gt, fill=0.0, base=0,
                                   pattern=[[1, P]], channel_multiplier=-1).then_inc(s_ready, 1)
                step(pool.memset(valid[:], 1.0))
                pool.affine_select(out=valid[:, NT - 1:NT], in_=valid[:, NT - 1:NT], compare_op=ALU.is_gt, fill=0.0, base=LAST,
                                   pattern=[[0, 1]], channel_multiplier=-1).then_inc(s_ready, 1)

            @block.vector
            def _(dve):
                step = Chain(dve, s_dve)
                wide = [P, NT, NE]
                dve.wait_ge(s_ready, 4)
                step(dve.tensor_copy(rank[:], rank_i[:]))
                step(dve.tensor_copy(tile_f[:], tile_i[:]))
                for k, values in enumerate((m.logits, rest)):
                    step(dve.reduce_max(top[k][:], values[:], AX.X))
                    step(dve.tensor_tensor(score[:], values[:], top[k][:].unsqueeze(2).to_broadcast(wide), ALU.is_equal))
                    step(dve.tensor_tensor(score[:], score[:], rank[:].unsqueeze(1).to_broadcast(wide), ALU.mult))
                    step(dve.reduce_max(most[:], score[:], AX.X))
                    step(dve.tensor_tensor(one[k][:], score[:], most[:].unsqueeze(2).to_broadcast(wide), ALU.is_equal))
                    if k == 0:
                        step(dve.scalar_tensor_tensor(out=rest[:].rearrange("p t e -> p (t e)"), in0=one[0][:].rearrange("p t e -> p (t e)"),
                                                      scalar=-3.0e38, in1=m.logits[:].rearrange("p t e -> p (t e)"),
                                                      op0=ALU.mult, op1=ALU.add))
                for k in range(2):
                    step(dve.tensor_tensor(one[k][:], one[k][:], valid[:].unsqueeze(2).to_broadcast(wide), ALU.mult))
                step(dve.tensor_tensor(both[:], one[0][:], one[1][:], ALU.add))
                dve.sem_inc(s_oh, 1)
                dve.tensor_tensor(m.weight[1][:], top[1][:], top[0][:], ALU.subtract).then_inc(s_diff, 1)
                dve.wait_ge(s_e, 1)
                step(dve.tensor_scalar(total[:], m.weight[1][:], 1.0, None, ALU.add))
                step(dve.reciprocal(m.weight[0][:], total[:]))
                step(dve.tensor_tensor(m.weight[1][:], m.weight[1][:], m.weight[0][:], ALU.mult))
                dve.wait_ge(s_mm, 1)
                for c in range(2):
                    flat = run[0][:].rearrange("p t e -> p (t e)")
                    step(dve.tensor_copy(flat[:, c * HALF:(c + 1) * HALF], tot[:, c, 0:HALF]))
                a, b, d = 0, 1, 1
                while d < NT:
                    step(dve.tensor_copy(run[b][:, 0:d, :], run[a][:, 0:d, :]))
                    step(dve.tensor_tensor(run[b][:, d:NT, :], run[a][:, d:NT, :], run[a][:, 0:NT - d, :], ALU.add))
                    a, b, d = b, a, 2 * d
                step(dve.tensor_scalar(start[:], run[a][:, NT - 1, :], float(P - 1), None, ALU.add))
                step(dve.tensor_copy(ntile_i[:], start[:]))
                step(dve.tensor_scalar(ntile_i[:], ntile_i[:], 7, None, ALU.arith_shift_right))
                step(dve.tensor_copy(end[0][:], ntile_i[:]))
                step(dve.tensor_copy(start[:], end[0][:]))
                x, y, d = 0, 1, 1
                while d < NE:
                    step(dve.tensor_copy(end[y][:, 0:d], end[x][:, 0:d]))
                    step(dve.tensor_tensor(end[y][:, d:NE], end[x][:, d:NE], end[x][:, 0:NE - d], ALU.add))
                    x, y, d = y, x, 2 * d
                step(dve.tensor_tensor(start[:], end[x][:], start[:], ALU.subtract))
                step(dve.tensor_scalar(start[:], start[:], float(P), None, ALU.mult))
                for c in range(2):
                    flat, place_f = run[a][:].rearrange("p t e -> p (t e)"), place[:].rearrange("p t e -> p (t e)")
                    span = slice(c * HALF, (c + 1) * HALF)
                    step(dve.tensor_tensor(place_f[:, span], flat[:, span], tot[:, c, 0:HALF], ALU.subtract))
                    step(dve.tensor_tensor(place_f[:, span], place_f[:, span], pre[:, c, 0:HALF], ALU.add))
                step(dve.tensor_tensor(place[:], place[:], start[:].unsqueeze(1).to_broadcast(wide), ALU.add))
                for k in range(2):
                    step(dve.tensor_tensor(score[:], place[:], one[k][:], ALU.mult))
                    step(dve.reduce_sum(slot_f[:], score[:], AX.X))
                    step(dve.tensor_copy(m.slot[k][:], slot_f[:]))
                step(dve.tensor_tensor(done[:], end[x][0:1, :].unsqueeze(1).to_broadcast([1, MT, NE]),
                                       tile_f[:].unsqueeze(2).to_broadcast([1, MT, NE]), ALU.is_le))
                step(dve.reduce_sum(exp_f[:], done[:], AX.X))
                step(dve.tensor_scalar(m.expert[:], exp_f[:], float(NE - 1), None, ALU.min))

            @block.scalar
            def _(act):
                act.wait_ge(s_diff, 1)
                act.activation(m.weight[1][:], m.weight[1][:], ACT.Exp).then_inc(s_e, 1)

            @block.tensor
            def _(pe):
                pe.wait_ge(s_oh, 1)
                for c in range(2):
                    part = both[:].rearrange("p t e -> p (t e)")[:, c * HALF:(c + 1) * HALF]
                    pe.matmul(pre[:, c, 0:HALF], below[:], part, start=True, stop=True)
                    last = pe.matmul(tot[:, c, 0:HALF], m.ones[:], part, start=True, stop=True)
                last.then_inc(s_mm, 1)


def scatter_stage(nc, m, eb1, ew2, eb2):
    RING = 4
    with ExitStack() as ctx:
        sem = m.sem

        xn = [ctx.enter_context(nc.sbuf_tensor(f"xn_s{i}", [P, D], F32)) for i in range(RING)]
        at = [[ctx.enter_context(nc.sbuf_tensor(f"at{k}_{i}", [P, 1], I32)) for i in range(RING)] for k in range(2)]
        brow = ctx.enter_context(nc.sbuf_tensor("bias_rows", [P, 96], F32))
        bres = ctx.enter_context(nc.sbuf_tensor("bias_rest", [P, 96], F32))
        bpart = ctx.enter_context(nc.sbuf_tensor("bias_parts", [P, 3, 96], BF16))
        s_w, s_b, s_pick, s_dve, s_parts, s_pst, s_pin = (sem(n) for n in (
            "expert_weights2_in", "expert_bias_in", "pick_step", "bias_step", "bias_parts_ready", "bias_parts_stored", "bias_parts_in"))
        s_in = sem("rows_copied")
        s_seen = sem("send_may_start")
        s_at, s_sent = sem("at_ready"), [sem(f"rows_sent{i}") for i in range(RING)]

        with nc.Block() as block:
            @block.sync
            def _(sp):
                sp.dma_start(brow[:, 0:64], eb1.rearrange("e f -> (e f)").rearrange("(p n) -> p n", p=P)).then_inc(s_b, 16)
                sp.dma_start(brow[:, 64:96], eb2.rearrange("e f -> (e f)").rearrange("(p n) -> p n", p=P)).then_inc(s_b, 16)
                sp.wait_ge(s_parts, 1)
                for k in range(3):
                    sp.dma_start(m.b1_parts[k, :].rearrange("(p n) -> p n", p=P), bpart[:, k, 0:64]).then_inc(s_pst, 16)
                    sp.dma_start(m.b2_parts[k, :].rearrange("(p n) -> p n", p=P), bpart[:, k, 64:96]).then_inc(s_pst, 16)
                sp.wait_ge(s_pst, 96)
                sp.dma_start(m.eb1[:], m.b1_parts.rearrange("k (e f) -> (k e) f", e=NE)).then_inc(s_pin, 16)
                sp.dma_start(m.eb2[:], m.b2_parts.rearrange("k (e f) -> (k e) f", e=NE)).then_inc(s_pin, 16)
                sp.wait_ge(s_pin, 32)

            @block.scalar
            def _(act):
                def copy(t, r, u):
                    wait(act, s_sent[r], 32 * u)
                    act.activation(xn[r][:].unsqueeze(1), m.xn[:, at_tile(t, 0), :], ACT.Copy).then_inc(s_in, 1)

                for k in range(4):
                    act.dma_start(m.ew2[:, k, :, :], ew2[:, k * P:(k + 1) * P, :].rearrange("e p f -> p e f")).then_inc(s_w, 16)
                for_slots(act, copy, NT, RING)
                act.wait_ge(m.s_weights, 32)
                act.wait_ge(s_w, 64)

            @block.vector
            def _(dve):
                step = Chain(dve, s_dve)
                dve.wait_ge(s_b, 32)
                step(dve.tensor_copy(bpart[:, 0, :], brow[:]))
                step(dve.tensor_tensor(bres[:], brow[:], bpart[:, 0, :], ALU.subtract))
                step(dve.tensor_copy(bpart[:, 1, :], bres[:]))
                step(dve.tensor_tensor(brow[:], bres[:], bpart[:, 1, :], ALU.subtract))
                step(dve.tensor_copy(bpart[:, 2, :], brow[:]))
                dve.sem_inc(s_parts, 1)

                def index(t, r, u):
                    wait(dve, s_sent[r], 32 * u)
                    for k in range(2):
                        dve.tensor_copy(at[k][r][:], m.slot[k][:, at_tile(t, 0)]).then_inc(s_at, 1)

                for_slots(dve, index, NT, RING)

            @block.gpsimd
            def _(pool):
                step = Chain(pool, s_pick)
                step(pool.memset(m.pick[:], 0.0))
                for k in range(3):
                    step(pool.affine_select(out=m.pick[:], in_=m.pick[:], compare_op=ALU.not_equal, fill=1.0, base=-NE * k,
                                            pattern=[[-1, NE], [0, P]], channel_multiplier=1))

                def send(t, r, u):
                    n = LAST if isinstance(t, int) and t == NT - 1 else P
                    pool.wait_ge(s_in, t + 1)
                    pool.wait_ge(s_at, 2 * (t + 1))
                    pool.sem_inc(s_seen, 1)
                    for k in range(2):
                        pool.indirect_dma_start(out=m.rows, out_offset=bass.IndirectOffsetOnAxis(ap=at[k][r][0:n, :], axis=0),
                                                in_=xn[r][0:n, :], in_offset=None).then_inc(s_sent[r], 16)

                for_slots(pool, send, NT, RING)
                for r in range(RING):
                    pool.wait_ge(s_sent[r], 32 * ((NT + RING - 1 - r) // RING))


def expert_stage(nc, m):
    RING = 2
    with ExitStack() as ctx:
        sem = m.sem

        def sb(name, shape, n, dt=F32):
            return [ctx.enter_context(nc.sbuf_tensor(f"{name}{i}", shape, dt)) for i in range(n)]

        def ps(name):
            return [ctx.enter_context(nc.psum_tensor(f"{name}{i}", [P, 512], F32)) for i in range(2)]

        xe, xT, hid, hT, ye = sb("xe", [P, D], 4), sb("xeT", [P, 2, P], 2), sb("hid", [P, FF], 2), sb("hidT", [P, 4, P], 2), sb("ye", [P, D], 4)
        xps, hps, tps, yps = ps("xe_ps"), ps("hid_ps"), ps("hidT_ps"), ps("ye_ps")
        s_in, s_out = [sem(f"xe_in{i}") for i in range(4)], [sem(f"ye_stored{i}") for i in range(4)]
        s_xt, s_xc, s_h, s_relu, s_ht, s_hc, s_y, s_yc = (sem(n) for n in (
            "xe_transposed", "xeT_copied", "hid_ready", "hid_relu", "hid_transposed", "hidT_copied", "ye_ready", "ye_copied"))

        def steps(engine, body):
            for t in range(8):
                body(t, t % 4, t // 4)
            rounds = (MT - 8) // 4
            with engine.Fori(0, rounds) as i:
                for k in range(4):
                    body(i * 4 + (8 + k), k, i + 2)
            for t in range(8 + 4 * rounds, MT + 3):
                body(t, t % 4, t // 4)

        def has(t, lag):
            return not isinstance(t, int) or 0 <= t - lag < MT

        with nc.Block() as block:
            @block.sync
            def _(sp):
                rows, ys = m.rows.rearrange("n d -> (n d)").bitcast(U8), m.ys.rearrange("n d -> (n d)").bitcast(U8)

                def load(t, r):
                    at = tile_at(sp, rows, t, D, F32)
                    wait(sp, s_xt, t - 3)
                    sp.dma_start(xe[r][:], at).then_inc(s_in[r], 16)

                load(0, 0)
                load(1, 1)

                def step(t, r, u):
                    if has(t, -2):
                        load(t + 2, (r + 2) % 4)
                    if has(t, 3):
                        q = (r + 1) % 4
                        at = tile_at(sp, ys, t - 3, D, F32)
                        sp.wait_ge(s_yc, t - 2)
                        sp.dma_start(at, ye[q][:]).then_inc(s_out[q], 16)

                steps(sp, step)
                for r in range(4):
                    sp.wait_ge(s_out[r], 16 * ((MT + 3 - r) // 4))

            @block.tensor
            def _(pe):
                def step(t, r, u):
                    if has(t, 0):
                        pe.wait_ge(s_in[r], 16 * (u + 1))
                        wait(pe, s_xc, t - 1)
                        for c in range(2):
                            last = pe.transpose(xps[r % 2][:, c * P:(c + 1) * P], xe[r][:, c * P:(c + 1) * P], m.ident[:])
                        last.then_inc(s_xt, 1)
                    if has(t, 2):
                        pe.wait_ge(s_relu, t - 1)
                        wait(pe, s_hc, t - 3)
                        for c in range(4):
                            last = pe.transpose(tps[r % 2][:, c * P:(c + 1) * P], hid[r % 2][:, c * P:(c + 1) * P], m.ident[:])
                        last.then_inc(s_ht, 1)
                    if has(t, 1):
                        q = (r + 1) % 2
                        e = pe.value_load(m.expert[0:1, at_tile(t, -1)], min_val=0, max_val=NE - 1)
                        pe.wait_ge(s_xc, t)
                        wait(pe, s_relu, t - 2)
                        pe.matmul(hps[q][:], m.pick[:, bass.ds(e, 1), :].rearrange("k o n -> k (o n)"), m.eb1[:], start=True, stop=False)
                        for k in range(2):
                            last = pe.matmul(hps[q][:], xT[q][:, k, :], m.ew1[:, k, bass.ds(e, 1), :].rearrange("p o f -> p (o f)"),
                                             start=False, stop=(k == 1))
                        last.then_inc(s_h, 1)
                    if has(t, 3):
                        q = (r + 1) % 2
                        e = pe.value_load(m.expert[0:1, at_tile(t, -3)], min_val=0, max_val=NE - 1)
                        pe.wait_ge(s_hc, t - 2)
                        wait(pe, s_yc, t - 4)
                        pe.matmul(yps[q][:, 0:D], m.pick[:, bass.ds(e, 1), :].rearrange("k o n -> k (o n)"), m.eb2[:], start=True, stop=False)
                        for k in range(4):
                            last = pe.matmul(yps[q][:, 0:D], hT[q][:, k, :], m.ew2[:, k, bass.ds(e, 1), :].rearrange("p o f -> p (o f)"),
                                             start=False, stop=(k == 3))
                        last.then_inc(s_y, 1)

                steps(pe, step)

            @block.scalar
            def _(act):
                def step(t, r, u):
                    if has(t, 0):
                        act.wait_ge(s_xt, t + 1)
                        wait(act, s_h, t - 1)
                        act.activation(xT[r % 2][:].rearrange("p c n -> p (c n)"), xps[r % 2][:, 0:D], ACT.Copy).then_inc(s_xc, 1)
                    if has(t, 1):
                        q = (r + 1) % 2
                        act.wait_ge(s_h, t)
                        wait(act, s_ht, t - 2)
                        act.activation(hid[q][:], hps[q][:], ACT.Relu).then_inc(s_relu, 1)

                steps(act, step)

            @block.vector
            def _(dve):
                def step(t, r, u):
                    if has(t, 2):
                        dve.wait_ge(s_ht, t - 1)
                        wait(dve, s_y, t - 3)
                        dve.tensor_copy(hT[r % 2][:].rearrange("p c n -> p (c n)"), tps[r % 2][:]).then_inc(s_hc, 1)
                    if has(t, 3):
                        q = (r + 1) % 4
                        dve.wait_ge(s_y, t - 2)
                        wait(dve, s_out[q], 16 * (u if r == 3 else u - 1))
                        dve.tensor_copy(ye[q][:], yps[q % 2][:, 0:D]).then_inc(s_yc, 1)

                steps(dve, step)


def combine_stage(nc, m, gamma, beta, out):
    RING = 4
    with ExitStack() as ctx:
        sem = m.sem

        def sb(name, shape, n, dt=F32):
            return [ctx.enter_context(nc.sbuf_tensor(f"{name}{i}", shape, dt)) for i in range(n)]

        gam = ctx.enter_context(nc.sbuf_tensor("gamma_sb", [P, D], F32))
        bet = ctx.enter_context(nc.sbuf_tensor("beta_sb", [P, D], F32))
        y1, y2, x1, res = (sb(n, [P, D], RING) for n in ("y1_", "y2_", "x1_c", "res"))
        at = [sb(f"from{k}_", [P, 1], RING, I32) for k in range(2)]
        part, yv, scaled, x1b = (sb(n, [P, D], 2) for n in ("part", "yv", "scaled", "x1_beta"))
        st, mv, root, rstd = sb("ln2_stats", [P, 6], 2), sb("ln2_mv", [P, 2], 2), sb("ln2_root", [P, 1], 2), sb("ln2_rstd", [P, 1], 2)
        s_gb = sem("gamma_beta_in")
        s_in, s_got, s_out = ([sem(f"{n}{i}") for i in range(RING)] for n in ("c_rows_in", "expert_rows_in", "out_stored"))
        s_at, s_seen, s_part, s_x1b, s_y, s_st, s_seen2, s_mv, s_root, s_rstd, s_scaled, s_res = (sem(n) for n in (
            "from_ready", "from_seen", "c_part", "c_x1_beta", "c_y", "c_stats", "c_stats_seen", "c_mv", "c_root", "c_rstd", "c_scaled", "c_result"))

        def steps(engine, body):
            for t in range(8):
                body(t, t % RING, t // RING)
            with engine.Fori(0, 9) as i:
                for k in range(4):
                    body(i * 4 + (8 + k), k, i + 2)
            for t in range(44, NT + 1):
                body(t, t % RING, t // RING)

        def has(t, lag):
            return not isinstance(t, int) or 0 <= t - lag < NT

        with nc.Block() as block:
            @block.sync
            def _(sp):
                sp.dma_start(gam[:], gamma.rearrange("(a n) -> a n", a=1).to_broadcast([P, D])).then_inc(s_gb, 16)
                sp.dma_start(bet[:], beta.rearrange("(a n) -> a n", a=1).to_broadcast([P, D])).then_inc(s_gb, 16)
                out_bytes = out.rearrange("n d -> (n d)").bitcast(U8)

                def load(t, r):
                    a = tile_at(sp, m.x1, t, D, F32)
                    wait(sp, s_x1b, t - RING + 1)
                    sp.dma_start(x1[r][:], a).then_inc(s_in[r], 16)

                load(0, 0)
                load(1, 1)

                def step(t, r, u):
                    if has(t, -2):
                        load(t + 2, (r + 2) % RING)
                    if has(t, 1):
                        q = (r + 3) % 4
                        if isinstance(t, int) and t == NT:
                            sp.wait_ge(s_res, t)
                            sp.dma_start(out[(NT - 1) * P:N, :], res[q][0:LAST, :]).then_inc(s_out[q], 16)
                        else:
                            to = tile_at(sp, out_bytes, t - 1, D, F32)
                            sp.wait_ge(s_res, t)
                            sp.dma_start(to, res[q][:]).then_inc(s_out[q], 16)

                steps(sp, step)
                for r in range(RING):
                    sp.wait_ge(s_out[r], 16 * ((NT + RING - 1 - r) // RING))

            @block.gpsimd
            def _(pool):
                def step(t, r, u):
                    if has(t, 0):
                        pool.wait_ge(s_at, 2 * (t + 1))
                        wait(pool, s_y, t - RING + 1)
                        pool.sem_inc(s_seen, 1)
                        for k, y in enumerate((y1, y2)):
                            pool.indirect_dma_start(out=y[r][:], out_offset=None, in_=m.ys,
                                                    in_offset=bass.IndirectOffsetOnAxis(ap=at[k][r][:], axis=0)).then_inc(s_got[r], 16)

                steps(pool, step)

            @block.vector
            def _(dve):
                def index(t, r, u):
                    wait(dve, s_got[r], 32 * u)
                    for k in range(2):
                        dve.tensor_copy(at[k][r][:], m.slot[k][:, at_tile(t, 0)]).then_inc(s_at, 1)

                for t in range(3):
                    index(t, t, 0)
                dve.wait_ge(s_gb, 32)

                def step(t, r, u):
                    if has(t, -3):
                        index(t + 3, (r + 3) % RING, u if r == 0 else u + 1)
                    q, p = r % 2, (r + 1) % 2
                    if has(t, 0):
                        dve.wait_ge(s_got[r], 32 * (u + 1))
                        wait(dve, s_y, t - 1)
                        dve.scalar_tensor_tensor(out=part[q][:].unsqueeze(1), in0=y1[r][:].unsqueeze(1), scalar=m.weight[0][:, at_tile(t, 0)],
                                                 in1=m.xn[:, at_tile(t, 0), :], op0=ALU.mult, op1=ALU.add).then_inc(s_part, 1)
                        dve.wait_ge(s_in[r], 16 * (u + 1))
                        wait(dve, s_res, t - 1)
                        dve.tensor_tensor(x1b[q][:], x1[r][:], bet[:], ALU.add).then_inc(s_x1b, 1)
                        dve.wait_ge(s_part, t + 1)
                        wait(dve, s_scaled, t - 1)
                        dve.scalar_tensor_tensor(out=yv[q][:], in0=y2[r][:], scalar=m.weight[1][:, at_tile(t, 0)], in1=part[q][:],
                                                 op0=ALU.mult, op1=ALU.add).then_inc(s_y, 1)
                    if has(t, 1):
                        dve.wait_ge(s_root, t)
                        wait(dve, s_res, t - 2)
                        dve.reciprocal(rstd[p][:], root[p][:]).then_inc(s_rstd, 1)
                    if has(t, 0):
                        dve.wait_ge(s_y, t + 1)
                        wait(dve, s_mv, t - 1)
                        dve.bn_stats(st[q][:], yv[q][:]).then_inc(s_st, 1)
                    if has(t, 1):
                        wait(dve, s_res, t - 2)
                        dve.scalar_tensor_tensor(out=scaled[p][:], in0=yv[p][:], scalar=mv[p][:, 0:1], in1=gam[:],
                                                 op0=ALU.subtract, op1=ALU.mult).then_inc(s_scaled, 1)
                    if has(t, 0):
                        dve.wait_ge(s_st, t + 1)
                        wait(dve, s_root, t - 1)
                        wait(dve, s_scaled, t - 1)
                        dve.sem_inc(s_seen2, 1)
                        dve.bn_aggr(mv[q][:], st[q][:]).then_inc(s_mv, 1)
                    if has(t, 1):
                        o = (r + 3) % 4
                        dve.wait_ge(s_rstd, t)
                        dve.wait_ge(s_scaled, t)
                        wait(dve, s_out[o], 16 * (u if r > 0 else u - 1))
                        dve.scalar_tensor_tensor(out=res[o][:], in0=scaled[p][:], scalar=rstd[p][:], in1=x1b[p][:],
                                                 op0=ALU.mult, op1=ALU.add).then_inc(s_res, 1)

                steps(dve, step)

            @block.scalar
            def _(act):
                def step(t, r, u):
                    if has(t, 0):
                        q = r % 2
                        act.wait_ge(s_mv, t + 1)
                        wait(act, s_rstd, t - 1)
                        act.activation(root[q][:], mv[q][:, 1:2], ACT.Sqrt, bias=m.eps[:, 0:1]).then_inc(s_root, 1)

                steps(act, step)




def program(nc, x, src, dst, w0, b0, g0, bt0, w1, b1, g1, bt1, gate_w, gate_b, ew1, eb1, ew2, eb2, gamma, beta, out):
    def dram(name, shape, dt):
        return nc.dram_tensor(name, shape, dt).ap()

    m = Names()
    m.codes = dram("edge_codes", [EPAD], I32)
    m.deg = dram("degrees", [NBLK * BD], F32)
    m.counts = dram("counts", [NT * P * NT * P], U8)
    m.zT = dram("z_t", [NT * P * D * 4], U8)
    m.x1 = dram("x1_dram", [NT * P * D * 4], U8)
    m.any_h = dram("any_h_dram", [(NT + 1) * P * D * 4], U8)
    m.any_sum = dram("any_sum_dram", [(NT + 1) * P * D * 4], U8)
    m.rows = dram("expert_rows", [MT * P, D], F32)
    m.ys = dram("expert_out", [MT * P, D], F32)
    m.b1_parts = dram("b1_parts", [3, NE * FF], BF16)
    m.b2_parts = dram("b2_parts", [3, NE * D], BF16)
    m.sem = Semaphores(nc)
    m.s_weights = nc.alloc_semaphore("expert_weights_in")
    with ExitStack() as ctx:
        def sb(name, shape, dt):
            return ctx.enter_context(nc.sbuf_tensor(name, shape, dt))

        m.iota16, m.iota4 = sb("iota16", [P, P], FP16), sb("iota4", [P, P, 4], FP16)
        m.ident, m.ones = sb("ident", [P, P], F32), sb("ones", [P, P], F32)
        m.flags = sb("flags", [P, 2], I32)
        m.dis = sb("dis", [P, NT], F32)
        m.eps = sb("eps", [P, 1], F32)
        m.stats = sb("z_stats", [P, 2, NT * 6], F32)
        m.b0, m.b1, m.g0, m.g1, m.bt0, m.bt1 = (sb(n, [P, 2], F32) for n in ("b0_sb", "b1_sb", "g0_sb", "g1_sb", "bt0_sb", "bt1_sb"))
        m.scale, m.offset = sb("bn_scale", [P, 2], F32), sb("bn_offset", [P, 2], F32)
        with nc.sbuf_tensor("keyT", [P, NBLK], FP16) as m.keyT, nc.sbuf_tensor("loT", [P, NBLK], FP16) as m.loT:
            edge_stage(nc, m, src, dst)
            parameter_stage(nc, m, [(m.b0, b0), (m.g0, g0), (m.bt0, bt0), (m.b1, b1), (m.g1, g1), (m.bt1, bt1)])
            dis_stage(nc, m)
            any_degrees(nc, m)
            with nc.sbuf_tensor("h", [P, NT, 2, D], F32R) as m.h:
                input_stage(nc, m, x, w0)
                build_stage(nc, m)
                m.sem.renew()
                any_sums(nc, m, "_any0", m.b0)
                norm_stage(nc, m, "0", m.g0, m.bt0)
                project_stage(nc, m, w1)
                product_stage(nc, m)
                m.sem.renew()
                any_sums(nc, m, "_any1", m.b1)
                norm_stage(nc, m, "1", m.g1, m.bt1)
        m.sem.renew()
        m.weight = [sb(f"weight{k}", [P, NT], F32) for k in range(2)]
        m.slot = [sb(f"slot{k}", [P, NT], I32) for k in range(2)]
        m.expert = sb("tile_expert", [1, MT], I32)
        m.xn = sb("xn_kept", [P, NT, D], F32)
        with ExitStack() as big:
            def big_sb(name, shape, dt):
                return big.enter_context(nc.sbuf_tensor(name, shape, dt))

            m.ew1 = big_sb("ew1", [P, 2, NE, FF], F32)
            with nc.sbuf_tensor("logits", [P, NT, NE], F32) as m.logits:
                gate_stage(nc, m, x, gate_w, gate_b, ew1)
                route_stage(nc, m)
            m.ew2 = big_sb("ew2", [P, 4, NE, D], F32)
            m.eb1, m.eb2 = big_sb("eb1", [3 * NE, FF], BF16), big_sb("eb2", [3 * NE, D], BF16)
            m.pick = big_sb("pick", [3 * NE, NE, P], BF16)
            m.sem.renew()
            scatter_stage(nc, m, eb1, ew2, eb2)
            expert_stage(nc, m)
        combine_stage(nc, m, gamma, beta, out)


def parameter_stage(nc, m, columns):
    s_in, s_eps = m.sem("parameters_in"), m.sem("eps_set")
    with nc.Block() as block:
        @block.sync
        def _(sp):
            with nc.allow_non_contiguous_dma(reason="six vectors of 256 words"):
                for t, v in columns:
                    sp.dma_start(t[:], v.rearrange("(c p) -> p c", p=P)).then_inc(s_in, 16)
            sp.wait_ge(s_in, 16 * len(columns))

        @block.vector
        def _(dve):
            dve.memset(m.eps[:], EPS).then_inc(s_eps, 1)


_INS = ["x", "src", "dst", "L0_gnn_W0", "L0_gnn_b0", "L0_gnn_g0", "L0_gnn_bt0", "L0_gnn_W1", "L0_gnn_b1", "L0_gnn_g1", "L0_gnn_bt1",
        "L0_ffn_gate_w", "L0_ffn_gate_b", "L0_ffn_w1", "L0_ffn_b1", "L0_ffn_w2", "L0_ffn_b2", "L0_ffn_gamma", "L0_ffn_beta"]


def kernel(**inputs):
    import concourse.bacc as bacc
    from concourse.bass_utils import run_bass_kernel_spmd

    nc = bacc.Bacc("TRN2", target_bir_lowering=False, num_devices=1)
    arrays, args = {}, []
    for name in _INS:
        a = np.ascontiguousarray(inputs[name])
        arrays["in_" + name] = a
        args.append(nc.dram_tensor("in_" + name, a.shape, mybir.dt.from_np(a.dtype), kind="ExternalInput").ap())
    args.append(nc.dram_tensor("out", (N, D), F32, kind="ExternalOutput").ap())
    program(nc, *args)
    return run_bass_kernel_spmd(nc, [arrays], core_ids=[0]).results[0]["out"]
```

```python
from contextlib import ExitStack, contextmanager

import numpy as np
import concourse.bass as bass
from concourse import mybir

F32 = mybir.dt.float32
F32R = mybir.dt.float32r
BF16 = mybir.dt.bfloat16
FP16 = mybir.dt.float16
I32 = mybir.dt.int32
U8 = mybir.dt.uint8
ALU = mybir.AluOpType
ACT = mybir.ActivationFunctionType
AX = mybir.AxisListType

P = 128
N = 6250
D = 256
NT = -(-N // P)
NPAD = NT * P
LAST = N - (NT - 1) * P
E = 206250
ROWS = -(-E // (P * P))
CH = ROWS * P
EPAD = P * CH
CODE = 13
BD = 2
SLOTS = P
REAL = SLOTS - BD
WIN = 8
BW = WIN // BD
WSLOTS = 3 * P
WT = 7
NBLK = WT * P * BW
KEYS = NT * BD
UNITS = P // BD
GROUPS = UNITS // 8
NO_NODE = (1 << CODE) - 1
EPS = 1e-5
NE = 16
FF = 512
GOOD, BAD = 0, 1
MT = -(-(2 * N + (P - 1) * NE) // P)


class Names:
    pass


class Chain:

    def __init__(self, engine, sem):
        self.engine, self.sem, self.n = engine, sem, 0

    def __call__(self, ins):
        self.later(ins)
        self.engine.wait_ge(self.sem, self.n)

    def later(self, ins):
        self.n += 1
        ins.then_inc(self.sem, 1)

    def settle(self):
        self.engine.wait_ge(self.sem, self.n)


def edge_stage(nc, m, src, dst):
    with ExitStack() as ctx:
        def sb(name, shape, dt):
            return ctx.enter_context(nc.sbuf_tensor(name, shape, dt))

        def ps(name, shape):
            return ctx.enter_context(nc.psum_tensor(name, shape, F32))

        sem = m.sem

        iota_i = sb("iota_i", [P, P], I32)
        src_i, dst_i = sb("src_i", [P, CH], I32), sb("dst_i", [P, CH], I32)
        head_i, head = sb("head_i", [P, ROWS], I32), sb("head", [P, ROWS], FP16)
        ident16, ones16 = sb("ident16", [P, P], FP16), sb("ones16", [P, P], FP16)
        head_diag, heads = sb("head_diag", [P, ROWS, P], FP16), sb("heads", [P, ROWS * P], FP16)
        window_i, window = sb("window_i", [P, WT], I32), sb("window", [P, WT], F32)
        first_i, first = sb("first_i", [P, WT, BW], I32), sb("first", [P, WT, WIN // BD], F32)
        below = sb("below", [P, ROWS * P], BF16)
        rowf, rowi = sb("rowf", [P, WT], F32), sb("rowi", [P, WT], I32)
        row_i = sb("row_i", [P, WT, P], I32)
        cnt = sb("cnt", [P, WT], F32)
        win_start, win_start_i = sb("win_start", [P, WT], F32), sb("win_start_i", [P, WT], I32)
        win_i = sb("win_i", [P, WT, WSLOTS], I32)
        sub = sb("sub", [P, WT, BW], F32)
        start_i = sb("start_i", [P, WT, BW], I32)
        code = sb("code", [P, WT, BW, SLOTS], I32)
        slot_dst, hi, lo_i = (sb(n, [P, WT, BW, SLOTS], I32) for n in ("slot_dst", "hi", "lo_i"))
        dl, no_dst, key, lo = (sb(n, [P, 2, BW, SLOTS], F32) for n in ("dl", "no_dst", "key", "lo"))
        hit = sb("hit", [P, 2, WIN, SLOTS], BF16)
        minus = sb("minus_128", [P, 1], F32)
        deg = sb("deg", [P, WT, WIN], F32)
        over = sb("over", [P, WT * WIN], BF16)
        sums, bad = sb("sums", [P, 2], F32), sb("bad", [P, 1], F32)
        head_ps = ps("head_ps", [P, 4, 512])
        pt = [ps(f"keys_ps{i}", [P, 512]) for i in range(2)]
        lt = [ps(f"los_ps{i}", [P, 512]) for i in range(2)]

        (s_pads, s_pads_src, s_src_in, s_dst_in, s_code, s_codes, s_const, s_pool, s_dve, s_diag, s_heads, s_row, s_rows, s_win, s_start, s_lo_i, s_lo,
         s_keys, s_key_t, s_lo_t, s_ev, s_ev2, s_deg, s_degd, s_sums, s_total) = (sem(n) for n in (
             "dst_pads_set", "src_pads_set", "src_in", "dst_in", "codes_packed", "codes_stored", "constants_ready", "pool_step", "dve_step",
             "head_diagonals_ready", "heads_ready", "row_index_ready", "rows_in", "window_starts_ready", "block_starts_ready",
             "los_ready", "los_widened", "keys_ready", "keys_transposed", "los_transposed", "keys_copied", "los_copied",
             "degrees_ready", "degrees_stored", "sums_ready", "total_ready"))
        s_heads_copied, s_dl, s_no_dst = sem("heads_copied"), sem("dl_ready"), sem("no_dst_ready")
        s_window = [sem(f"window_in{w}") for w in range(WT)]
        s_slots = [sem(f"slots_in{w}") for w in range(WT)]
        full = E // CH
        head_sums = head_ps[:].rearrange("p a b -> p (a b)")[:, 0:ROWS * P]

        with nc.Block() as block:
            @block.sync
            def _(sp):
                sp.wait_ge(s_pads, 1)
                sp.dma_start(dst_i[0:full, :], dst[0:full * CH].rearrange("(p c) -> p c", p=full)).then_inc(s_dst_in, 16)
                sp.dma_start(dst_i[full:full + 1, 0:E - full * CH], dst[full * CH:E].rearrange("(a c) -> a c", a=1)).then_inc(s_dst_in, 16)
                sp.wait_ge(s_code, 1)
                sp.dma_start(m.codes.rearrange("(p c) -> p c", p=P), dst_i[:]).then_inc(s_codes, 16)
                sp.wait_ge(s_deg, 1)
                sp.dma_start(m.deg.rearrange("(w p d) -> p w d", p=P, d=WIN), deg[:]).then_inc(s_degd, 16)
                sp.wait_ge(s_degd, 16)

            @block.scalar
            def _(act):
                act.wait_ge(s_pads_src, 1)
                act.dma_start(src_i[0:full, :], src[0:full * CH].rearrange("(p c) -> p c", p=full)).then_inc(s_src_in, 16)
                act.dma_start(src_i[full:full + 1, 0:E - full * CH], src[full * CH:E].rearrange("(a c) -> a c", a=1)).then_inc(s_src_in, 16)
                act.wait_ge(s_heads, 1)
                act.activation(heads[:], head_sums, ACT.Copy).then_inc(s_heads_copied, 1)
                for w in range(WT):
                    act.wait_ge(s_dl, w + 1)
                    if w >= 2:
                        act.wait_ge(s_keys, w - 1)
                    act.activation(no_dst[:, w % 2, :, :], dl[:, w % 2, :, :], ACT.Relu, scale=128.0, bias=minus[:, 0:1]).then_inc(s_no_dst, 1)
                    act.wait_ge(s_lo_i, w + 1)
                    if w >= 2:
                        act.wait_ge(s_lo_t, w - 1)
                    act.activation(lo[:, w % 2, :, :], lo_i[:, w, :, :], ACT.Copy).then_inc(s_lo, 1)
                    if w >= 1:
                        act.wait_ge(s_lo_t, w)
                        act.activation(block_columns(m.loT, w - 1), lt[(w - 1) % 2][:].rearrange("p (j b) -> p j b", j=BW), ACT.Copy).then_inc(s_ev2, 1)
                act.wait_ge(s_lo_t, WT)
                act.activation(block_columns(m.loT, WT - 1), lt[(WT - 1) % 2][:].rearrange("p (j b) -> p j b", j=BW), ACT.Copy).then_inc(s_ev2, 1)

            @block.gpsimd
            def _(pool):
                step = Chain(pool, s_pool)
                pool.memset(src_i[96:P, :], 0).then_inc(s_pads_src, 1)
                pool.wait_ge(s_pads_src, 1)
                step(pool.memset(m.ident[:], 0.0))
                pool.affine_select(out=m.ident[:], in_=m.ident[:], compare_op=ALU.not_equal, fill=1.0, base=0,
                                   pattern=[[-1, P]], channel_multiplier=1).then_inc(s_const, 1)
                pool.memset(m.ones[:], 1.0).then_inc(s_const, 1)
                pool.iota(first_i[:], pattern=[[P * WIN, WT], [BD, BW]], base=0, channel_multiplier=WIN).then_inc(s_const, 1)
                pool.iota(window_i[:], pattern=[[P, WT]], base=0, channel_multiplier=1).then_inc(s_const, 1)
                step(pool.iota(iota_i[:], pattern=[[1, P]], base=0, channel_multiplier=0))
                pool.tensor_copy(m.iota16[:], iota_i[:]).then_inc(s_const, 1)
                loop = (1 << CODE) + 1
                for w in range(WT):
                    pool.iota(code[:, w, :, REAL:SLOTS], pattern=[[loop * BD, BW], [loop, BD]], base=loop * P * WIN * w,
                              channel_multiplier=loop * WIN).then_inc(s_const, 1)
                rows = m.codes.rearrange("(r c) -> r c", c=P)
                edges = m.codes.rearrange("(e o) -> e o", o=1)
                pool.wait_ge(s_codes, 16)
                pool.wait_ge(s_row, 1)
                for w in range(WT):
                    pool.indirect_dma_start(out=row_i[:, w, :], out_offset=None, in_=rows,
                                            in_offset=bass.IndirectOffsetOnAxis(ap=rowi[:, w:w + 1], axis=0)).then_inc(s_rows, 16)
                pool.wait_ge(s_win, 1)
                for w in range(WT):
                    pool.indirect_dma_start(out=win_i[:, w, :], out_offset=None, in_=edges,
                                            in_offset=bass.IndirectOffsetOnAxis(ap=win_start_i[:, w:w + 1], axis=0)).then_inc(s_window[w], 16)
                for w in range(WT):
                    pool.wait_ge(s_start, w + 1)
                    for j in range(BW):
                        pool.indirect_dma_start(out=code[:, w, j, 0:REAL], out_offset=None, in_=edges,
                                                in_offset=bass.IndirectOffsetOnAxis(ap=start_i[:, w, j:j + 1], axis=0)).then_inc(s_slots[w], 16)

            @block.vector
            def _(dve):
                step = Chain(dve, s_dve)
                dve.memset(dst_i[96:P, :], NO_NODE).then_inc(s_pads, 1)
                step.later(dve.memset(minus[:], -128.0))
                dve.wait_ge(s_const, 5 + WT)
                step.later(dve.tensor_copy(first[:], first_i[:]))
                step.later(dve.tensor_copy(m.iota4[:], m.iota16[:].unsqueeze(2).to_broadcast([P, P, 4])))
                step.later(dve.tensor_copy(window[:], window_i[:]))
                step.later(dve.tensor_copy(ident16[:], m.ident[:]))
                step(dve.tensor_copy(ones16[:], m.ones[:]))
                dve.wait_ge(s_dst_in, 32)
                step(dve.tensor_scalar(head_i[:], dst_i[:].rearrange("p (r c) -> p r c", c=P)[:, :, 0], 3, None, ALU.arith_shift_right))
                step(dve.tensor_copy(head[:], head_i[:]))
                dve.tensor_tensor(head_diag[:], ident16[:].unsqueeze(1).to_broadcast([P, ROWS, P]),
                                  head[:].unsqueeze(2).to_broadcast([P, ROWS, P]), ALU.mult).then_inc(s_diag, 1)
                dve.wait_ge(s_src_in, 32)
                dve.scalar_tensor_tensor(out=dst_i[:], in0=dst_i[:], scalar=CODE, in1=src_i[:], op0=ALU.logical_shift_left,
                                         op1=ALU.bitwise_or).then_inc(s_code, 1)
                dve.wait_ge(s_heads_copied, 1)
                for w in range(WT):
                    step(dve.tensor_scalar(below[:], heads[:], window[:, w:w + 1], 0.0, ALU.is_lt, ALU.add, accum_out=rowf[:, w:w + 1]))
                step(dve.tensor_scalar(rowf[:], rowf[:], -1.0, 0.0, ALU.add, ALU.max))
                dve.tensor_copy(rowi[:], rowf[:]).then_inc(s_row, 1)
                dve.wait_ge(s_rows, 16 * WT)
                step(dve.tensor_scalar(row_i[:], row_i[:], CODE, None, ALU.arith_shift_right))
                for w in range(WT):
                    step(dve.tensor_scalar(below[:, 0:P], row_i[:, w, :], first[:, w, 0:1], 0.0, ALU.is_lt, ALU.add,
                                           accum_out=cnt[:, w:w + 1]))
                step(dve.scalar_tensor_tensor(out=win_start[:], in0=rowf[:], scalar=float(P), in1=cnt[:], op0=ALU.mult, op1=ALU.add))
                dve.tensor_copy(win_start_i[:], win_start[:]).then_inc(s_win, 1)
                step(dve.memset(sub[:], 0.0))
                for w in range(WT):
                    dve.wait_ge(s_window[w], 16)
                    step(dve.tensor_scalar(win_i[:, w, :], win_i[:, w, :], CODE, None, ALU.arith_shift_right))
                    for j in range(1, BW):
                        step.later(dve.tensor_scalar(below[:, j * WSLOTS:(j + 1) * WSLOTS], win_i[:, w, :], first[:, w, j:j + 1], 0.0, ALU.is_lt, ALU.add,
                                               accum_out=sub[:, w, j:j + 1]))
                    step.settle()
                    step(dve.tensor_scalar(sub[:, w, :], sub[:, w, :], win_start[:, w:w + 1], None, ALU.add))
                    dve.tensor_copy(start_i[:, w, :], sub[:, w, :]).then_inc(s_start, 1)

                def copy_keys(w):
                    dve.wait_ge(s_key_t, w + 1)
                    dve.tensor_scalar(block_columns(m.keyT, w), pt[w % 2][:].rearrange("p (j b) -> p j b", j=BW), 500.0, None,
                                      ALU.min).then_inc(s_ev, 1)

                for w in range(WT):
                    q = w % 2
                    dve.wait_ge(s_slots[w], 16 * BW)
                    dve.tensor_scalar(lo_i[:, w, :, :], code[:, w, :, :], P - 1, None, ALU.bitwise_and).then_inc(s_lo_i, 1)
                    step.later(dve.tensor_scalar(hi[:, w, :, :], code[:, w, :, :], 7, (1 << CODE - 7) - 1, ALU.arith_shift_right, ALU.bitwise_and))
                    step(dve.tensor_scalar(slot_dst[:, w, :, :], code[:, w, :, :], CODE, None, ALU.arith_shift_right))
                    if w >= 2:
                        dve.wait_ge(s_no_dst, w - 1)
                    dve.tensor_tensor(dl[:, q, :, :], slot_dst[:, w, :, :], first[:, w, :].unsqueeze(2).to_broadcast([P, BW, SLOTS]),
                                      ALU.subtract).then_inc(s_dl, 1)
                    dve.wait_ge(s_dl, w + 1)
                    if w >= 2:
                        dve.wait_ge(s_key_t, w - 1)
                    step(dve.scalar_tensor_tensor(out=key[:, q, :, :], in0=hi[:, w, :, :], scalar=float(BD), in1=dl[:, q, :, :],
                                                  op0=ALU.mult, op1=ALU.add))
                    for j in range(BW):
                        for d in range(BD):
                            step.later(dve.tensor_scalar(hit[:, q, j * BD + d, :], dl[:, q, j, :], float(d), 0.0, ALU.is_equal, ALU.add,
                                                         accum_out=deg[:, w, j * BD + d:j * BD + d + 1]))
                    dve.wait_ge(s_no_dst, w + 1)
                    dve.tensor_tensor(key[:, q, :, :], key[:, q, :, :], no_dst[:, q, :, :], ALU.add).then_inc(s_keys, 1)
                    if w >= 1:
                        copy_keys(w - 1)
                step.settle()
                dve.sem_inc(s_deg, 1)
                step(dve.reduce_sum(sums[:, 0:1], deg[:].rearrange("p w d -> p (w d)"), AX.X))
                step(dve.tensor_scalar(over[:], deg[:].rearrange("p w d -> p (w d)"), 255.0, 0.0, ALU.is_gt, ALU.add,
                                       accum_out=sums[:, 1:2]))
                dve.sem_inc(s_sums, 1)
                copy_keys(WT - 1)
                dve.wait_ge(s_total, 1)
                step(dve.tensor_scalar(bad[:], head_sums[:, 0:1], float(E + NBLK * BD), None, ALU.not_equal))
                step(dve.tensor_tensor(bad[:], bad[:], head_sums[:, 1:2], ALU.add))
                step(dve.tensor_scalar(m.flags[:, BAD:BAD + 1], bad[:], 0.0, None, ALU.is_gt))
                step(dve.tensor_scalar(m.flags[:, GOOD:GOOD + 1], bad[:], 0.0, None, ALU.is_equal))

            @block.tensor
            def _(pe):
                pe.wait_ge(s_const, 5 + WT)
                pe.wait_ge(s_diag, 1)
                diag = head_diag[:].rearrange("p r c -> p (r c)")
                for a in range(0, ROWS * P, 512):
                    end = min(a + 512, ROWS * P)
                    last = pe.matmul(head_sums[:, a:end], ones16[:], diag[:, a:end], start=True, stop=True)
                last.then_inc(s_heads, 1)
                for w in range(WT):
                    pe.wait_ge(s_lo, w + 1)
                    if w >= 2:
                        pe.wait_ge(s_ev2, w - 1)
                    for j in range(BW):
                        last = pe.transpose(lt[w % 2][:, j * P:(j + 1) * P], lo[:, w % 2, j, :], m.ident[:])
                    last.then_inc(s_lo_t, 1)
                    pe.wait_ge(s_keys, w + 1)
                    if w >= 2:
                        pe.wait_ge(s_ev, w - 1)
                    for j in range(BW):
                        last = pe.transpose(pt[w % 2][:, j * P:(j + 1) * P], key[:, w % 2, j, :], m.ident[:])
                    last.then_inc(s_key_t, 1)
                pe.wait_ge(s_sums, 1)
                pe.matmul(head_sums[:, 0:2], m.ones[:], sums[:], start=True, stop=True).then_inc(s_total, 1)


def block_columns(t, w):
    return t[:, w * P * BW:(w + 1) * P * BW].rearrange("p (b j) -> p j b", j=BW)


class Semaphores:

    def __init__(self, nc):
        self.nc, self.live = nc, []

    def __call__(self, name):
        self.live.append(self.nc.alloc_semaphore(f"{name}_{len(self.live)}"))
        return self.live[-1]

    def renew(self):
        self.nc.clear_and_free_semaphores(self.live)
        self.nc.all_engine_barrier()
        self.live = []


def wait(engine, sem, value):
    if not isinstance(value, int) or value > 0:
        engine.wait_ge(sem, value)


def for_tiles(engine, body, total, unroll, first=None):
    first = unroll if first is None else first
    rounds = (total - first) // unroll
    for t in range(first):
        body(t, t % unroll)
    if rounds:
        with engine.Fori(0, rounds) as i:
            for k in range(unroll):
                body(first + k + i * unroll, (first + k) % unroll)
    for t in range(first + rounds * unroll, total):
        body(t, t % unroll)


def dis_stage(nc, m):
    with ExitStack() as ctx:
        deg = ctx.enter_context(nc.sbuf_tensor("deg_rows", [NT, P], F32))
        root = ctx.enter_context(nc.sbuf_tensor("deg_root", [NT, P], F32))
        pt = ctx.enter_context(nc.psum_tensor("dis_ps", [P, NT], F32))
        s_in, s_root, s_inv, s_t, s_done = (m.sem(n) for n in
                                            ("deg_in", "root_ready", "dis_ready", "dis_transposed", "dis_done"))
        with nc.Block() as block:
            @block.sync
            def _(sp):
                sp.dma_start(deg[:], m.deg[0:NPAD].rearrange("(t p) -> t p", p=P)).then_inc(s_in, 16)

            @block.scalar
            def _(act):
                act.wait_ge(s_in, 16)
                act.activation(root[:], deg[:], ACT.Sqrt).then_inc(s_root, 1)

            @block.vector
            def _(dve):
                dve.wait_ge(s_root, 1)
                dve.reciprocal(deg[:], root[:]).then_inc(s_inv, 1)
                dve.wait_ge(s_t, 1)
                dve.tensor_copy(m.dis[:], pt[:]).then_inc(s_done, 1)

            @block.tensor
            def _(pe):
                pe.wait_ge(s_inv, 1)
                pe.transpose(pt[:], deg[:], m.ident[0:NT, 0:NT]).then_inc(s_t, 1)


def project_pe(pe, t, r, m, s, w):
    pe.wait_ge(s.lhs, t + 1)
    wait(pe, s.hf, t - 1)
    for k in range(2):
        last = pe.matmul(s.hp_ps[r % 2][:, 0:D], s.lhs_t[r % 2][:, k, :], w[:, k, :], start=(k == 0), stop=(k == 1))
    last.then_inc(s.h, 1)


def project_scale(act, t, r, m, s):
    act.wait_ge(s.h, t + 1)
    wait(act, s.split, t - 1)
    act.activation(s.hf_t[r % 2][:], s.hp_ps[r % 2][:, 0:D], ACT.Copy, scale=m.dis[:, bass.ds(t, 1)]).then_inc(s.hf, 1)


def project_hi(dve, t, r, m, s):
    dve.wait_ge(s.hf, t + 1)
    dve.tensor_copy(m.h[:, bass.ds(t, 1), 0, :], s.hf_t[r % 2][:].unsqueeze(1)).then_inc(s.hi, 1)


def project_lo(dve, t, r, m, s):
    dve.wait_ge(s.hi, t + 1)
    dve.tensor_tensor(m.h[:, bass.ds(t, 1), 1, :], s.hf_t[r % 2][:].unsqueeze(1), m.h[:, bass.ds(t, 1), 0, :].bitcast(F32),
                      ALU.subtract).then_inc(s.split, 1)


def project_buffers(ctx, nc, m, tag):
    def sem(name):
        return m.sem(f"{name}{tag}")

    s = Names()
    s.lhs_t = [ctx.enter_context(nc.sbuf_tensor(f"lhs{tag}{i}", [P, 2, P], F32)) for i in range(2)]
    s.hf_t = [ctx.enter_context(nc.sbuf_tensor(f"hf{tag}{i}", [P, D], F32)) for i in range(2)]
    s.hp_ps = [ctx.enter_context(nc.psum_tensor(f"h_ps{tag}{i}", [P, 512], F32)) for i in range(2)]
    s.lhs = sem("lhs_ready")
    s.h = sem("h_ready")
    s.hf = sem("hf_ready")
    s.hi = sem("hi_ready")
    s.split = sem("h_split")
    return s


def input_stage(nc, m, x, w0):
    RING = 4
    with ExitStack() as ctx:
        sem = m.sem

        def sb(name, shape, n):
            return [ctx.enter_context(nc.sbuf_tensor(f"{name}{i}", shape, F32)) for i in range(n)]

        s = project_buffers(ctx, nc, m, "0")
        xs = sb("x_rows", [P, D], RING)
        w = ctx.enter_context(nc.sbuf_tensor("w0_sb", [P, 2, D], F32))
        st, mv, root, rstd = sb("ln0_stats", [P, 6], 2), sb("ln0_mv", [P, 2], 2), sb("ln0_root", [P, 1], 2), sb("ln0_rstd", [P, 1], 2)
        pt = [ctx.enter_context(nc.psum_tensor(f"xt_ps{i}", [P, 512], F32)) for i in range(2)]
        s_x = [sem(f"x_in{i}") for i in range(RING)]
        s_w, s_st, s_mv, s_root, s_rstd, s_xn, s_tr, s_zero, s_seen = (sem(n) for n in (
            "w0_in", "ln0_stats_ready", "ln0_mv_ready", "ln0_root_ready", "ln0_rstd_ready", "xn_ready", "xt_ready", "x_tail_zeroed", "ln0_stats_seen"))

        def steps(engine, body):
            for t in range(8):
                body(t, t % RING, t // RING)
            with engine.Fori(0, 9) as i:
                for k in range(4):
                    body(i * 4 + (8 + k), k, i + 2)
            for t in range(44, NT + 4):
                body(t, t % RING, t // RING)

        def has(t, lag):
            return not isinstance(t, int) or 0 <= t - lag < NT

        with nc.Block() as block:
            @block.sync
            def _(sp):
                x_bytes = x.rearrange("n d -> (n d)").bitcast(U8)

                def load(t, r):
                    if isinstance(t, int) and t == NT - 1:
                        sp.wait_ge(s_zero, 1)
                        sp.dma_start(xs[r][0:LAST, :], x[(NT - 1) * P:N, :]).then_inc(s_x[r], 16)
                    else:
                        at = tile_at(sp, x_bytes, t, D, F32)
                        wait(sp, s_tr, t - RING + 1)
                        sp.dma_start(xs[r][:], at).then_inc(s_x[r], 16)

                for t in range(3):
                    load(t, t)
                sp.dma_start(w[:], w0.rearrange("(k p) n -> p k n", p=P)).then_inc(s_w, 16)
                steps(sp, lambda t, r, u: load(t + 3, (r + 3) % RING) if has(t, -3) else None)

            @block.vector
            def _(dve):
                def step(t, r, u):
                    q, p = r % 2, (r + 1) % 2
                    if has(t, 1):
                        dve.wait_ge(s_root, t)
                        dve.reciprocal(rstd[p][:], root[p][:]).then_inc(s_rstd, 1)
                    if has(t, 0):
                        dve.wait_ge(s_x[r], 16 * (u + 1))
                        wait(dve, s_mv, t - 1)
                        dve.bn_stats(st[q][:], xs[r][:]).then_inc(s_st, 1)
                    if has(t, 1):
                        o = (r + 3) % RING
                        dve.wait_ge(s_rstd, t)
                        dve.tensor_scalar(xs[o][:], xs[o][:], mv[p][:, 0:1], rstd[p][:], ALU.subtract, ALU.mult).then_inc(s_xn, 1)
                    if has(t, 4):
                        project_hi(dve, t - 4, r, m, s)
                    if has(t, 0):
                        dve.wait_ge(s_st, t + 1)
                        wait(dve, s_root, t - 1)
                        wait(dve, s_xn, t - 1)
                        dve.sem_inc(s_seen, 1)
                        dve.bn_aggr(mv[q][:], st[q][:]).then_inc(s_mv, 1)
                    if has(t, 4):
                        project_lo(dve, t - 4, r, m, s)
                    if isinstance(t, int) and t == NT - 4:
                        dve.wait_ge(s_tr, NT - 4)
                        dve.memset(xs[(NT - 1) % RING][96:P, :], 0.0).then_inc(s_zero, 1)

                steps(dve, step)

            @block.tensor
            def _(pe):
                pe.wait_ge(s_w, 16)

                def step(t, r, u):
                    if has(t, 1):
                        p, o = (r + 1) % 2, (r + 3) % RING
                        pe.wait_ge(s_xn, t)
                        wait(pe, s.lhs, t - 2)
                        for c in range(2):
                            last = pe.transpose(pt[p][:, c * P:(c + 1) * P], xs[o][:, c * P:(c + 1) * P], m.ident[:])
                        last.then_inc(s_tr, 1)
                    if has(t, 2):
                        project_pe(pe, t - 2, r, m, s, w)

                steps(pe, step)

            @block.scalar
            def _(act):
                def step(t, r, u):
                    if has(t, 2):
                        act.wait_ge(s_tr, t - 1)
                        wait(act, s.h, t - 3)
                        act.activation(s.lhs_t[r % 2][:].rearrange("p k n -> p (k n)"), pt[r % 2][:, 0:D], ACT.Copy).then_inc(s.lhs, 1)
                    if has(t, 3):
                        project_scale(act, t - 3, r + 1, m, s)
                    if has(t, 0):
                        act.wait_ge(s_mv, t + 1)
                        wait(act, s_rstd, t - 1)
                        act.activation(root[r % 2][:], mv[r % 2][:, 1:2], ACT.Sqrt, bias=m.eps[:, 0:1]).then_inc(s_root, 1)

                steps(act, step)


def tail_buffers(ctx, nc, m, tag, bias):
    def sem(name):
        return m.sem(f"{name}{tag}")

    s = Names()
    s.sum_ps = [ctx.enter_context(nc.psum_tensor(f"sum_ps{tag}{i}", [P, 512], F32)) for i in range(2)]
    s.zt_ps = [ctx.enter_context(nc.psum_tensor(f"zt_ps{tag}{i}", [P, 512], F32)) for i in range(2)]
    s.low_t = [ctx.enter_context(nc.sbuf_tensor(f"low{tag}{i}", [P, D], F32)) for i in range(2)]
    s.z_t = [ctx.enter_context(nc.sbuf_tensor(f"z{tag}{i}", [P, D], F32)) for i in range(2)]
    s.zt_t = [ctx.enter_context(nc.sbuf_tensor(f"zt{tag}{i}", [P, 2, P], F32)) for i in range(2)]
    s.bias = bias
    s.sum = sem("sum_ready")
    s.low = sem("low_scaled")
    s.z = sem("z_ready")
    s.tr = sem("z_transposed")
    s.relu = sem("z_relu")
    s.stats = sem("z_stats_ready")
    s.store = [sem(f"z_stored{i}_") for i in range(2)]
    return s


def tail_low(act, t, r, m, s):
    act.wait_ge(s.sum, t + 1)
    wait(act, s.z, t - 1)
    act.activation(s.low_t[r][:], s.sum_ps[r][:, D:2 * D], ACT.Copy, scale=m.dis[:, bass.ds(t, 1)]).then_inc(s.low, 1)


def tail_add(dve, t, r, m, s):
    dve.wait_ge(s.low, t + 1)
    wait(dve, s.tr, t - 1)
    dve.scalar_tensor_tensor(out=s.z_t[r][:], in0=s.sum_ps[r][:, 0:D], scalar=m.dis[:, bass.ds(t, 1)], in1=s.low_t[r][:],
                             op0=ALU.mult, op1=ALU.add).then_inc(s.z, 1)


def tail_transpose(pe, t, r, m, s):
    pe.wait_ge(s.z, t + 1)
    wait(pe, s.relu, 2 * (t - 1))
    for c in range(2):
        last = pe.transpose(s.zt_ps[r][:, c * P:(c + 1) * P], s.z_t[r][:, c * P:(c + 1) * P], m.ident[:])
    last.then_inc(s.tr, 1)


def tail_relu(act, t, r, u, m, s):
    act.wait_ge(s.tr, t + 1)
    wait(act, s.stats, 2 * (t - 1))
    wait(act, s.store[r], 16 * u)
    for c in range(2):
        act.activation(s.zt_t[r][:, c, :], s.zt_ps[r][:, c * P:(c + 1) * P], ACT.Relu, bias=s.bias[:, c:c + 1]).then_inc(s.relu, 1)


def tail_stats(dve, t, r, m, s, n=P):
    dve.wait_ge(s.relu, 2 * (t + 1))
    for c in range(2):
        out = m.stats[:, c, t * 6:(t + 1) * 6] if isinstance(t, int) else m.stats[:, c, bass.ds(t * 6, 6)]
        dve.bn_stats(out, s.zt_t[r][:, c, 0:n]).then_inc(s.stats, 1)


def tile_at(engine, store, t, width, dt):
    size = P * width * (1 if dt == U8 else 4)
    at = t * size if isinstance(t, int) else engine.snap(engine.to_reg(t * size), min_val=0, max_val=store.shape[0] - size)
    flat = store[bass.ds(at, size)]
    return (flat if dt == U8 else flat.bitcast(dt)).rearrange("(p n) -> p n", p=P)


def before_wait(engine, value):
    return value if isinstance(value, int) else engine.snap(engine.to_reg(value), min_val=0, max_val=1 << 20)


def tail_store(sp, t, r, m, s):
    at = tile_at(sp, m.zT, t, D, F32)
    sp.wait_ge(s.relu, 2 * (t + 1))
    sp.dma_start(at, s.zt_t[r][:].rearrange("p c n -> p (c n)")).then_inc(s.store[r], 16)


def tail_stored(sp, s):
    for r in range(2):
        sp.wait_ge(s.store[r], 16 * ((NT + 1 - r) // 2))


def build_stage(nc, m):
    RING = 2
    AHEAD = 4
    ROUND = MT // 6
    BY_VECTOR = (2, 4, 6)
    with ExitStack() as ctx:
        sem = m.sem

        s = tail_buffers(ctx, nc, m, "_b", m.b0)
        key1 = [ctx.enter_context(nc.sbuf_tensor(f"key_onehot{i}", [P, 2, KEYS, 4], BF16)) for i in range(AHEAD)]
        lo1 = [ctx.enter_context(nc.sbuf_tensor(f"lo_onehot{i}", [P, 2, P, 4], BF16)) for i in range(AHEAD)]
        counts = [ctx.enter_context(nc.sbuf_tensor(f"counts{i}", [P, NT, P], F32R)) for i in range(2)]
        bytes_ = [ctx.enter_context(nc.sbuf_tensor(f"count_bytes{i}", [P, NT, P], U8)) for i in range(2)]
        zero = ctx.enter_context(nc.sbuf_tensor("zero_row", [P, D], F32))
        group_ps = [ctx.enter_context(nc.psum_tensor(f"group_ps{i}", [P, 8, P], F32)) for i in range(RING)]
        s_one, s_group, s_ev, s_byte, s_byte_v = (sem(n) for n in (
            "onehots_ready", "group_ready", "group_copied", "bytes_by_scalar", "bytes_by_vector"))
        s_bst = [sem(f"bytes_stored{i}") for i in range(2)]
        s_zero, s_zeroed = sem("zero_set"), sem("slots_zeroed")
        by_scalar = GROUPS - len(BY_VECTOR)

        def steps(engine, body):
            for t in range(4):
                body(t, t % 2, t // 2, True, t >= 1, t >= 2)
            with engine.Fori(0, (NT - 4) // 2) as i:
                for k in range(2):
                    body(i * 2 + (4 + k), k, i + 2, True, True, True)
            body(NT - 1, (NT - 1) % 2, (NT - 1) // 2, True, True, True)
            body(NT, NT % 2, NT // 2, False, True, True)
            body(NT + 1, (NT + 1) % 2, (NT + 1) // 2, False, False, True)

        def eighth(q):
            return q * 6, (q + 1) * 6 if q < GROUPS - 1 else NT

        def one_hots(dve, out, width, column):
            dve.tensor_tensor(out[:], m.iota4[:, 0:width, :].unsqueeze(1).to_broadcast([P, 2, width, 4]),
                              column.rearrange("p (g c) -> p g c", g=2).unsqueeze(2).to_broadcast([P, 2, width, 4]),
                              ALU.is_equal).then_inc(s_one, 1)

        with nc.Block() as block:
            @block.vector
            def _(dve):
                with when(dve, m, GOOD):
                    def step(t, r, u, build, prod, tail):
                        for q in range(GROUPS):
                            if build:
                                wait(dve, s_group, t * GROUPS + (q - AHEAD + 1))
                                blocks = slice(t * UNITS + q * 8, t * UNITS + q * 8 + 8) if isinstance(t, int) else bass.ds(t * UNITS + q * 8, 8)
                                one_hots(dve, key1[q % AHEAD], KEYS, m.keyT[:, blocks])
                                one_hots(dve, lo1[q % AHEAD], P, m.loT[:, blocks])
                            if prod and q in BY_VECTOR:
                                if q == BY_VECTOR[0]:
                                    dve.wait_ge(s_ev, t * GROUPS)
                                    wait(dve, s_bst[1 - r], 16 * (u + (r - 1)))
                                first, end = eighth(q)
                                dve.tensor_copy(bytes_[1 - r][:, first:end, :], counts[1 - r][:, first:end, :].bitcast(F32)).then_inc(s_byte_v, 1)
                            if tail and q == 1:
                                tail_add(dve, t - 2, r, m, s)
                            if tail and q == 5:
                                tail_stats(dve, t - 2, r, m, s, LAST if isinstance(t, int) and t - 2 == NT - 1 else P)

                    steps(dve, step)

            @block.tensor
            def _(pe):
                with when(pe, m, GOOD):
                    def step(t, r, u, build, prod, tail):
                        for q in range(GROUPS):
                            if build:
                                pe.wait_ge(s_one, t * (2 * GROUPS) + 2 * (q + 1))
                                wait(pe, s_ev, t * GROUPS + (q - RING + 1))
                                for g in range(2):
                                    for c in range(4):
                                        last = pe.matmul(group_ps[q % RING][:, 4 * g + c, 0:KEYS], lo1[q % AHEAD][:, g, :, c],
                                                         key1[q % AHEAD][:, g, :, c], start=True, stop=True)
                                last.then_inc(s_group, 1)
                            if prod:
                                first, end = eighth(q)
                                if q == 0:
                                    pe.wait_ge(s_ev, t * GROUPS)
                                    wait(pe, s.z, t - 2)
                                for h in range(first, end):
                                    last = pe.matmul(s.sum_ps[1 - r][:], counts[1 - r][:, h, :], m.h[:, h, :, :].rearrange("p a d -> p (a d)"),
                                                     start=(h == 0), stop=(h == NT - 1))
                                if end == NT:
                                    last.then_inc(s.sum, 1)
                            if tail and q == 3:
                                tail_transpose(pe, t - 2, r, m, s)

                    steps(pe, step)

            @block.scalar
            def _(act):
                with when(act, m, GOOD):
                    def step(t, r, u, build, prod, tail):
                        for q in range(GROUPS):
                            if tail and q == 0:
                                tail_low(act, t - 2, r, m, s)
                            if build:
                                if q == 0:
                                    wait(act, s.sum, t - 1)
                                    wait(act, s_byte, (t - 1) * by_scalar)
                                    wait(act, s_byte_v, (t - 1) * len(BY_VECTOR))
                                act.wait_ge(s_group, t * GROUPS + (q + 1))
                                act.activation(counts[r][:, :, q * 16:(q + 1) * 16].rearrange("p h (v d) -> p h v d", d=BD),
                                               group_ps[q % RING][:, :, 0:KEYS].rearrange("p v (h d) -> p h v d", d=BD),
                                               ACT.Copy).then_inc(s_ev, 1)
                            if prod and q not in BY_VECTOR:
                                if q == 0:
                                    act.wait_ge(s_ev, t * GROUPS)
                                    wait(act, s_bst[1 - r], 16 * (u + (r - 1)))
                                first, end = eighth(q)
                                act.activation(bytes_[1 - r][:, first:end, :], counts[1 - r][:, first:end, :].bitcast(F32),
                                               ACT.Copy).then_inc(s_byte, 1)
                            if tail and q == 4:
                                tail_relu(act, t - 2, r, u - 1, m, s)

                    steps(act, step)

            @block.sync
            def _(sp):
                with when(sp, m, GOOD):
                    def step(t, r, u, build, prod, tail):
                        if tail:
                            tail_store(sp, t - 2, r, m, s)
                        if prod:
                            at, done = tile_at(sp, m.counts, t - 1, NPAD, U8), before_wait(sp, t * by_scalar)
                            sp.wait_ge(s_byte_v, t * len(BY_VECTOR))
                            sp.wait_ge(s_byte, done)
                            sp.dma_start(at, bytes_[1 - r][:].rearrange("p h n -> p (h n)")).then_inc(s_bst[1 - r], 16)

                    steps(sp, step)
                    tail_stored(sp, s)
                    for r in range(2):
                        sp.wait_ge(s_bst[r], 16 * ((NT + 1 - r) // 2))

            @block.gpsimd
            def _(pool):
                pool.memset(zero[:], 0.0).then_inc(s_zero, 1)
                pool.wait_ge(s_zero, 1)
                for g in range(MT // ROUND):
                    pool.dma_start(m.rows[g * ROUND * P:(g + 1) * ROUND * P, :].rearrange("(p n) d -> p n d", p=P),
                                   zero[:].unsqueeze(1).to_broadcast([P, ROUND, D])).then_inc(s_zeroed, 16)
                pool.wait_ge(s_zeroed, 16 * (MT // ROUND))


@contextmanager
def when(engine, m, flag):
    value = engine.value_load(m.flags[0:1, flag:flag + 1], min_val=0, max_val=1)
    with engine.If(value):
        yield


def any_degrees(nc, m):
    RING = 4
    with ExitStack() as ctx:
        def sb(name, shape, dt):
            return ctx.enter_context(nc.sbuf_tensor(name, shape, dt))

        code, part_i = sb("any_codes", [P, CH], I32), sb("any_dst_part", [P, CH], I32)
        lo, hi = sb("any_lo", [P, CH], F32), sb("any_hi", [P, CH], F32)
        lo1 = [sb(f"any_lo_onehot{i}", [P, P], BF16) for i in range(RING)]
        hi1 = [sb(f"any_hi_onehot{i}", [P, NT], BF16) for i in range(RING)]
        root = sb("any_root", [P, NT], F32)
        total = ctx.enter_context(nc.psum_tensor("any_degree_ps", [P, NT], F32))
        s_in, s_step, s_one, s_used, s_root, s_dis = (m.sem(n) for n in (
            "any_dst_in", "any_degree_step", "any_onehots_ready", "any_onehots_used", "any_root_ready", "any_dis_ready"))
        with nc.Block() as block:
            @block.sync
            def _(sp):
                with when(sp, m, BAD):
                    sp.dma_start(code[:], m.codes.rearrange("(p c) -> p c", p=P)).then_inc(s_in, 16)

            @block.vector
            def _(dve):
                with when(dve, m, BAD):
                    step = Chain(dve, s_step)
                    dve.wait_ge(s_in, 16)
                    step(dve.tensor_scalar(part_i[:], code[:], CODE, P - 1, ALU.arith_shift_right, ALU.bitwise_and))
                    step(dve.tensor_copy(lo[:], part_i[:]))
                    step(dve.tensor_scalar(part_i[:], code[:], CODE + 7, None, ALU.arith_shift_right))
                    step(dve.tensor_copy(hi[:], part_i[:]))

                    def onehots(t, r, u):
                        wait(dve, s_used, t - RING + 1)
                        dve.tensor_scalar(lo1[r][:], m.iota16[:, 0:P], lo[:, at_tile(t, 0)], None, ALU.is_equal)
                        dve.tensor_scalar(hi1[r][:], m.iota16[:, 0:NT], hi[:, at_tile(t, 0)], None, ALU.is_equal).then_inc(s_one, 1)

                    for_slots(dve, onehots, CH, RING)
                    dve.wait_ge(s_root, 1)
                    dve.reciprocal(m.dis[:], root[:]).then_inc(s_dis, 1)

            @block.tensor
            def _(pe):
                with when(pe, m, BAD):
                    def count(t, r, u):
                        pe.wait_ge(s_one, t + 1)
                        pe.matmul(total[:], lo1[r][:], hi1[r][:], start=isinstance(t, int) and t == 0,
                                  stop=isinstance(t, int) and t == CH - 1).then_inc(s_used, 1)

                    for_slots(pe, count, CH, RING)

            @block.scalar
            def _(act):
                with when(act, m, BAD):
                    act.wait_ge(s_used, CH)
                    act.activation(root[:], total[:], ACT.Sqrt, bias=m.ones[:, 0:1]).then_inc(s_root, 1)


def any_sums(nc, m, tag, bias):
    RING = 4
    with ExitStack() as ctx:
        def sb(name, shape, n, dt=F32):
            return [ctx.enter_context(nc.sbuf_tensor(f"{name}{tag}{i}", shape, dt)) for i in range(n)]

        def sem(name):
            return m.sem(f"{name}{tag}")

        s = tail_buffers(ctx, nc, m, tag, bias)
        edges = sb("any_edges", [P, CH], 2, I32)
        row = sb("any_h_row", [P, D], 2)
        src_now, dst_now, dst_f = sb("any_src_now", [P, 1], RING, I32), sb("any_dst_now", [P, 1], RING, I32), sb("any_dst_f", [P, 1], RING)
        diag, equal = sb("any_diag", [P, P], 2), sb("any_equal", [P, P], 2)
        h_rows, sums, new = sb("any_h_rows", [P, D], RING), sb("any_sums", [P, D], RING), sb("any_new", [P, D], RING)
        final = sb("any_final", [P, D], 2)
        dst_ps = [ctx.enter_context(nc.psum_tensor(f"any_dst_ps{tag}{i}", [P, 512], F32)) for i in range(2)]
        part_ps = s.sum_ps
        s_edges, s_split, s_row, s_now, s_diag, s_dst, s_equal, s_part, s_new, s_seen, s_seen2 = (sem(n) for n in (
            "any_edges_in", "any_edges_split", "any_row_ready", "any_now_ready", "any_diag_ready", "any_dst_rows_ready", "any_equal_ready",
            "any_part_ready", "any_new_ready", "any_rows_may_load", "any_sums_may_load"))
        s_stored = [sem(f"any_row_stored{i}_") for i in range(2)]
        s_h, s_old, s_sent = ([sem(f"{n}{i}_") for i in range(RING)] for n in ("any_h_rows_in", "any_sums_in", "any_sums_stored"))
        s_final = [sem(f"any_final_in{i}_") for i in range(2)]
        h_at, sum_at = m.any_h.rearrange("(n d) -> n d", d=4 * D).bitcast(F32), m.any_sum.rearrange("(n d) -> n d", d=4 * D).bitcast(F32)

        with nc.Block() as block:
            @block.sync
            def _(sp):
                with when(sp, m, BAD):
                    sp.dma_start(edges[0][:], m.codes.rearrange("(p c) -> p c", p=P)).then_inc(s_edges, 16)

                    def store(t, r, u):
                        h_to, sum_to = tile_at(sp, m.any_h, t, D, F32), tile_at(sp, m.any_sum, t, D, F32)
                        sp.wait_ge(s_row, t + 1)
                        sp.dma_start(h_to, row[r][:]).then_inc(s_stored[r], 16)
                        sp.dma_start(sum_to, row[r][:]).then_inc(s_stored[r], 16)

                    for_slots(sp, store, NT + 1, 2)

                    def load(t, r, u):
                        at = tile_at(sp, m.any_sum, t, D, F32)
                        wait(sp, s.z, t - 1)
                        sp.dma_start(final[r][:], at).then_inc(s_final[r], 16)
                        if not isinstance(t, int) or t >= 1:
                            tail_store(sp, t - 1, 1 - r, m, s)

                    for r in range(RING):
                        sp.wait_ge(s_sent[r], 16 * ((CH + RING - 1 - r) // RING))
                    for_slots(sp, load, NT, 2)
                    tail_store(sp, NT - 1, (NT - 1) % 2, m, s)
                    tail_stored(sp, s)

            @block.vector
            def _(dve):
                with when(dve, m, BAD):
                    def whole(t, r, u):
                        wait(dve, s_stored[r], 32 * u)
                        dve.tensor_tensor(row[r][:].unsqueeze(1), m.h[:, at_tile(t, 0), 0, :].bitcast(F32),
                                          m.h[:, at_tile(t, 0), 1, :].bitcast(F32), ALU.add).then_inc(s_row, 1)

                    for_slots(dve, whole, NT, 2)
                    dve.wait_ge(s_stored[NT % 2], 32 * (NT // 2))
                    dve.memset(row[NT % 2][:], 0.0).then_inc(s_row, 1)
                    dve.wait_ge(s_edges, 16)
                    dve.tensor_scalar(edges[1][:], edges[0][:], CODE, None, ALU.arith_shift_right).then_inc(s_split, 1)
                    dve.wait_ge(s_split, 1)
                    dve.tensor_scalar(edges[0][:], edges[0][:], (1 << CODE) - 1, None, ALU.bitwise_and).then_inc(s_split, 1)
                    dve.wait_ge(s_split, 2)

                    def now(t, r, u):
                        wait(dve, s_sent[r], 16 * u)
                        dve.tensor_copy(src_now[r][:], edges[0][:, at_tile(t, 0)]).then_inc(s_now, 1)
                        dve.tensor_scalar(dst_now[r][:], edges[1][:, at_tile(t, 0)], float(NPAD), None, ALU.min).then_inc(s_now, 1)
                        dve.tensor_scalar(dst_f[r][:], edges[1][:, at_tile(t, 0)], float(NPAD), None, ALU.min).then_inc(s_now, 1)
                        dve.wait_ge(s_now, 3 * (t + 1))
                        wait(dve, s_dst, t - 1)
                        dve.tensor_scalar(diag[r % 2][:], m.ident[:], dst_f[r][:], None, ALU.mult).then_inc(s_diag, 1)

                    def add(t, r, u):
                        now(t, r, u)
                        dve.wait_ge(s_dst, t + 1)
                        wait(dve, s_part, t - 1)
                        dve.tensor_scalar(equal[r % 2][:], dst_ps[r % 2][:, 0:P], dst_f[r][:], None, ALU.is_equal).then_inc(s_equal, 1)
                        dve.wait_ge(s_part, t + 1)
                        dve.wait_ge(s_old[r], 16 * (u + 1))
                        dve.tensor_tensor(new[r][:], sums[r][:], part_ps[r % 2][:, 0:D], ALU.add).then_inc(s_new, 1)

                    for_slots(dve, add, CH, RING)

                    def scale(t, r, u):
                        dve.wait_ge(s_final[r], 16 * (u + 1))
                        wait(dve, s.tr, t - 1)
                        dve.tensor_scalar(s.z_t[r][:], final[r][:], m.dis[:, at_tile(t, 0)], None, ALU.mult).then_inc(s.z, 1)
                        if not isinstance(t, int) or t >= 1:
                            tail_stats(dve, t - 1, 1 - r, m, s)

                    for_slots(dve, scale, NT, 2)
                    tail_stats(dve, NT - 1, (NT - 1) % 2, m, s, LAST)

            @block.tensor
            def _(pe):
                with when(pe, m, BAD):
                    def add(t, r, u):
                        pe.wait_ge(s_diag, t + 1)
                        wait(pe, s_equal, t - 1)
                        pe.matmul(dst_ps[r % 2][:, 0:P], m.ones[:], diag[r % 2][:], start=True, stop=True).then_inc(s_dst, 1)
                        pe.wait_ge(s_equal, t + 1)
                        pe.wait_ge(s_h[r], 16 * (u + 1))
                        wait(pe, s_new, t - 1)
                        pe.matmul(part_ps[r % 2][:, 0:D], equal[r % 2][:], h_rows[r][:], start=True, stop=True).then_inc(s_part, 1)

                    for_slots(pe, add, CH, RING)
                    for_slots(pe, lambda t, r, u: tail_transpose(pe, t, r, m, s), NT, 2)

            @block.scalar
            def _(act):
                with when(act, m, BAD):
                    for_slots(act, lambda t, r, u: tail_relu(act, t, r, u, m, s), NT, 2)

            @block.gpsimd
            def _(pool):
                with when(pool, m, BAD):
                    for r in range(2):
                        pool.wait_ge(s_stored[r], 32 * ((NT + 2 - r) // 2))

                    def add(t, r, u):
                        pool.wait_ge(s_now, 3 * (t + 1))
                        wait(pool, s_part, t - RING + 1)
                        wait(pool, s_sent[(r + 3) % RING], 16 * (u + 1 if r > 0 else u))
                        wait(pool, s_new, t - RING + 1)
                        pool.sem_inc(s_seen, 1)
                        pool.indirect_dma_start(out=sums[r][:], out_offset=None, in_=sum_at,
                                                in_offset=bass.IndirectOffsetOnAxis(ap=dst_now[r][:], axis=0)).then_inc(s_old[r], 16)
                        pool.indirect_dma_start(out=h_rows[r][:], out_offset=None, in_=h_at,
                                                in_offset=bass.IndirectOffsetOnAxis(ap=src_now[r][:], axis=0)).then_inc(s_h[r], 16)
                        pool.wait_ge(s_new, t + 1)
                        pool.sem_inc(s_seen2, 1)
                        pool.indirect_dma_start(out=sum_at, out_offset=bass.IndirectOffsetOnAxis(ap=dst_now[r][:], axis=0),
                                                in_=new[r][:], in_offset=None).then_inc(s_sent[r], 16)

                    for_slots(pool, add, CH, RING)


def norm_stage(nc, m, tag, gain, shift):
    with ExitStack() as ctx:
        mv = ctx.enter_context(nc.sbuf_tensor("bn_mv" + tag, [P, 2, 2], F32))
        root = ctx.enter_context(nc.sbuf_tensor("bn_root" + tag, [P, 2], F32))
        inv = ctx.enter_context(nc.sbuf_tensor("bn_inv" + tag, [P, 2], F32))
        off = ctx.enter_context(nc.sbuf_tensor("bn_off" + tag, [P, 2], F32))
        s_mv, s_root, s_dve = (m.sem(n + tag) for n in ("bn_mv_ready", "bn_root_ready", "bn_step"))
        with nc.Block() as block:
            @block.vector
            def _(dve):
                for c in range(2):
                    last = dve.bn_aggr(mv[:, c, :], m.stats[:, c, :])
                last.then_inc(s_mv, 1)
                dve.wait_ge(s_root, 1)
                step = Chain(dve, s_dve)
                step(dve.reciprocal(inv[:], root[:]))
                step(dve.tensor_tensor(m.scale[:], inv[:], gain[:], ALU.mult))
                step(dve.tensor_tensor(off[:], mv[:, :, 0], m.scale[:], ALU.mult))
                step(dve.tensor_tensor(m.offset[:], shift[:], off[:], ALU.subtract))

            @block.scalar
            def _(act):
                act.wait_ge(s_mv, 1)
                act.activation(root[:], mv[:, :, 1], ACT.Sqrt, bias=m.eps[:, 0:1]).then_inc(s_root, 1)


def load_zt(sp, t, r, u, m, zt, s_in, s_free, free):
    at = tile_at(sp, m.zT, t, D, F32)
    wait(sp, s_free, free)
    sp.dma_start(zt[r][:].rearrange("p c n -> p (c n)"), at).then_inc(s_in[r], 16)


def project_stage(nc, m, w_dram):
    RING = 4
    with ExitStack() as ctx:
        s = project_buffers(ctx, nc, m, "1")
        zt = [ctx.enter_context(nc.sbuf_tensor(f"zt_in{i}", [P, 2, P], F32)) for i in range(RING)]
        w = ctx.enter_context(nc.sbuf_tensor("w1_sb", [P, 2, D], F32))
        s_in = [m.sem(f"zt_loaded{i}") for i in range(RING)]
        s_w, s_half = m.sem("w1_in"), m.sem("lhs_half_ready")

        with nc.Block() as block:
            @block.sync
            def _(sp):
                sp.dma_start(w[:], w_dram.rearrange("(k p) n -> p k n", p=P)).then_inc(s_w, 16)
                for_slots(sp, lambda t, r, u: load_zt(sp, t, r, u, m, zt, s_in, s.h, t - RING + 1), NT, RING)

            @block.scalar
            def _(act):
                def tile(t, r, u):
                    act.wait_ge(s_in[r], 16 * (u + 1))
                    wait(act, s.h, t - 1)
                    act.activation(s.lhs_t[r % 2][:, 0, :], zt[r][:, 0, :], ACT.Identity, bias=m.offset[:, 0:1],
                                   scale=m.scale[:, 0:1]).then_inc(s.lhs, 1)
                    if not isinstance(t, int) or t > 0:
                        project_scale(act, t - 1, r + 1, m, s)

                for_slots(act, tile, NT, RING)
                project_scale(act, NT - 1, NT - 1, m, s)

            @block.tensor
            def _(pe):
                pe.wait_ge(s_w, 16)

                def tile(t, r, u):
                    pe.wait_ge(s_half, t + 1)
                    project_pe(pe, t, r, m, s, w)

                for_slots(pe, tile, NT, RING)

            @block.vector
            def _(dve):
                def half(t, r, u):
                    dve.wait_ge(s_in[r], 16 * (u + 1))
                    wait(dve, s.h, t - 1)
                    dve.tensor_scalar(s.lhs_t[r % 2][:, 1, :], zt[r][:, 1, :], m.scale[:, 1:2], m.offset[:, 1:2], ALU.mult, ALU.add).then_inc(s_half, 1)

                def tile(t, r, u):
                    if not isinstance(t, int) or t >= 2:
                        project_hi(dve, t - 2, r, m, s)
                    half(t, r, u)
                    if not isinstance(t, int) or t >= 2:
                        project_lo(dve, t - 2, r, m, s)

                for_slots(dve, tile, NT, RING)
                for t in range(NT - 2, NT):
                    project_hi(dve, t, t, m, s)
                    project_lo(dve, t, t, m, s)


def for_slots(engine, body, total, ring):
    rounds = (total - 1) // ring - 1
    for t in range(ring):
        body(t, t, 0)
    if rounds > 0:
        with engine.Fori(0, rounds) as i:
            for k in range(ring):
                body(i * ring + (ring + k), k, i + 1)
    for t in range(ring * (1 + max(rounds, 0)), total):
        body(t, t % ring, t // ring)


def product_stage(nc, m):
    SPLIT = 30
    with ExitStack() as ctx:
        sem = m.sem

        s = tail_buffers(ctx, nc, m, "_p", m.b1)
        counts = [ctx.enter_context(nc.sbuf_tensor(f"wide{i}", [P, NT, P], F32R)) for i in range(2)]
        bytes_ = [ctx.enter_context(nc.sbuf_tensor(f"bytes_in{i}", [P, NT, P], U8)) for i in range(2)]
        s_in = [sem(f"bytes_loaded{i}") for i in range(2)]
        s_v, s_a = sem("wide_by_vector"), sem("wide_by_scalar")

        def steps(engine, body):
            for t in range(4):
                body(t, t % 2, t // 2, True, t >= 1)
            with engine.Fori(0, (NT - 7) // 2) as i:
                for k in range(2):
                    body(i * 2 + (4 + k), k, i + 2, True, True)
            for t in range(NT - 3, NT):
                body(t, t % 2, t // 2, True, True)
            body(NT, NT % 2, NT // 2, False, True)

        def widen(engine, t, r, u, first, end, s_done):
            engine.wait_ge(s_in[r], 16 * (u + 1))
            wait(engine, s.sum, t - 1)
            if s_done is s_v:
                engine.tensor_copy(counts[r][:, first:end, :], bytes_[r][:, first:end, :]).then_inc(s_done, 1)
            else:
                engine.activation(counts[r][:, first:end, :], bytes_[r][:, first:end, :], ACT.Copy).then_inc(s_done, 1)

        with nc.Block() as block:
            @block.sync
            def _(sp):
                with when(sp, m, GOOD):
                    def load(t, r):
                        at = tile_at(sp, m.counts, t, NPAD, U8)
                        wait(sp, s_v, t - 1)
                        wait(sp, s_a, t - 1)
                        sp.dma_start(bytes_[r][:].rearrange("p h n -> p (h n)"), at).then_inc(s_in[r], 16)

                    def step(t, r, u, prod, tail):
                        if not isinstance(t, int) or t + 2 < NT:
                            load(t + 2, r)
                        if tail:
                            tail_store(sp, t - 1, 1 - r, m, s)

                    load(0, 0)
                    load(1, 1)
                    steps(sp, step)
                    tail_stored(sp, s)

            @block.vector
            def _(dve):
                with when(dve, m, GOOD):
                    def step(t, r, u, prod, tail):
                        if tail:
                            tail_add(dve, t - 1, 1 - r, m, s)
                        if not isinstance(t, int) or t + 1 < NT:
                            widen(dve, t + 1, 1 - r, u + r, 0, SPLIT, s_v)
                        if tail:
                            tail_stats(dve, t - 1, 1 - r, m, s, LAST if isinstance(t, int) and t - 1 == NT - 1 else P)

                    widen(dve, 0, 0, 0, 0, SPLIT, s_v)
                    steps(dve, step)

            @block.scalar
            def _(act):
                with when(act, m, GOOD):
                    def step(t, r, u, prod, tail):
                        if tail:
                            tail_low(act, t - 1, 1 - r, m, s)
                        if not isinstance(t, int) or t + 1 < NT:
                            widen(act, t + 1, 1 - r, u + r, SPLIT, NT, s_a)
                        if tail:
                            tail_relu(act, t - 1, 1 - r, u + (r - 1), m, s)

                    widen(act, 0, 0, 0, SPLIT, NT, s_a)
                    steps(act, step)

            @block.tensor
            def _(pe):
                with when(pe, m, GOOD):
                    def step(t, r, u, prod, tail):
                        if prod:
                            pe.wait_ge(s_v, t + 1)
                            wait(pe, s.z, t - 1)
                        for h in range(NT):
                            if h == 16 and tail:
                                tail_transpose(pe, t - 1, 1 - r, m, s)
                            if h == SPLIT and prod:
                                pe.wait_ge(s_a, t + 1)
                            if prod:
                                last = pe.matmul(s.sum_ps[r][:], counts[r][:, h, :], m.h[:, h, :, :].rearrange("p a d -> p (a d)"),
                                                 start=(h == 0), stop=(h == NT - 1))
                        if prod:
                            last.then_inc(s.sum, 1)

                    steps(pe, step)


def gate_stage(nc, m, x, gate_w, gate_b, beta, ew1):
    RING = 4
    with ExitStack() as ctx:
        sem = m.sem

        def sb(name, shape, dt=F32):
            return ctx.enter_context(nc.sbuf_tensor(name, shape, dt))

        def ps(name, n):
            return [ctx.enter_context(nc.psum_tensor(f"{name}{i}", [P, 512], F32)) for i in range(n)]

        zt = [sb(f"zt_gate{i}", [P, 2, P]) for i in range(RING)]
        xin = [sb(f"x_gate{i}", [P, D]) for i in range(RING)]
        zn = [sb(f"zn{i}", [P, 2, P]) for i in range(2)]
        x1 = [sb(f"x1_{i}", [P, D]) for i in range(RING)]
        xn = [sb(f"xn{i}", [P, D]) for i in range(RING)]
        x1b = [sb(f"x1_beta{i}", [P, D]) for i in range(2)]
        bet = sb("beta_sb", [P, D])
        xnT = [sb(f"xnT{i}", [P, 2, P]) for i in range(2)]
        st = [sb(f"ln1_stats{i}", [P, 6]) for i in range(2)]
        mv = [sb(f"ln1_mv{i}", [P, 2]) for i in range(2)]
        root = [sb(f"ln1_root{i}", [P, 1]) for i in range(2)]
        rstd = [sb(f"ln1_rstd{i}", [P, 1]) for i in range(2)]
        gw = sb("gate_w_sb", [P, 2, NE])
        gb = sb("gate_b_sb", [P, NE])
        zps, xps, gps = ps("z_back_ps", 2), ps("xn_t_ps", 2), ps("gate_ps", 2)
        s_zt = [sem(f"zt_gate_in{i}") for i in range(RING)]
        s_x = [sem(f"x_gate_in{i}") for i in range(RING)]
        s_x1o = [sem(f"x1_stored{i}") for i in range(2)]
        s_bet, s_seen2, s_x1b = sem("beta_in"), sem("x1_seen"), sem("x1_beta_ready")
        s_kept = sem("xn_kept")
        (s_w, s_zero, s_zn, s_zb, s_x1, s_st, s_seen, s_mv, s_root, s_rstd, s_xn, s_xt, s_xc, s_g, s_lg) = (sem(n) for n in (
            "gate_w_in", "x_gate_tail_zeroed", "zn_ready", "z_back", "x1_ready", "ln1_stats_ready", "ln1_stats_seen", "ln1_mv_ready",
            "ln1_root_ready", "ln1_rstd_ready", "xn1_ready", "xn1_transposed", "xn1_t_copied", "gate_ready", "logit_ready"))

        def steps(engine, body):
            for t in range(8):
                body(t, t % RING, t // RING)
            with engine.Fori(0, 9) as i:
                for k in range(4):
                    body(i * 4 + (8 + k), k, i + 2)
            for t in range(44, NT + 5):
                body(t, t % RING, t // RING)

        def has(t, lag):
            return not isinstance(t, int) or 0 <= t - lag < NT

        with nc.Block() as block:
            @block.sync
            def _(sp):
                sp.dma_start(gw[:], gate_w.rearrange("(k p) n -> p k n", p=P)).then_inc(s_w, 16)
                sp.dma_start(bet[:], beta.rearrange("(a n) -> a n", a=1).to_broadcast([P, D])).then_inc(s_bet, 16)
                sp.dma_start(gb[:], gate_b.rearrange("(a n) -> a n", a=1).to_broadcast([P, NE])).then_inc(s_w, 16)

                def load(t, r, u):
                    load_zt(sp, t, r, u, m, zt, s_zt, s_zn, 2 * (t - RING + 1))
                    at = None if isinstance(t, int) and t == NT - 1 else tile_at(sp, x.rearrange("n d -> (n d)").bitcast(U8), t, D, F32)
                    wait(sp, s_x1, t - RING + 1)
                    if at is None:
                        sp.wait_ge(s_zero, 1)
                        sp.dma_start(xin[r][0:LAST, :], x[(NT - 1) * P:N, :]).then_inc(s_x[r], 16)
                    else:
                        sp.dma_start(xin[r][:], at).then_inc(s_x[r], 16)

                def step(t, r, u):
                    if has(t, -3):
                        load(t + 3, (r + 3) % 4, u)

                for t in range(3):
                    load(t, t, 0)
                steps(sp, step)

            @block.gpsimd
            def _(pool):
                pool.wait_ge(s_bet, 16)

                def step(t, r, u):
                    if has(t, 1):
                        q = (r + 1) % 2
                        at = tile_at(pool, m.x1b, t - 1, D, F32)
                        pool.wait_ge(s_x1, t)
                        wait(pool, s_x1o[q], 16 * (2 * u + (r - 1) // 2))
                        pool.sem_inc(s_seen2, 1)
                        pool.tensor_tensor(x1b[q][:], x1[(r + 3) % RING][:], bet[:], ALU.add).then_inc(s_x1b, 1)
                        pool.wait_ge(s_x1b, t)
                        pool.dma_start(at, x1b[q][:]).then_inc(s_x1o[q], 16)

                steps(pool, step)
                for r in range(2):
                    pool.wait_ge(s_x1o[r], 16 * ((NT + 1 - r) // 2))

            @block.scalar
            def _(act):
                def normalize(t, r, u):
                    act.wait_ge(s_zt[r], 16 * (u + 1))
                    wait(act, s_zb, t - 1)
                    for c in range(2):
                        act.activation(zn[r % 2][:, c, :], zt[r][:, c, :], ACT.Identity, bias=m.offset[:, c:c + 1],
                                       scale=m.scale[:, c:c + 1]).then_inc(s_zn, 1)

                def step(t, r, u):
                    if has(t, 1):
                        q = (r + 1) % 2
                        act.wait_ge(s_mv, t)
                        wait(act, s_rstd, t - 2)
                        act.activation(root[q][:], mv[q][:, 1:2], ACT.Sqrt, bias=m.eps[:, 0:1]).then_inc(s_root, 1)
                    if has(t, -1):
                        normalize(t + 1, (r + 1) % RING, u if r < 3 else u + 1)
                    if has(t, 3):
                        q = (r + 1) % 2
                        act.wait_ge(s_xt, t - 2)
                        wait(act, s_g, t - 4)
                        act.activation(xnT[q][:].rearrange("p c n -> p (c n)"), xps[q][:, 0:D], ACT.Copy).then_inc(s_xc, 1)
                        act.activation(m.xn[:, at_tile(t, -3), :], xn[(r + 1) % 4][:].unsqueeze(1), ACT.Copy).then_inc(s_kept, 1)

                for k in range(2):
                    act.dma_start(m.ew1[:, k, :, :], ew1[:, k * P:(k + 1) * P, :].rearrange("e p f -> p e f")).then_inc(m.s_weights, 16)
                normalize(0, 0, 0)
                steps(act, step)

            @block.tensor
            def _(pe):
                pe.wait_ge(s_w, 32)

                def back(t, r):
                    pe.wait_ge(s_zn, 2 * (t + 1))
                    wait(pe, s_x1, t - 1)
                    for c in range(2):
                        last = pe.transpose(zps[r % 2][:, c * P:(c + 1) * P], zn[r % 2][:, c, :], m.ident[:])
                    last.then_inc(s_zb, 1)

                back(0, 0)

                def step(t, r, u):
                    if has(t, -1):
                        back(t + 1, r + 1)
                    if has(t, 2):
                        pe.wait_ge(s_xn, t - 1)
                        wait(pe, s_xc, t - 3)
                        for c in range(2):
                            last = pe.transpose(xps[r % 2][:, c * P:(c + 1) * P], xn[(r + 2) % 4][:, c * P:(c + 1) * P], m.ident[:])
                        last.then_inc(s_xt, 1)
                    if has(t, 4):
                        q = r % 2
                        pe.wait_ge(s_xc, t - 3)
                        wait(pe, s_lg, t - 5)
                        for c in range(2):
                            last = pe.matmul(gps[q][:, 0:NE], xnT[q][:, c, :], gw[:, c, :], start=(c == 0), stop=(c == 1))
                        last.then_inc(s_g, 1)

                steps(pe, step)

            @block.vector
            def _(dve):
                def step(t, r, u):
                    if isinstance(t, int) and t == NT - 4:
                        dve.wait_ge(s_x1, NT - RING)
                        dve.memset(xin[(NT - 1) % RING][96:P, :], 0.0).then_inc(s_zero, 1)
                    if has(t, 0):
                        dve.wait_ge(s_zb, t + 1)
                        dve.wait_ge(s_x[r], 16 * (u + 1))
                        wait(dve, s_x1b, t - RING + 1)
                        dve.tensor_tensor(x1[r][:], zps[r % 2][:, 0:D], xin[r][:], ALU.add).then_inc(s_x1, 1)
                        dve.wait_ge(s_x1, t + 1)
                        wait(dve, s_mv, t - 1)
                        dve.bn_stats(st[r % 2][:], x1[r][:]).then_inc(s_st, 1)
                    if has(t, 1):
                        p, q = (r + 3) % 4, (r + 1) % 2
                        dve.wait_ge(s_root, t)
                        dve.reciprocal(rstd[q][:], root[q][:]).then_inc(s_rstd, 1)
                        dve.wait_ge(s_rstd, t)
                        wait(dve, s_xt, t - RING)
                        wait(dve, s_kept, t - RING)
                        dve.tensor_scalar(xn[p][:], x1[p][:], mv[q][:, 0:1], rstd[q][:], ALU.subtract, ALU.mult).then_inc(s_xn, 1)
                    if has(t, 0):
                        dve.wait_ge(s_st, t + 1)
                        wait(dve, s_root, t - 1)
                        wait(dve, s_xn, t - 1)
                        dve.sem_inc(s_seen, 1)
                        dve.bn_aggr(mv[r % 2][:], st[r % 2][:]).then_inc(s_mv, 1)
                    if has(t, 5):
                        dve.wait_ge(s_g, t - 4)
                        dve.tensor_tensor(m.logits[:, at_tile(t, -5), :], gps[(r + 1) % 2][:, 0:NE].unsqueeze(1), gb[:].unsqueeze(1),
                                          ALU.add).then_inc(s_lg, 1)

                steps(dve, step)


def at_tile(t, lag):
    return slice(t + lag, t + lag + 1) if isinstance(t, int) else bass.ds(t + lag, 1)


def route_stage(nc, m):
    TE = NT * NE
    HALF = TE // 2
    with ExitStack() as ctx:
        sem = m.sem

        def sb(name, shape, dt=F32):
            return ctx.enter_context(nc.sbuf_tensor(name, shape, dt))

        rank_i, rank = sb("rank_i", [P, NE], I32), sb("rank", [P, NE])
        tile_i, tile_f = sb("tile_i", [1, MT], I32), sb("tile_f", [1, MT])
        below, all_ones = sb("below_diag", [P, P], BF16), sb("all_ones", [P, P], BF16)
        valid = sb("valid", [P, NT])
        rest, score = sb("rest", [P, NT, NE]), sb("score", [P, NT, NE])
        one = [sb(f"one{i}", [P, NT, NE]) for i in range(2)]
        both, place = sb("both", [P, NT, NE], BF16), sb("place", [P, NT, NE])
        run = [sb(f"run{i}", [P, NT, NE]) for i in range(2)]
        top = [sb(f"top{i}", [P, NT]) for i in range(2)]
        most, total = sb("most", [P, NT]), sb("weight_sum", [P, NT])
        ntile_i = sb("ntile_i", [P, NE], I32)
        end = [sb(f"end{i}", [P, NE]) for i in range(2)]
        start = sb("expert_start", [P, NE])
        done = sb("done", [1, MT, NE])
        slot_f = sb("slot_f", [P, NT])
        exp_f = sb("expert_f", [1, MT])
        pre = ctx.enter_context(nc.psum_tensor("prefix_ps", [P, 2, 512], F32))
        tot = ctx.enter_context(nc.psum_tensor("total_ps", [P, 2, 512], F32))
        s_pool, s_ready, s_dve, s_oh, s_mm, s_diff, s_e = (sem(n) for n in (
            "route_pool_step", "route_constants", "route_step", "one_hots_ready", "ranks_ready", "gap_ready", "exp_ready"))

        with nc.Block() as block:
            @block.gpsimd
            def _(pool):
                step = Chain(pool, s_pool)
                pool.iota(rank_i[:], pattern=[[-1, NE]], base=NE, channel_multiplier=0).then_inc(s_ready, 1)
                pool.iota(tile_i[:], pattern=[[1, MT]], base=0, channel_multiplier=0).then_inc(s_ready, 1)
                step(pool.memset(below[:], 1.0))
                pool.memset(all_ones[:], 1.0).then_inc(s_ready, 1)
                pool.affine_select(out=below[:], in_=below[:], compare_op=ALU.is_gt, fill=0.0, base=0,
                                   pattern=[[1, P]], channel_multiplier=-1).then_inc(s_ready, 1)
                step(pool.memset(valid[:], 1.0))
                pool.affine_select(out=valid[:, NT - 1:NT], in_=valid[:, NT - 1:NT], compare_op=ALU.is_gt, fill=0.0, base=LAST,
                                   pattern=[[0, 1]], channel_multiplier=-1).then_inc(s_ready, 1)
                step(pool.memset(m.pick[:], 0.0))
                for k in range(3):
                    step(pool.affine_select(out=m.pick[:], in_=m.pick[:], compare_op=ALU.not_equal, fill=1.0, base=-NE * k,
                                            pattern=[[-1, NE], [0, P]], channel_multiplier=1))

            @block.vector
            def _(dve):
                step = Chain(dve, s_dve)
                wide = [P, NT, NE]
                dve.wait_ge(s_ready, 5)
                step(dve.tensor_copy(rank[:], rank_i[:]))
                step(dve.tensor_copy(tile_f[:], tile_i[:]))
                for k, values in enumerate((m.logits, rest)):
                    step(dve.reduce_max(top[k][:], values[:], AX.X))
                    step(dve.tensor_tensor(score[:], values[:], top[k][:].unsqueeze(2).to_broadcast(wide), ALU.is_equal))
                    step(dve.tensor_tensor(score[:], score[:], rank[:].unsqueeze(1).to_broadcast(wide), ALU.mult))
                    step(dve.reduce_max(most[:], score[:], AX.X))
                    step(dve.tensor_tensor(one[k][:], score[:], most[:].unsqueeze(2).to_broadcast(wide), ALU.is_equal))
                    if k == 0:
                        step(dve.scalar_tensor_tensor(out=rest[:].rearrange("p t e -> p (t e)"), in0=one[0][:].rearrange("p t e -> p (t e)"),
                                                      scalar=-3.0e38, in1=m.logits[:].rearrange("p t e -> p (t e)"),
                                                      op0=ALU.mult, op1=ALU.add))
                for k in range(2):
                    step(dve.tensor_tensor(one[k][:], one[k][:], valid[:].unsqueeze(2).to_broadcast(wide), ALU.mult))
                step(dve.tensor_tensor(both[:], one[0][:], one[1][:], ALU.add))
                dve.sem_inc(s_oh, 1)
                dve.tensor_tensor(m.weight[1][:], top[1][:], top[0][:], ALU.subtract).then_inc(s_diff, 1)
                dve.wait_ge(s_e, 1)
                step(dve.tensor_scalar(total[:], m.weight[1][:], 1.0, None, ALU.add))
                step(dve.reciprocal(m.weight[0][:], total[:]))
                step(dve.tensor_tensor(m.weight[1][:], m.weight[1][:], m.weight[0][:], ALU.mult))
                dve.wait_ge(s_mm, 1)
                for c in range(2):
                    flat = run[0][:].rearrange("p t e -> p (t e)")
                    step(dve.tensor_copy(flat[:, c * HALF:(c + 1) * HALF], tot[:, c, 0:HALF]))
                a, b, d = 0, 1, 1
                while d < NT:
                    step(dve.tensor_copy(run[b][:, 0:d, :], run[a][:, 0:d, :]))
                    step(dve.tensor_tensor(run[b][:, d:NT, :], run[a][:, d:NT, :], run[a][:, 0:NT - d, :], ALU.add))
                    a, b, d = b, a, 2 * d
                step(dve.tensor_scalar(start[:], run[a][:, NT - 1, :], float(P - 1), None, ALU.add))
                step(dve.tensor_copy(ntile_i[:], start[:]))
                step(dve.tensor_scalar(ntile_i[:], ntile_i[:], 7, None, ALU.arith_shift_right))
                step(dve.tensor_copy(end[0][:], ntile_i[:]))
                step(dve.tensor_copy(start[:], end[0][:]))
                x, y, d = 0, 1, 1
                while d < NE:
                    step(dve.tensor_copy(end[y][:, 0:d], end[x][:, 0:d]))
                    step(dve.tensor_tensor(end[y][:, d:NE], end[x][:, d:NE], end[x][:, 0:NE - d], ALU.add))
                    x, y, d = y, x, 2 * d
                step(dve.tensor_tensor(start[:], end[x][:], start[:], ALU.subtract))
                step(dve.tensor_scalar(start[:], start[:], float(P), None, ALU.mult))
                for c in range(2):
                    flat, place_f = run[a][:].rearrange("p t e -> p (t e)"), place[:].rearrange("p t e -> p (t e)")
                    span = slice(c * HALF, (c + 1) * HALF)
                    step(dve.tensor_tensor(place_f[:, span], flat[:, span], tot[:, c, 0:HALF], ALU.subtract))
                    step(dve.tensor_tensor(place_f[:, span], place_f[:, span], pre[:, c, 0:HALF], ALU.add))
                step(dve.tensor_tensor(place[:], place[:], start[:].unsqueeze(1).to_broadcast(wide), ALU.add))
                for k in range(2):
                    step(dve.tensor_tensor(score[:], place[:], one[k][:], ALU.mult))
                    step(dve.reduce_sum(slot_f[:], score[:], AX.X))
                    step(dve.tensor_copy(m.slot[k][:], slot_f[:]))
                step(dve.tensor_tensor(done[:], end[x][0:1, :].unsqueeze(1).to_broadcast([1, MT, NE]),
                                       tile_f[:].unsqueeze(2).to_broadcast([1, MT, NE]), ALU.is_le))
                step(dve.reduce_sum(exp_f[:], done[:], AX.X))
                step(dve.tensor_scalar(m.expert[:], exp_f[:], float(NE - 1), None, ALU.min))

            @block.scalar
            def _(act):
                act.wait_ge(s_diff, 1)
                act.activation(m.weight[1][:], m.weight[1][:], ACT.Exp).then_inc(s_e, 1)

            @block.tensor
            def _(pe):
                pe.wait_ge(s_oh, 1)
                for c in range(2):
                    part = both[:].rearrange("p t e -> p (t e)")[:, c * HALF:(c + 1) * HALF]
                    pe.matmul(pre[:, c, 0:HALF], below[:], part, start=True, stop=True)
                    last = pe.matmul(tot[:, c, 0:HALF], all_ones[:], part, start=True, stop=True)
                last.then_inc(s_mm, 1)


def scatter_stage(nc, m, eb1, ew2, eb2):
    RING = 4
    with ExitStack() as ctx:
        sem = m.sem

        xn = [ctx.enter_context(nc.sbuf_tensor(f"xn_s{i}", [P, D], F32)) for i in range(RING)]
        at = [[ctx.enter_context(nc.sbuf_tensor(f"at{k}_{i}", [P, 1], I32)) for i in range(RING)] for k in range(2)]
        rows1 = ctx.enter_context(nc.sbuf_tensor("bias1_rows", [NE * FF // P, P], F32))
        brow = ctx.enter_context(nc.sbuf_tensor("bias2_rows", [P, NE * D // P], F32))
        bres = ctx.enter_context(nc.sbuf_tensor("bias2_rest", [P, NE * D // P], F32))
        bpart = ctx.enter_context(nc.sbuf_tensor("bias2_parts", [P, 3, NE * D // P], BF16))
        columns = ctx.enter_context(nc.psum_tensor("bias1_ps", [P, NE * FF // P], F32))
        s_w, s_b, s_b1, s_col, s_b1t, s_dve, s_parts, s_pst, s_pin = (sem(n) for n in (
            "expert_weights2_in", "bias2_in", "bias1_in", "bias1_columns_ready", "bias1_copied", "bias_step", "bias_parts_ready",
            "bias_parts_stored", "bias_parts_in"))
        s_in = sem("rows_copied")
        s_seen = sem("send_may_start")
        s_at, s_sent = sem("at_ready"), [sem(f"rows_sent{i}") for i in range(RING)]

        with nc.Block() as block:
            @block.sync
            def _(sp):
                sp.dma_start(rows1[:], eb1.rearrange("e (c p) -> (e c) p", p=P)).then_inc(s_b1, 16)
                sp.dma_start(brow[:], eb2.rearrange("e f -> (e f)").rearrange("(p n) -> p n", p=P)).then_inc(s_b, 16)
                for k in range(4):
                    sp.dma_start(m.ew2[:, k, :, :], ew2[:, k * P:(k + 1) * P, :].rearrange("e p f -> p e f")).then_inc(s_w, 16)
                sp.wait_ge(s_parts, 1)
                for k in range(3):
                    sp.dma_start(m.b2_parts[k, :].rearrange("(p n) -> p n", p=P), bpart[:, k, :]).then_inc(s_pst, 16)
                sp.wait_ge(s_pst, 48)
                sp.dma_start(m.eb2[:], m.b2_parts.rearrange("k (e f) -> (k e) f", e=NE)).then_inc(s_pin, 16)
                sp.wait_ge(s_pin, 16)
                sp.wait_ge(m.s_weights, 32)
                sp.wait_ge(s_w, 64)

            @block.tensor
            def _(pe):
                pe.wait_ge(s_b1, 16)
                pe.transpose(columns[:], rows1[:], m.ident[0:NE * FF // P, 0:NE * FF // P]).then_inc(s_col, 1)

            @block.scalar
            def _(act):
                def copy(t, r, u):
                    wait(act, s_sent[r], 32 * u)
                    act.activation(xn[r][:].unsqueeze(1), m.xn[:, at_tile(t, 0), :], ACT.Copy).then_inc(s_in, 1)

                for_slots(act, copy, NT, RING)

            @block.vector
            def _(dve):
                def index(t, r, u):
                    wait(dve, s_sent[r], 32 * u)
                    for k in range(2):
                        dve.tensor_copy(at[k][r][:], m.slot[k][:, at_tile(t, 0)]).then_inc(s_at, 1)

                for_slots(dve, index, NT, RING)
                step = Chain(dve, s_dve)
                dve.wait_ge(s_col, 1)
                dve.tensor_copy(m.b1t[:], columns[:]).then_inc(s_b1t, 1)
                dve.wait_ge(s_b, 16)
                step(dve.tensor_copy(bpart[:, 0, :], brow[:]))
                step(dve.tensor_tensor(bres[:], brow[:], bpart[:, 0, :], ALU.subtract))
                step(dve.tensor_copy(bpart[:, 1, :], bres[:]))
                step(dve.tensor_tensor(brow[:], bres[:], bpart[:, 1, :], ALU.subtract))
                step(dve.tensor_copy(bpart[:, 2, :], brow[:]))
                dve.sem_inc(s_parts, 1)

            @block.gpsimd
            def _(pool):
                def send(t, r, u):
                    n = LAST if isinstance(t, int) and t == NT - 1 else P
                    pool.wait_ge(s_in, t + 1)
                    pool.wait_ge(s_at, 2 * (t + 1))
                    pool.sem_inc(s_seen, 1)
                    for k in range(2):
                        pool.indirect_dma_start(out=m.rows, out_offset=bass.IndirectOffsetOnAxis(ap=at[k][r][0:n, :], axis=0),
                                                in_=xn[r][0:n, :], in_offset=None).then_inc(s_sent[r], 16)

                for_slots(pool, send, NT, RING)
                for r in range(RING):
                    pool.wait_ge(s_sent[r], 32 * ((NT + RING - 1 - r) // RING))


def expert_stage(nc, m):
    with ExitStack() as ctx:
        sem = m.sem

        def sb(name, shape, n, dt=F32):
            return [ctx.enter_context(nc.sbuf_tensor(f"{name}{i}", shape, dt)) for i in range(n)]

        def ps(name):
            return [ctx.enter_context(nc.psum_tensor(f"{name}{i}", [P, 512], F32)) for i in range(2)]

        xe, xT, hid, hT, ye = sb("xe", [P, D], 4), sb("xeT", [P, 2, P], 2), sb("hid", [P, FF], 2), sb("hidT", [P, 4, P], 2), sb("ye", [P, D], 4)
        xps, hps, tps, yps = ps("xe_ps"), ps("hid_ps"), ps("hidT_ps"), ps("ye_ps")
        s_in, s_out = [sem(f"xe_in{i}") for i in range(4)], [sem(f"ye_stored{i}") for i in range(4)]
        s_xt, s_xc, s_h, s_hid, s_ht, s_hc, s_y, s_yc = (sem(n) for n in (
            "xe_transposed", "xeT_copied", "hid_ready", "hid_copied", "hid_transposed", "hidT_copied", "ye_ready", "ye_copied"))

        def steps(engine, body):
            for t in range(8):
                body(t, t % 4, t // 4)
            rounds = (MT - 8) // 4
            with engine.Fori(0, rounds) as i:
                for k in range(4):
                    body(i * 4 + (8 + k), k, i + 2)
            for t in range(8 + 4 * rounds, MT + 3):
                body(t, t % 4, t // 4)

        def has(t, lag):
            return not isinstance(t, int) or 0 <= t - lag < MT

        with nc.Block() as block:
            @block.sync
            def _(sp):
                rows, ys = m.rows.rearrange("n d -> (n d)").bitcast(U8), m.ys.rearrange("n d -> (n d)").bitcast(U8)

                def load(t, r):
                    at = tile_at(sp, rows, t, D, F32)
                    wait(sp, s_xt, t - 3)
                    sp.dma_start(xe[r][:], at).then_inc(s_in[r], 16)

                load(0, 0)
                load(1, 1)

                def step(t, r, u):
                    if has(t, -2):
                        load(t + 2, (r + 2) % 4)
                    if has(t, 3):
                        q = (r + 1) % 4
                        at = tile_at(sp, ys, t - 3, D, F32)
                        sp.wait_ge(s_yc, t - 2)
                        sp.dma_start(at, ye[q][:]).then_inc(s_out[q], 16)

                steps(sp, step)
                for r in range(4):
                    sp.wait_ge(s_out[r], 16 * ((MT + 3 - r) // 4))

            @block.tensor
            def _(pe):
                def step(t, r, u):
                    if has(t, 0):
                        pe.wait_ge(s_in[r], 16 * (u + 1))
                        wait(pe, s_xc, t - 1)
                        for c in range(2):
                            last = pe.transpose(xps[r % 2][:, c * P:(c + 1) * P], xe[r][:, c * P:(c + 1) * P], m.ident[:])
                        last.then_inc(s_xt, 1)
                    if has(t, 2):
                        pe.wait_ge(s_hid, t - 1)
                        wait(pe, s_hc, t - 3)
                        for c in range(4):
                            last = pe.transpose(tps[r % 2][:, c * P:(c + 1) * P], hid[r % 2][:, c * P:(c + 1) * P], m.ident[:])
                        last.then_inc(s_ht, 1)
                    if has(t, 1):
                        q = (r + 1) % 2
                        e = pe.value_load(m.expert[0:1, at_tile(t, -1)], min_val=0, max_val=NE - 1)
                        pe.wait_ge(s_xc, t)
                        wait(pe, s_hid, t - 2)
                        for k in range(2):
                            last = pe.matmul(hps[q][:], xT[q][:, k, :], m.ew1[:, k, bass.ds(e, 1), :].rearrange("p o f -> p (o f)"),
                                             start=(k == 0), stop=(k == 1))
                        last.then_inc(s_h, 1)
                    if has(t, 3):
                        q = (r + 1) % 2
                        e = pe.value_load(m.expert[0:1, at_tile(t, -3)], min_val=0, max_val=NE - 1)
                        pe.wait_ge(s_hc, t - 2)
                        wait(pe, s_yc, t - 4)
                        pe.matmul(yps[q][:, 0:D], m.pick[:, bass.ds(e, 1), :].rearrange("k o n -> k (o n)"), m.eb2[:], start=True, stop=False)
                        for k in range(4):
                            last = pe.matmul(yps[q][:, 0:D], hT[q][:, k, :], m.ew2[:, k, bass.ds(e, 1), :].rearrange("p o f -> p (o f)"),
                                             start=False, stop=(k == 3))
                        last.then_inc(s_y, 1)

                steps(pe, step)

            @block.scalar
            def _(act):
                def step(t, r, u):
                    if has(t, 0):
                        act.wait_ge(s_xt, t + 1)
                        wait(act, s_h, t - 1)
                        act.activation(xT[r % 2][:].rearrange("p c n -> p (c n)"), xps[r % 2][:, 0:D], ACT.Copy).then_inc(s_xc, 1)
                    if has(t, 1):
                        q = (r + 1) % 2
                        act.wait_ge(s_h, t)
                        wait(act, s_ht, t - 2)
                        act.activation(hid[q][:], hps[q][:], ACT.Copy).then_inc(s_hid, 1)

                steps(act, step)

            @block.vector
            def _(dve):
                def step(t, r, u):
                    if has(t, 2):
                        e = dve.value_load(m.expert[0:1, at_tile(t, -2)], min_val=0, max_val=NE - 1)
                        dve.wait_ge(s_ht, t - 1)
                        wait(dve, s_y, t - 3)
                        for c in range(4):
                            last = dve.tensor_scalar(hT[r % 2][:, c, :], tps[r % 2][:, c * P:(c + 1) * P], m.b1t[:, bass.ds(e * 4 + c, 1)], 0.0,
                                                     ALU.add, ALU.max)
                        last.then_inc(s_hc, 1)
                    if has(t, 3):
                        q = (r + 1) % 4
                        dve.wait_ge(s_y, t - 2)
                        wait(dve, s_out[q], 16 * (u if r == 3 else u - 1))
                        dve.tensor_copy(ye[q][:], yps[q % 2][:, 0:D]).then_inc(s_yc, 1)

                steps(dve, step)


def combine_stage(nc, m, gamma, out):
    RING = 4
    with ExitStack() as ctx:
        sem = m.sem

        def sb(name, shape, n, dt=F32):
            return [ctx.enter_context(nc.sbuf_tensor(f"{name}{i}", shape, dt)) for i in range(n)]

        gam = ctx.enter_context(nc.sbuf_tensor("gamma_sb", [P, D], F32))
        y1, y2, x1, res = (sb(n, [P, D], RING) for n in ("y1_", "y2_", "x1_beta_c", "res"))
        at = [sb(f"from{k}_", [P, 1], RING, I32) for k in range(2)]
        part, yv, scaled = (sb(n, [P, D], 2) for n in ("part", "yv", "scaled"))
        st, mv, root, rstd = sb("ln2_stats", [P, 6], 2), sb("ln2_mv", [P, 2], 2), sb("ln2_root", [P, 1], 2), sb("ln2_rstd", [P, 1], 2)
        s_gb = sem("gamma_in")
        s_in, s_got, s_out = ([sem(f"{n}{i}") for i in range(RING)] for n in ("c_rows_in", "expert_rows_in", "out_stored"))
        s_at, s_seen, s_part, s_y, s_st, s_seen2, s_mv, s_root, s_rstd, s_scaled, s_res = (sem(n) for n in (
            "from_ready", "from_seen", "c_part", "c_y", "c_stats", "c_stats_seen", "c_mv", "c_root", "c_rstd", "c_scaled", "c_result"))

        def steps(engine, body):
            for t in range(8):
                body(t, t % RING, t // RING)
            with engine.Fori(0, 9) as i:
                for k in range(4):
                    body(i * 4 + (8 + k), k, i + 2)
            for t in range(44, NT + 2):
                body(t, t % RING, t // RING)

        def has(t, lag):
            return not isinstance(t, int) or 0 <= t - lag < NT

        with nc.Block() as block:
            @block.sync
            def _(sp):
                sp.dma_start(gam[:], gamma.rearrange("(a n) -> a n", a=1).to_broadcast([P, D])).then_inc(s_gb, 16)
                out_bytes = out.rearrange("n d -> (n d)").bitcast(U8)

                def load(t, r):
                    a = tile_at(sp, m.x1b, t, D, F32)
                    wait(sp, s_res, t - RING + 1)
                    sp.dma_start(x1[r][:], a).then_inc(s_in[r], 16)

                load(0, 0)
                load(1, 1)

                def step(t, r, u):
                    if has(t, -2):
                        load(t + 2, (r + 2) % RING)
                    if has(t, 2):
                        q = (r + 2) % 4
                        if isinstance(t, int) and t == NT + 1:
                            sp.wait_ge(s_res, NT)
                            sp.dma_start(out[(NT - 1) * P:N, :], res[q][0:LAST, :]).then_inc(s_out[q], 16)
                        else:
                            to = tile_at(sp, out_bytes, t - 2, D, F32)
                            sp.wait_ge(s_res, t - 1)
                            sp.dma_start(to, res[q][:]).then_inc(s_out[q], 16)

                steps(sp, step)
                for r in range(RING):
                    sp.wait_ge(s_out[r], 16 * ((NT + RING - 1 - r) // RING))

            @block.gpsimd
            def _(pool):
                def step(t, r, u):
                    if has(t, 0):
                        pool.wait_ge(s_at, 2 * (t + 1))
                        wait(pool, s_y, t - RING + 1)
                        pool.sem_inc(s_seen, 1)
                        for k, y in enumerate((y1, y2)):
                            pool.indirect_dma_start(out=y[r][:], out_offset=None, in_=m.ys,
                                                    in_offset=bass.IndirectOffsetOnAxis(ap=at[k][r][:], axis=0)).then_inc(s_got[r], 16)

                steps(pool, step)

            @block.vector
            def _(dve):
                dve.wait_ge(s_gb, 16)

                def step(t, r, u):
                    q, p = r % 2, (r + 1) % 2
                    o = (r + 2) % 4
                    if has(t, 0):
                        dve.wait_ge(s_got[r], 32 * (u + 1))
                        wait(dve, s_y, t - 1)
                        dve.scalar_tensor_tensor(out=part[q][:].unsqueeze(1), in0=y1[r][:].unsqueeze(1), scalar=m.weight[0][:, at_tile(t, 0)],
                                                 in1=m.xn[:, at_tile(t, 0), :], op0=ALU.mult, op1=ALU.add).then_inc(s_part, 1)
                    if has(t, 1):
                        dve.wait_ge(s_st, t)
                        wait(dve, s_root, t - 2)
                        wait(dve, s_scaled, t - 2)
                        dve.sem_inc(s_seen2, 1)
                        dve.bn_aggr(mv[p][:], st[p][:]).then_inc(s_mv, 1)
                    if has(t, 2):
                        dve.wait_ge(s_rstd, t - 1)
                        dve.wait_ge(s_scaled, t - 1)
                        dve.wait_ge(s_in[o], 16 * (u + 1 if r > 1 else u))
                        wait(dve, s_out[o], 16 * (u if r > 1 else u - 1))
                        dve.scalar_tensor_tensor(out=res[o][:], in0=scaled[q][:], scalar=rstd[q][:], in1=x1[o][:],
                                                 op0=ALU.mult, op1=ALU.add).then_inc(s_res, 1)
                    if has(t, 0):
                        dve.wait_ge(s_part, t + 1)
                        wait(dve, s_scaled, t - 1)
                        dve.scalar_tensor_tensor(out=yv[q][:], in0=y2[r][:], scalar=m.weight[1][:, at_tile(t, 0)], in1=part[q][:],
                                                 op0=ALU.mult, op1=ALU.add).then_inc(s_y, 1)
                    if has(t, 1):
                        dve.wait_ge(s_mv, t)
                        wait(dve, s_res, t - 2)
                        dve.scalar_tensor_tensor(out=scaled[p][:], in0=yv[p][:], scalar=mv[p][:, 0:1], in1=gam[:],
                                                 op0=ALU.subtract, op1=ALU.mult).then_inc(s_scaled, 1)
                        dve.wait_ge(s_root, t)
                        dve.reciprocal(rstd[p][:], root[p][:]).then_inc(s_rstd, 1)
                    if has(t, 0):
                        dve.wait_ge(s_y, t + 1)
                        wait(dve, s_mv, t - 1)
                        dve.bn_stats(st[q][:], yv[q][:]).then_inc(s_st, 1)
                steps(dve, step)

            @block.scalar
            def _(act):
                def index(t, r, u):
                    wait(act, s_got[r], 32 * u)
                    for k in range(2):
                        act.activation(at[k][r][:], m.slot[k][:, at_tile(t, 0)], ACT.Copy).then_inc(s_at, 1)

                for t in range(3):
                    index(t, t, 0)

                def step(t, r, u):
                    if has(t, -3):
                        index(t + 3, (r + 3) % RING, u if r == 0 else u + 1)
                    if has(t, 1):
                        q = (r + 1) % 2
                        act.wait_ge(s_mv, t)
                        wait(act, s_rstd, t - 2)
                        act.activation(root[q][:], mv[q][:, 1:2], ACT.Sqrt, bias=m.eps[:, 0:1]).then_inc(s_root, 1)

                steps(act, step)



def program(nc, x, src, dst, w0, b0, g0, bt0, w1, b1, g1, bt1, gate_w, gate_b, ew1, eb1, ew2, eb2, gamma, beta, out):
    def dram(name, shape, dt):
        return nc.dram_tensor(name, shape, dt).ap()

    m = Names()
    m.codes = dram("edge_codes", [EPAD], I32)
    m.deg = dram("degrees", [NBLK * BD], F32)
    m.counts = dram("counts", [NT * P * NT * P], U8)
    m.zT = dram("z_t", [NT * P * D * 4], U8)
    m.x1b = dram("x1_beta_dram", [NT * P * D * 4], U8)
    m.any_h = dram("any_h_dram", [(NT + 1) * P * D * 4], U8)
    m.any_sum = dram("any_sum_dram", [(NT + 1) * P * D * 4], U8)
    m.rows = dram("expert_rows", [MT * P, D], F32)
    m.ys = dram("expert_out", [MT * P, D], F32)
    m.b2_parts = dram("b2_parts", [3, NE * D], BF16)
    m.sem = Semaphores(nc)
    m.s_weights = nc.alloc_semaphore("expert_weights_in")
    with ExitStack() as ctx:
        def sb(name, shape, dt):
            return ctx.enter_context(nc.sbuf_tensor(name, shape, dt))

        m.iota16, m.iota4 = sb("iota16", [P, P], FP16), sb("iota4", [P, P, 4], FP16)
        m.ident, m.ones = sb("ident", [P, P], F32), sb("ones", [P, P], F32)
        m.flags = sb("flags", [P, 2], I32)
        m.dis = sb("dis", [P, NT], F32)
        m.eps = sb("eps", [P, 1], F32)
        m.stats = sb("z_stats", [P, 2, NT * 6], F32)
        m.b0, m.b1, m.g0, m.g1, m.bt0, m.bt1 = (sb(n, [P, 2], F32) for n in ("b0_sb", "b1_sb", "g0_sb", "g1_sb", "bt0_sb", "bt1_sb"))
        m.scale, m.offset = sb("bn_scale", [P, 2], F32), sb("bn_offset", [P, 2], F32)
        with nc.sbuf_tensor("keyT", [P, NBLK], FP16) as m.keyT, nc.sbuf_tensor("loT", [P, NBLK], FP16) as m.loT:
            edge_stage(nc, m, src, dst)
            parameter_stage(nc, m, [(m.b0, b0), (m.g0, g0), (m.bt0, bt0), (m.b1, b1), (m.g1, g1), (m.bt1, bt1)])
            dis_stage(nc, m)
            any_degrees(nc, m)
            with nc.sbuf_tensor("h", [P, NT, 2, D], F32R) as m.h:
                input_stage(nc, m, x, w0)
                build_stage(nc, m)
                m.sem.renew()
                any_sums(nc, m, "_any0", m.b0)
                norm_stage(nc, m, "0", m.g0, m.bt0)
                project_stage(nc, m, w1)
                product_stage(nc, m)
                m.sem.renew()
                any_sums(nc, m, "_any1", m.b1)
                norm_stage(nc, m, "1", m.g1, m.bt1)
        m.sem.renew()
        m.weight = [sb(f"weight{k}", [P, NT], F32) for k in range(2)]
        m.slot = [sb(f"slot{k}", [P, NT], I32) for k in range(2)]
        m.expert = sb("tile_expert", [1, MT], I32)
        m.xn = sb("xn_kept", [P, NT, D], F32)
        with ExitStack() as big:
            def big_sb(name, shape, dt):
                return big.enter_context(nc.sbuf_tensor(name, shape, dt))

            m.ew1 = big_sb("ew1", [P, 2, NE, FF], F32)
            m.pick = big_sb("pick", [3 * NE, NE, P], BF16)
            with nc.sbuf_tensor("logits", [P, NT, NE], F32) as m.logits:
                gate_stage(nc, m, x, gate_w, gate_b, beta, ew1)
                route_stage(nc, m)
            m.ew2 = big_sb("ew2", [P, 4, NE, D], F32)
            m.b1t, m.eb2 = big_sb("b1_columns", [P, NE * FF // P], F32), big_sb("eb2", [3 * NE, D], BF16)
            m.sem.renew()
            scatter_stage(nc, m, eb1, ew2, eb2)
            expert_stage(nc, m)
        combine_stage(nc, m, gamma, out)


def parameter_stage(nc, m, columns):
    s_in, s_eps = m.sem("parameters_in"), m.sem("eps_set")
    with nc.Block() as block:
        @block.sync
        def _(sp):
            with nc.allow_non_contiguous_dma(reason="six vectors of 256 words"):
                for t, v in columns:
                    sp.dma_start(t[:], v.rearrange("(c p) -> p c", p=P)).then_inc(s_in, 16)
            sp.wait_ge(s_in, 16 * len(columns))

        @block.vector
        def _(dve):
            dve.memset(m.eps[:], EPS).then_inc(s_eps, 1)


_INS = ["x", "src", "dst", "L0_gnn_W0", "L0_gnn_b0", "L0_gnn_g0", "L0_gnn_bt0", "L0_gnn_W1", "L0_gnn_b1", "L0_gnn_g1", "L0_gnn_bt1",
        "L0_ffn_gate_w", "L0_ffn_gate_b", "L0_ffn_w1", "L0_ffn_b1", "L0_ffn_w2", "L0_ffn_b2", "L0_ffn_gamma", "L0_ffn_beta"]


def kernel(**inputs):
    import concourse.bacc as bacc
    from concourse.bass_utils import run_bass_kernel_spmd

    nc = bacc.Bacc("TRN2", target_bir_lowering=False, num_devices=1)
    arrays, args = {}, []
    for name in _INS:
        a = np.ascontiguousarray(inputs[name])
        arrays["in_" + name] = a
        args.append(nc.dram_tensor("in_" + name, a.shape, mybir.dt.from_np(a.dtype), kind="ExternalInput").ap())
    args.append(nc.dram_tensor("out", (N, D), F32, kind="ExternalOutput").ap())
    program(nc, *args)
    return run_bass_kernel_spmd(nc, [arrays], core_ids=[0]).results[0]["out"]
```
